# Optimizing a Trainium2 kernel written in Bass

```python
import numpy as np
import jax
import jax.numpy as jnp

def _softmax(x, axis=-1):
    return jax.nn.softmax(x, axis=axis)

def _gelu(x):
    return jax.nn.gelu(x, approximate=True)

def _silu(x):
    return jax.nn.silu(x)

def _sigmoid(x):
    return jax.nn.sigmoid(x)

def _layernorm(x, axis=-1, eps=1e-05):
    m = jnp.mean(x, axis=axis, keepdims=True)
    v = jnp.var(x, axis=axis, keepdims=True)
    return (x - m) / jnp.sqrt(v + eps)

def _scatter_add(tgt, idx, src, axis=0):
    return tgt.at[idx].add(src)

def _segment_sum(src, seg, n):
    return jax.ops.segment_sum(src, seg, n)
kernel_name = 'mk_seq_preln_d2_jaxref_r8_4f5690'

def setup_inputs(seed: int=0):
    np.random.seed(seed)
    _w = jnp.asarray

    def _L0_attn_setup():
        import jax, jax.numpy as jnp
        import numpy as np
        IN_FEATURES = 256
        HEAD_NUM = 64
        D = IN_FEATURES // HEAD_NUM
        SCALE = float(np.sqrt(D))
        key = jax.random.key(seed)
        ks = jax.random.split(key, 9)
        F = IN_FEATURES
        x = jax.random.normal(ks[0], (4, 128, F), dtype=jnp.float32)
        w = lambda k: jax.random.normal(k, (F, F), dtype=jnp.float32) * 0.02
        b = lambda k: jax.random.normal(k, (F,), dtype=jnp.float32) * 0.01
        return {'x': x, 'Wq': w(ks[1]), 'bq': b(ks[2]), 'Wk': w(ks[3]), 'bk': b(ks[4]), 'Wv': w(ks[5]), 'bv': b(ks[6]), 'Wo': w(ks[7]), 'bo': b(ks[8])}
    _L0_attn_in = _L0_attn_setup()

    def _L0_ffn_setup():
        import jax, jax.numpy as jnp
        import numpy as np
        B, T, D = (2, 128, 256)
        E, F, K = (64, 64, 4)
        S, HS = (2, 64 * 4)
        key = jax.random.key(seed)
        ks = jax.random.split(key, 9)
        s = 0.02
        f32 = jnp.float32
        return {'x': jax.random.normal(ks[0], (B, T, D), f32), 'router_w': jax.random.normal(ks[1], (D, E), f32) * s, 'router_bias': jnp.zeros((E,), f32), 'wg': jax.random.normal(ks[2], (E, D, F), f32) * s, 'wu': jax.random.normal(ks[3], (E, D, F), f32) * s, 'wd': jax.random.normal(ks[4], (E, F, D), f32) * s, 'swg': jax.random.normal(ks[5], (S, D, HS), f32) * s, 'swu': jax.random.normal(ks[6], (S, D, HS), f32) * s, 'swd': jax.random.normal(ks[7], (S, HS, D), f32) * s}
    _L0_ffn_in = _L0_ffn_setup()

    def _L1_attn_setup():
        import jax, jax.numpy as jnp
        import numpy as np
        import math
        D = 256
        K = 64
        NUM_HEADS = 32
        HEAD_DIM = K // NUM_HEADS
        SPARSITY = 0.1
        LN_EPS = 1e-05
        key = jax.random.key(seed)
        ks = jax.random.split(key, 12)
        B, S = (1, 128)
        sc = 0.02
        inp = {'x': jax.random.normal(ks[0], (B, S, D), dtype=jnp.float32), 'gamma': jnp.ones((D,), jnp.float32), 'beta': jnp.zeros((D,), jnp.float32), 'W1': jax.random.normal(ks[1], (128, D), jnp.float32) * sc, 'b1': jnp.zeros((128,), jnp.float32), 'W2': jax.random.normal(ks[2], (64, 128), jnp.float32) * sc, 'b2': jnp.zeros((64,), jnp.float32), 'W3': jax.random.normal(ks[3], (1, 64), jnp.float32) * sc, 'b3': jnp.zeros((1,), jnp.float32), 'Wqkv': jax.random.normal(ks[4], (3 * K, D), jnp.float32) * sc, 'bqkv': jnp.zeros((3 * K,), jnp.float32), 'Wout': jax.random.normal(ks[5], (D, K), jnp.float32) * sc, 'bout': jnp.zeros((D,), jnp.float32)}
        return inp
    _L1_attn_in = _L1_attn_setup()

    def _L1_ffn_setup():
        import jax, jax.numpy as jnp
        import numpy as np
        key = jax.random.key(seed)
        k1, k2, k3, k4 = jax.random.split(key, 4)
        B, S, D_IN, D_OUT = (4, 512, 256, 256)
        x = jax.random.normal(k1, (B, S, D_IN), dtype=jnp.float32)
        weight = jax.random.normal(k2, (D_OUT, D_IN), dtype=jnp.float32) * 0.02
        scale_weight = jax.random.uniform(k3, (D_OUT,), dtype=jnp.float32, minval=0.5, maxval=1.5)
        bias = jax.random.normal(k4, (D_OUT,), dtype=jnp.float32) * 0.02
        return {'x': x, 'weight': weight, 'scale_weight': scale_weight, 'bias': bias}
    _L1_ffn_in = _L1_ffn_setup()
    _d = {'L0_attn_x': _L0_attn_in['x'], 'L0_attn_Wq': _L0_attn_in['Wq'], 'L0_attn_bq': _L0_attn_in['bq'], 'L0_attn_Wk': _L0_attn_in['Wk'], 'L0_attn_bk': _L0_attn_in['bk'], 'L0_attn_Wv': _L0_attn_in['Wv'], 'L0_attn_bv': _L0_attn_in['bv'], 'L0_attn_Wo': _L0_attn_in['Wo'], 'L0_attn_bo': _L0_attn_in['bo'], 'L0_ffn_router_w': _L0_ffn_in['router_w'], 'L0_ffn_router_bias': _L0_ffn_in['router_bias'], 'L0_ffn_wg': _L0_ffn_in['wg'], 'L0_ffn_wu': _L0_ffn_in['wu'], 'L0_ffn_wd': _L0_ffn_in['wd'], 'L0_ffn_swg': _L0_ffn_in['swg'], 'L0_ffn_swu': _L0_ffn_in['swu'], 'L0_ffn_swd': _L0_ffn_in['swd'], 'L1_attn_gamma': _L1_attn_in['gamma'], 'L1_attn_beta': _L1_attn_in['beta'], 'L1_attn_W1': _L1_attn_in['W1'], 'L1_attn_b1': _L1_attn_in['b1'], 'L1_attn_W2': _L1_attn_in['W2'], 'L1_attn_b2': _L1_attn_in['b2'], 'L1_attn_W3': _L1_attn_in['W3'], 'L1_attn_b3': _L1_attn_in['b3'], 'L1_attn_Wqkv': _L1_attn_in['Wqkv'], 'L1_attn_bqkv': _L1_attn_in['bqkv'], 'L1_attn_Wout': _L1_attn_in['Wout'], 'L1_attn_bout': _L1_attn_in['bout'], 'L1_ffn_weight': _L1_ffn_in['weight'], 'L1_ffn_scale_weight': _L1_ffn_in['scale_weight'], 'L1_ffn_bias': _L1_ffn_in['bias']}
    _x0 = _d['L0_attn_x']
    _d['L0_attn_x'] = jax.random.normal(jax.random.fold_in(jax.random.key(seed), 1), (4, 512, 256), dtype=_x0.dtype)
    del _x0
    return _d

def reference(L0_attn_x, L0_attn_Wq, L0_attn_bq, L0_attn_Wk, L0_attn_bk, L0_attn_Wv, L0_attn_bv, L0_attn_Wo, L0_attn_bo, L0_ffn_router_w, L0_ffn_router_bias, L0_ffn_wg, L0_ffn_wu, L0_ffn_wd, L0_ffn_swg, L0_ffn_swu, L0_ffn_swd, L1_attn_gamma, L1_attn_beta, L1_attn_W1, L1_attn_b1, L1_attn_W2, L1_attn_b2, L1_attn_W3, L1_attn_b3, L1_attn_Wqkv, L1_attn_bqkv, L1_attn_Wout, L1_attn_bout, L1_ffn_weight, L1_ffn_scale_weight, L1_ffn_bias):

    def _L0_attn_ref(x, Wq, bq, Wk, bk, Wv, bv, Wo, bo):
        import jax, jax.numpy as jnp
        import numpy as np
        IN_FEATURES = 256
        HEAD_NUM = 64
        D = IN_FEATURES // HEAD_NUM
        SCALE = float(np.sqrt(D))
        B, S, F = x.shape
        d = D
        h = F // d
        q = x @ Wq + bq
        k = x @ Wk + bk
        v = x @ Wv + bv

        def to_heads(t):
            return t.reshape(B, S, d, h).transpose(0, 2, 1, 3)
        q, k, v = (to_heads(q), to_heads(k), to_heads(v))
        scores = jnp.einsum('bdsh,bdth->bdst', q, k) / SCALE
        weights = jax.nn.softmax(scores, axis=-1)
        feats = jnp.einsum('bdst,bdth->bdsh', weights, v)
        feats = feats.transpose(0, 2, 1, 3).reshape(B, S, F)
        return feats @ Wo + bo

    def _L0_ffn_ref(x, router_w, router_bias, wg, wu, wd, swg, swu, swd):
        import jax, jax.numpy as jnp
        import numpy as np
        B, T, D = (2, 128, 256)
        E, F, K = (64, 64, 4)
        S, HS = (2, 64 * 4)
        b, t, d = x.shape
        flat = x.reshape(b * t, d)
        n = flat.shape[0]
        logits = flat @ router_w
        scores = jax.nn.softmax(logits, axis=-1)
        _, topk_idx = jax.lax.top_k(logits + router_bias, K)
        topk_scores = jnp.take_along_axis(scores, topk_idx, axis=-1)
        topk_scores = topk_scores / topk_scores.sum(axis=-1, keepdims=True)
        comb = jnp.zeros((n, E), dtype=flat.dtype).at[jnp.arange(n)[:, None], topk_idx].set(topk_scores)
        g = jax.nn.silu(jnp.einsum('nd,edf->nef', flat, wg))
        u = jnp.einsum('nd,edf->nef', flat, wu)
        routed = jnp.einsum('ne,nef,efd->nd', comb, g * u, wd)
        sg = jax.nn.silu(jnp.einsum('nd,sdh->nsh', flat, swg))
        su = jnp.einsum('nd,sdh->nsh', flat, swu)
        shared = jnp.einsum('nsh,shd->nd', sg * su, swd)
        return (routed + shared).reshape(b, t, d)

    def _L1_attn_ref(x, gamma, beta, W1, b1, W2, b2, W3, b3, Wqkv, bqkv, Wout, bout):
        import jax, jax.numpy as jnp
        import numpy as np
        import math
        D = 256
        K = 64
        NUM_HEADS = 32
        HEAD_DIM = K // NUM_HEADS
        SPARSITY = 0.1
        LN_EPS = 1e-05
        B, S, d = x.shape
        mu = jnp.mean(x, -1, keepdims=True)
        var = jnp.var(x, -1, keepdims=True)
        xn = (x - mu) * jax.lax.rsqrt(var + LN_EPS) * gamma + beta
        h = jnp.einsum('bsd,fd->bsf', xn, W1)
        pair = jax.nn.relu(h[:, :, None, :] - h[:, None, :, :] + b1)
        pair = jax.nn.relu(jnp.einsum('bijf,gf->bijg', pair, W2) + b2)
        sim = jnp.einsum('bijg,og->bijo', pair, W3)[..., 0] + b3[0]
        diag = jnp.arange(S)
        sim = sim.at[:, diag, diag].set(0.0)
        k_sparse = max(1, int(S * SPARSITY))
        _, top_idx = jax.lax.top_k(sim, k_sparse)
        mask = jnp.full((B, S, S), -jnp.inf, dtype=x.dtype)
        bidx = jnp.arange(B)[:, None, None]
        iidx = jnp.arange(S)[None, :, None]
        mask = mask.at[bidx, iidx, top_idx].set(0.0)
        qkv = jnp.einsum('bsd,ed->bse', xn, Wqkv) + bqkv
        q, k, v = jnp.split(qkv, 3, axis=-1)

        def heads(t):
            return t.reshape(B, S, NUM_HEADS, HEAD_DIM).transpose(0, 2, 1, 3)
        q, k, v = (heads(q), heads(k), heads(v))
        scores = jnp.einsum('bhid,bhjd->bhij', q, k) / math.sqrt(HEAD_DIM)
        scores = scores + mask[:, None, :, :]
        attn = jax.nn.softmax(scores, axis=-1)
        ao = jnp.einsum('bhij,bhjd->bhid', attn, v)
        ao = ao.transpose(0, 2, 1, 3).reshape(B, S, K)
        out = jnp.einsum('bsk,dk->bsd', ao, Wout) + bout
        return x + out

    def _L1_ffn_ref(x, weight, scale_weight, bias):
        import jax, jax.numpy as jnp
        import numpy as np
        w = weight * scale_weight[:, None]
        out = jnp.einsum('bsi,oi->bso', x, w) + bias
        return out
    x = L0_attn_x
    x = x + _L0_attn_ref(_layernorm(x, axis=-1), L0_attn_Wq, L0_attn_bq, L0_attn_Wk, L0_attn_bk, L0_attn_Wv, L0_attn_bv, L0_attn_Wo, L0_attn_bo)
    x = x + _L0_ffn_ref(_layernorm(x, axis=-1), L0_ffn_router_w, L0_ffn_router_bias, L0_ffn_wg, L0_ffn_wu, L0_ffn_wd, L0_ffn_swg, L0_ffn_swu, L0_ffn_swd)
    x = x + _L1_attn_ref(_layernorm(x, axis=-1), L1_attn_gamma, L1_attn_beta, L1_attn_W1, L1_attn_b1, L1_attn_W2, L1_attn_b2, L1_attn_W3, L1_attn_b3, L1_attn_Wqkv, L1_attn_bqkv, L1_attn_Wout, L1_attn_bout)
    x = x + _L1_ffn_ref(_layernorm(x, axis=-1), L1_ffn_weight, L1_ffn_scale_weight, L1_ffn_bias)
    return x

_drawn_inputs = setup_inputs


def setup_inputs(seed=0):
    import zlib

    import numpy as np

    out = dict(_drawn_inputs(seed))
    spreads = {'L0_ffn_router_bias': (0.0, 0.8),
     'L1_attn_gamma': (1.0, 0.6),
     'L1_attn_beta': (0.0, 0.8),
     'L1_attn_b1': (0.0, 0.8),
     'L1_attn_b2': (0.0, 0.8),
     'L1_attn_bqkv': (0.0, 0.8),
     'L1_attn_bout': (0.0, 0.712)}
    factors = {'L0_attn_Wq': 8.0,
     'L0_attn_bq': 8.0,
     'L0_attn_Wk': 8.0,
     'L0_attn_bk': 64.0,
     'L0_attn_Wv': 8.0,
     'L0_attn_bv': 8.0,
     'L0_attn_Wo': 8.0,
     'L0_attn_bo': 5.999,
     'L0_ffn_router_w': 8.0,
     'L0_ffn_wg': 8.0,
     'L0_ffn_wu': 8.0,
     'L0_ffn_wd': 8.0,
     'L1_attn_W1': 8.0,
     'L1_attn_W2': 8.0,
     'L1_attn_W3': 8.0,
     'L1_attn_Wqkv': 8.0,
     'L1_attn_Wout': 5.992,
     'L1_ffn_bias': 28.242,
     'L1_ffn_scale_weight': 5.342}
    for name, (base, spread) in spreads.items():
        noise = np.random.default_rng([zlib.crc32(name.encode()), seed]).standard_normal(out[name].shape)
        drawn = base * np.exp(spread * noise) if base else spread * noise
        out[name] = jnp.asarray(drawn.astype(out[name].dtype))
    for name, factor in factors.items():
        out[name] = (out[name] * factor).astype(out[name].dtype)
    return out
```

```python
from contextlib import ExitStack

import concourse.bass as bass
from concourse import mybir

F32 = mybir.dt.float32
BF16 = mybir.dt.bfloat16
ALU = mybir.AluOpType
ACT = mybir.ActivationFunctionType
AX = mybir.AxisListType

P = 128
B, S, D = 4, 512, 256
N = B * S
TB = S // P
TILES = N // P
C = D // P
EPS = 1e-5
HEADS0, HD0 = 4, 64
EXPERTS, FE, TOPK = 64, 64, 4
SHARED = 512
HT = (EXPERTS * FE + SHARED) // P
HEADS1, HD1, KW = 32, 2, 64
G = HEADS1 // 4
KEEP = int(S * 0.1)
GONE = -3.0e38
OFF = float(2.0 ** 126)


class Tally:

    def __init__(self, t=0, per=0, start=0):
        self.base, self.n = t * per + start, 0

    def up(self):
        self.n += 1
        return 1

    def now(self):
        return self.base + self.n


def pause(eng, k):
    eng.sem_inc(k.passed, 1)


def chunked(ap):
    return ap.rearrange("(p c) n -> p c n", c=C)


def column(ap):
    return ap.rearrange("(p a) -> p a", a=1)


def everyone(ap):
    return ap.partition_broadcast(P)


class Kernel:
    def __init__(self, nc, ctx, ins, out):
        self.nc, self.ctx, self.i, self.out = nc, ctx, ins, out

    def sem(self, name):
        return self.ctx.enter_context(self.nc.semaphore(name))


def load_and_constants(k):
    nc = k.nc
    x_in, ident_step = k.sem("x_in"), k.sem("ident_step")
    with nc.Block() as block:
        @block.sync
        def _(sp):
            for t in range(4):
                sp.dma_start(k.x[:, 4 * t:4 * t + 4, :],
                             k.i["L0_attn_x"].rearrange("b (t p) d -> b p t d", p=P)[t]).then_inc(x_in, 16)
            sp.wait_ge(x_in, 64)

        @block.gpsimd
        def _(pool):
            pool.memset(k.ident[:, :], 0.0).then_inc(ident_step, 1)
            pool.memset(k.identb[:, :], 0.0).then_inc(ident_step, 1)
            pool.wait_ge(ident_step, 2)
            for m in (k.ident, k.identb):
                pool.affine_select(out=m[:, :], in_=m[:, :], compare_op=ALU.not_equal, fill=1.0, base=0,
                                   pattern=[[-1, P]], channel_multiplier=1).then_inc(ident_step, 1)
            pool.wait_ge(ident_step, 4)


def row_statistics(k, tag, src):
    nc = k.nc
    tile_done, step, root = k.sem(tag + "_tile_done"), k.sem(tag + "_step"), k.sem(tag + "_root")
    with ExitStack() as local:
        def sb(name, shape, dt=F32):
            return local.enter_context(nc.sbuf_tensor(tag + name, shape, dt))
        stats = sb("stats", [P, TILES, 6])
        half, spread, var, std, r0, r1 = (sb(n, [P, TILES]) for n in ("half", "spread", "var", "std", "r0", "r1"))
        block = local.enter_context(nc.Block())
        flat = src[:, :, :].rearrange("p t d -> p (t d)")
        sflat = stats[:, :, :].rearrange("p t d -> p (t d)")

        @block.vector
        def _(ve):
            with ve.Fori(0, TILES) as t:
                ve.bn_stats(sflat[:, bass.ds(t * 6, 6)], flat[:, bass.ds(t * D, D)]).then_inc(tile_done, 1)
            ve.wait_ge(tile_done, TILES)
            n = Tally()
            ve.tensor_tensor(k.mean[:, :], stats[:, :, 1], stats[:, :, 4], ALU.add).then_inc(step, n.up())
            ve.tensor_tensor(half[:, :], stats[:, :, 1], stats[:, :, 4], ALU.subtract).then_inc(step, n.up())
            ve.tensor_tensor(spread[:, :], stats[:, :, 2], stats[:, :, 5], ALU.add).then_inc(step, n.up())
            ve.wait_ge(step, n.now())
            ve.tensor_scalar(k.mean[:, :], k.mean[:, :], 0.5, None, ALU.mult).then_inc(step, n.up())
            ve.scalar_tensor_tensor(out=half[:, :], in0=half[:, :], scalar=0.25, in1=half[:, :],
                                    op0=ALU.mult, op1=ALU.mult).then_inc(step, n.up())
            ve.tensor_scalar(spread[:, :], spread[:, :], 1.0 / D, EPS, ALU.mult, ALU.add).then_inc(step, n.up())
            ve.wait_ge(step, n.now())
            ve.tensor_tensor(var[:, :], half[:, :], spread[:, :], ALU.add).then_inc(step, n.up())
            ve.wait_ge(root, 1)
            ve.reciprocal(r0[:, :], std[:, :]).then_inc(step, n.up())
            ve.wait_ge(step, n.now())
            ve.tensor_tensor(r1[:, :], r0[:, :], r0[:, :], ALU.mult).then_inc(step, n.up())
            ve.wait_ge(step, n.now())
            ve.tensor_tensor(r1[:, :], r1[:, :], var[:, :], ALU.mult).then_inc(step, n.up())
            ve.wait_ge(step, n.now())
            ve.tensor_scalar(r1[:, :], r1[:, :], -0.5, 1.5, ALU.mult, ALU.add).then_inc(step, n.up())
            ve.wait_ge(step, n.now())
            ve.tensor_tensor(k.rstd[:, :], r0[:, :], r1[:, :], ALU.mult).then_inc(step, n.up())
            ve.wait_ge(step, n.now())

        @block.scalar
        def _(act):
            act.wait_ge(step, 7)
            act.activation(std[:, :], var[:, :], ACT.Sqrt).then_inc(root, 1)


def normalise_tile(ve, k, src, dst, b, i):
    t = b * TB + i
    flat = src[:, :, :].rearrange("p t d -> p (t d)")
    return ve.tensor_scalar(dst[:, i, :], flat[:, bass.ds(t * D, D)], k.mean[:, bass.ds(t, 1)],
                            k.rstd[:, bass.ds(t, 1)], ALU.subtract, ALU.mult)


def transpose_features(pe, k, psum, rows, i, c):
    picked = rows[:, i, :].rearrange("p (f c) -> p f c", c=C)[:, :, c]
    return pe.transpose(psum[:, i * P:(i + 1) * P], picked, k.ident[:, :])


def first_attention(k):
    nc = k.nc
    i = k.i
    UNITS = HEADS0 * TB
    loaded = k.sem("a0_loaded")
    normed, turned, xt_ready = k.sem("a0_normed"), k.sem("a0_turned"), k.sem("a0_xt_ready")
    qk_done, qk_ready, v_done, v_ready = (k.sem("a0_" + n) for n in ("qk_done", "qk_ready", "v_done", "v_ready"))
    scored, peak, exped, inverse, weighted, wt_done, wt_ready = (
        k.sem("a0_" + n) for n in ("scored", "peak", "exped", "inverse", "weighted", "wt_done", "wt_ready"))
    mixed, mixed_ready, out_done, out_step = (k.sem("a0_" + n) for n in ("mixed", "mixed_ready", "out_done", "out_step"))
    with ExitStack() as local:
        def sb(name, shape, dt=F32):
            return local.enter_context(nc.sbuf_tensor("a0" + name, shape, dt))
        wq, wk, wv, wo = (sb(n, [P, C, D]) for n in ("wq", "wk", "wv", "wo"))
        bq, bk = sb("bq", [P, 2]), sb("bk", [P, 2])
        bv, bo = sb("bv", [P, D]), sb("bo", [P, D])
        rows = sb("rows", [P, TB, D])
        xt = sb("xt", [P, C, S])
        qt, kt = sb("qt", [P, 2, S]), sb("kt", [P, 2, S])
        v = sb("v", [P, TB, D])
        negpeak, total, inv = (sb(n, [P, UNITS]) for n in ("negpeak", "total", "inv"))
        w = sb("w", [P, 2, S])
        wt = sb("wt", [P, 2, TB, S])
        ft = sb("ft", [P, 2, S])
        tmp = sb("tmp", [P, 2, S])
        bank = local.enter_context(nc.psum_tensor("a0bank", [P, 8, 512], F32))
        xflat = k.x[:, :, :].rearrange("p t d -> p (t d)")
        block = local.enter_context(nc.Block())

        @block.sync
        def _(sp):
            sp.dma_start(wq[:, :, :], chunked(i["L0_attn_Wq"])).then_inc(loaded, 16)
            sp.dma_start(wk[:, :, :], chunked(i["L0_attn_Wk"])).then_inc(loaded, 16)
            sp.dma_start(wv[:, :, :], chunked(i["L0_attn_Wv"])).then_inc(loaded, 16)
            sp.dma_start(wo[:, :, :], i["L0_attn_Wo"].rearrange("(c p) n -> p c n", p=P)).then_inc(loaded, 16)
            for m in range(2):
                sp.dma_start(bq[:, m:m + 1], column(i["L0_attn_bq"][m * P:(m + 1) * P])).then_inc(loaded, 16)
                sp.dma_start(bk[:, m:m + 1], column(i["L0_attn_bk"][m * P:(m + 1) * P])).then_inc(loaded, 16)
            sp.dma_start(bv[:, :], everyone(i["L0_attn_bv"])).then_inc(loaded, 16)
            sp.dma_start(bo[:, :], everyone(i["L0_attn_bo"])).then_inc(loaded, 16)
        LOADED = 16 * 10

        def weigh(ve, b, u):
            ve.wait_ge(exped, b * UNITS + u + 1)
            ve.reciprocal(inv[:, u:u + 1], total[:, u:u + 1]).then_inc(inverse, 1)
            ve.wait_ge(inverse, b * UNITS + u + 1)
            ve.tensor_scalar(w[:, u % 2, :], w[:, u % 2, :], inv[:, u:u + 1], None, ALU.mult).then_inc(weighted, 1)

        @block.vector
        def _(ve):
            ve.wait_ge(loaded, LOADED)
            with ve.Fori(0, B) as b:
                for j in range(TB):
                    normalise_tile(ve, k, k.x, rows, b, j).then_inc(normed, 1)
                for h in range(2):
                    ve.wait_ge(v_done, b * 2 + h + 1)
                    ve.tensor_tensor(v[:, 2 * h:2 * h + 2, :],
                                     bank[:, 6 + h, :].rearrange("p (t n) -> p t n", t=2),
                                     bv[:, :].unsqueeze(1).broadcast_to([P, 2, D]), ALU.add).then_inc(v_ready, 1)
                for u in range(UNITS):
                    ve.wait_ge(scored, b * UNITS + u + 1)
                    ve.tensor_reduce(negpeak[:, u:u + 1], bank[:, 2 + u % 2, :], AX.X, ALU.max,
                                     negate=True).then_inc(peak, 1)
                    ve.wait_ge(peak, b * 2 * UNITS + 2 * u + 1)
                    ve.tensor_scalar(negpeak[:, u:u + 1], negpeak[:, u:u + 1], 0.5, None,
                                     ALU.mult).then_inc(peak, 1)
                    if u:
                        weigh(ve, b, u - 1)
                weigh(ve, b, UNITS - 1)
                for h in range(2):
                    ve.wait_ge(out_done, b * 2 + h + 1)
                    ve.tensor_tensor(tmp[:, h, :].rearrange("p (t n) -> p t n", t=2),
                                     bank[:, 6 + h, :].rearrange("p (t n) -> p t n", t=2),
                                     bo[:, :].unsqueeze(1).broadcast_to([P, 2, D]), ALU.add).then_inc(out_step, 1)
                for h in range(2):
                    at = b * (TB * D) + h * S
                    ve.wait_ge(out_step, b * 4 + 2)
                    ve.tensor_tensor(xflat[:, bass.ds(at, S)], xflat[:, bass.ds(at, S)], tmp[:, h, :],
                                     ALU.add).then_inc(out_step, 1)
                ve.wait_ge(out_step, b * 4 + 4)


        def turned_weights(act, b, u):
            h, q = divmod(u, TB)
            if q == 0 and h >= 1:
                mixed_head(act, b, h - 1)
            act.wait_ge(wt_done, b * UNITS + u + 1)
            act.activation(wt[:, h % 2, :, q * P:(q + 1) * P],
                           bank[:, u % 2, :].rearrange("p (j s) -> p j s", j=TB), ACT.Copy).then_inc(wt_ready, 1)

        def mixed_head(act, b, h):
            rows_of = slice(HD0 * (h % 2), HD0 * (h % 2) + HD0)
            act.wait_ge(mixed, b * HEADS0 + h + 1)
            act.activation(ft[rows_of, h // 2, :], bank[rows_of, 4 + h % 2, :], ACT.Copy).then_inc(mixed_ready, 1)

        @block.scalar
        def _(act):
            act.wait_ge(loaded, LOADED)
            with act.Fori(0, B) as b:
                for c in range(C):
                    act.wait_ge(turned, b * C + c + 1)
                    act.activation(xt[:, c, :], bank[:, c, :], ACT.Copy).then_inc(xt_ready, 1)
                for m in range(4):
                    act.wait_ge(qk_done, b * 4 + m + 1)
                    dst, bias = (qt, bq) if m < 2 else (kt, bk)
                    act.activation(dst[:, m % 2, :], bank[:, 2 + m, :], ACT.Identity,
                                   bias=bias[:, m % 2:m % 2 + 1]).then_inc(qk_ready, 1)
                for u in range(UNITS):
                    act.wait_ge(peak, b * 2 * UNITS + 2 * u + 2)
                    if u >= 2:
                        act.wait_ge(wt_done, b * UNITS + u - 1)
                    act.activation(w[:, u % 2, :], bank[:, 2 + u % 2, :], ACT.Exp, bias=negpeak[:, u:u + 1],
                                   scale=0.5, accum_out=total[:, u:u + 1]).then_inc(exped, 1)
                    if u:
                        turned_weights(act, b, u - 1)
                turned_weights(act, b, UNITS - 1)
                mixed_head(act, b, HEADS0 - 1)



        def turn_weights(pe, b, u):
            h, q = divmod(u, TB)
            pe.wait_ge(weighted, b * UNITS + u + 1)
            if u >= 2:
                pe.wait_ge(wt_ready, b * UNITS + u - 1)
            for j in range(TB):
                mm = pe.transpose(bank[:, u % 2, j * P:(j + 1) * P], w[:, u % 2, j * P:(j + 1) * P], k.ident[:, :])
            mm.then_inc(wt_done, 1)
            if q == TB - 1:
                pe.wait_ge(wt_ready, b * UNITS + u + 1)
                if h >= 2:
                    pe.wait_ge(mixed_ready, b * HEADS0 + h - 1)
                rows_of = slice(HD0 * (h % 2), HD0 * (h % 2) + HD0)
                for j in range(TB):
                    mm = pe.matmul(bank[rows_of, 4 + h % 2, :], v[:, j, h * HD0:(h + 1) * HD0], wt[:, h % 2, j, :],
                                   start=j == 0, stop=j == TB - 1)
                mm.then_inc(mixed, 1)

        @block.tensor
        def _(pe):
            pe.wait_ge(loaded, LOADED)
            with pe.Fori(0, B) as b:
                pe.wait_ge(normed, b * TB + TB)
                for c in range(C):
                    for j in range(TB):
                        mm = transpose_features(pe, k, bank[:, c, :], rows, j, c)
                    mm.then_inc(turned, 1)
                pe.wait_ge(xt_ready, b * C + C)
                for m in range(4):
                    wts = wq if m < 2 else wk
                    for c in range(C):
                        mm = pe.matmul(bank[:, 2 + m, :], wts[:, c, (m % 2) * P:(m % 2) * P + P], xt[:, c, :],
                                       start=c == 0, stop=c == C - 1)
                    mm.then_inc(qk_done, 1)
                for j in range(TB):
                    for c in range(C):
                        mm = pe.matmul(bank[:, 6 + j // 2, (j % 2) * D:(j % 2) * D + D],
                                       xt[:, c, j * P:(j + 1) * P], wv[:, c, :], start=c == 0, stop=c == C - 1)
                    if j % 2:
                        mm.then_inc(v_done, 1)
                pe.wait_ge(qk_ready, b * 4 + 4)
                pe.wait_ge(v_ready, b * 2 + 2)
                for u in range(UNITS + 1):
                    if u < UNITS:
                        h, q = divmod(u, TB)
                        if u >= 2:
                            pe.wait_ge(exped, b * UNITS + u - 1)
                        r = HD0 * (h % 2)
                        pe.matmul(bank[:, 2 + u % 2, :], qt[r:r + HD0, h // 2, q * P:(q + 1) * P],
                                  kt[r:r + HD0, h // 2, :], start=True, stop=True).then_inc(scored, 1)
                    if u:
                        turn_weights(pe, b, u - 1)
                for j in range(TB):
                    if j == 0:
                        pe.wait_ge(mixed_ready, b * HEADS0 + HEADS0)
                    for m in range(2):
                        mm = pe.matmul(bank[:, 6 + j // 2, (j % 2) * D:(j % 2) * D + D],
                                       ft[:, m, j * P:(j + 1) * P], wo[:, m, :], start=m == 0, stop=m == 1)
                    if j % 2:
                        mm.then_inc(out_done, 1)
                pe.wait_ge(out_step, b * 4 + 2)



def router(k):
    nc, i = k.nc, k.i
    loaded, set_up = k.sem("r_loaded"), k.sem("r_set_up")
    normed, turned, xt_ready = k.sem("r_normed"), k.sem("r_turned"), k.sem("r_xt_ready")
    logit_done, logit_ready, logit_turned = k.sem("r_logit_done"), k.sem("r_logit_ready"), k.sem("r_logit_turned")
    step, exped, comb_turned, comb_ready, stored = (k.sem("r_" + n) for n in (
        "step", "exped", "comb_turned", "comb_ready", "stored"))
    PAD = EXPERTS + 8
    with ExitStack() as local:
        def sb(name, shape, dt=F32):
            return local.enter_context(nc.sbuf_tensor("r" + name, shape, dt))
        wr, bias = sb("wr", [P, C, EXPERTS]), sb("bias", [P, EXPERTS])
        rows = sb("rows", [P, TB, D])
        logit_t = sb("logit_t", [EXPERTS, S])
        logit = sb("logit", [P, TB, EXPERTS])
        ranked = sb("ranked", [P, TB, PAD])
        best, cap = sb("best", [P, TB, 8]), sb("cap", [P, 8])
        negpeak, total, inv = sb("negpeak", [P, TB]), sb("total", [P, TB]), sb("inv", [P, TB])
        picked, inv2 = sb("picked", [P, TB]), sb("inv2", [P, TB])
        share = sb("share", [P, TB, EXPERTS])
        comb_t = sb("comb_t", [EXPERTS, S])
        ones = sb("ones", [SHARED // FE, N])
        bank = local.enter_context(nc.psum_tensor("rbank", [P, 8, 512], F32))
        block = local.enter_context(nc.Block())
        xt_flat = k.xt[:, :, :].rearrange("p c n -> p (c n)")

        @block.sync
        def _(sp):
            sp.dma_start(wr[:, :, :], chunked(i["L0_ffn_router_w"])).then_inc(loaded, 16)
            sp.dma_start(bias[:, :], everyone(i["L0_ffn_router_bias"])).then_inc(loaded, 16)
            sp.wait_ge(set_up, 3)
            sp.dma_start(k.shares_dram[EXPERTS:, :], ones[:, :]).then_inc(stored, 16)
            with sp.Fori(0, B) as b:
                sp.wait_ge(comb_ready, b + 1)
                pause(sp, k)
                sp.dma_start(k.shares_dram[0:EXPERTS, bass.ds(b * S, S)], comb_t[:, :]).then_inc(stored, 16)
                sp.wait_ge(stored, b * 16 + 32)
                pause(sp, k)

        @block.gpsimd
        def _(pool):
            pool.memset(cap[:, 0:TOPK], -GONE).then_inc(set_up, 1)
            pool.memset(cap[:, TOPK:8], GONE).then_inc(set_up, 1)
            pool.memset(ones[:, :], 1.0).then_inc(set_up, 1)

        @block.vector
        def _(ve):
            ve.wait_ge(loaded, 32)
            ve.wait_ge(set_up, 3)
            with ve.Fori(0, B) as b:
                for j in range(TB):
                    normalise_tile(ve, k, k.x, rows, b, j).then_inc(normed, 1)
                n = Tally(b, 4 * TB + 9)
                ve.wait_ge(logit_turned, b + 1)
                turned_logits = bank[:, 3, 0:TB * EXPERTS].rearrange("p (t e) -> p t e", t=TB)
                ve.tensor_copy(logit[:, :, :], turned_logits).then_inc(step, n.up())
                ve.memset(ranked[:, :, EXPERTS:PAD], GONE).then_inc(step, n.up())
                ve.wait_ge(step, n.now())
                ve.tensor_reduce(negpeak[:, :], logit[:, :, :], AX.X, ALU.max, negate=True).then_inc(step, n.up())
                ve.tensor_tensor(ranked[:, :, 0:EXPERTS], logit[:, :, :],
                                 bias[:, :].unsqueeze(1).broadcast_to([P, TB, EXPERTS]), ALU.add).then_inc(step, n.up())
                ve.wait_ge(step, n.now())
                pause(ve, k)
                for j in range(TB):
                    ve.max(best[:, j, :], ranked[:, j, :]).then_inc(step, n.up())
                ve.wait_ge(step, n.now())
                ve.tensor_tensor(best[:, :, :], best[:, :, :], cap[:, :].unsqueeze(1).broadcast_to([P, TB, 8]),
                                 ALU.min).then_inc(step, n.up())
                ve.wait_ge(step, n.now())
                pause(ve, k)
                for j in range(TB):
                    ve.match_replace(ranked[:, j, :], best[:, j, :], ranked[:, j, :], GONE).then_inc(step, n.up())
                ve.wait_ge(exped, b * TB + TB)
                ve.reciprocal(inv[:, :], total[:, :]).then_inc(step, n.up())
                ve.wait_ge(step, n.now())
                for j in range(TB):
                    ve.tensor_scalar(share[:, j, :], share[:, j, :], inv[:, j:j + 1], None, ALU.mult).then_inc(step, n.up())
                ve.wait_ge(step, n.now())
                for j in range(TB):
                    ve.scalar_tensor_tensor(out=share[:, j, :], in0=ranked[:, j, 0:EXPERTS], scalar=GONE,
                                            in1=share[:, j, :], op0=ALU.is_equal, op1=ALU.mult).then_inc(step, n.up())
                ve.wait_ge(step, n.now())
                ve.tensor_reduce(picked[:, :], share[:, :, :], AX.X, ALU.add).then_inc(step, n.up())
                ve.wait_ge(step, n.now())
                ve.reciprocal(inv2[:, :], picked[:, :]).then_inc(step, n.up())
                ve.wait_ge(step, n.now())
                ve.tensor_tensor(share[:, :, :], share[:, :, :],
                                 inv2[:, :].unsqueeze(2).broadcast_to([P, TB, EXPERTS]), ALU.mult).then_inc(step, n.up())
                assert n.n == 4 * TB + 9, n.n

        @block.scalar
        def _(act):
            with act.Fori(0, B) as b:
                for c in range(C):
                    act.wait_ge(turned, b * C + c + 1)
                    act.activation(xt_flat[:, bass.ds(b * S + c * N, S)], bank[:, c, :], ACT.Copy).then_inc(xt_ready, 1)
                act.wait_ge(logit_done, b + 1)
                act.activation(logit_t[:, :], bank[0:EXPERTS, 2, :], ACT.Copy).then_inc(logit_ready, 1)
                act.wait_ge(step, b * (4 * TB + 9) + 3)
                for j in range(TB):
                    act.activation(share[:, j, :], logit[:, j, :], ACT.Exp, bias=negpeak[:, j:j + 1],
                                   accum_out=total[:, j:j + 1]).then_inc(exped, 1)
                act.wait_ge(comb_turned, b + 1)
                act.wait_ge(stored, b * 16 + 16)
                act.activation(comb_t[:, :], bank[0:EXPERTS, 4, :], ACT.Copy).then_inc(comb_ready, 1)

        @block.tensor
        def _(pe):
            pe.wait_ge(loaded, 32)
            with pe.Fori(0, B) as b:
                pe.wait_ge(normed, b * TB + TB)
                for c in range(C):
                    for j in range(TB):
                        mm = transpose_features(pe, k, bank[:, c, :], rows, j, c)
                    mm.then_inc(turned, 1)
                pe.wait_ge(xt_ready, b * C + C)
                pause(pe, k)
                for c in range(C):
                    mm = pe.matmul(bank[0:EXPERTS, 2, :], wr[:, c, :], xt_flat[:, bass.ds(b * S + c * N, S)],
                                   start=c == 0, stop=c == C - 1)
                mm.then_inc(logit_done, 1)
                pe.wait_ge(logit_ready, b + 1)
                pause(pe, k)
                for j in range(TB):
                    mm = pe.transpose(bank[:, 3, j * EXPERTS:(j + 1) * EXPERTS], logit_t[:, j * P:(j + 1) * P],
                                      k.ident[0:EXPERTS, 0:EXPERTS])
                mm.then_inc(logit_turned, 1)
                pe.wait_ge(step, b * (4 * TB + 9) + 4 * TB + 9)
                pause(pe, k)
                for j in range(TB):
                    mm = pe.transpose(bank[0:EXPERTS, 4, j * P:(j + 1) * P], share[:, j, :], k.ident[:, :])
                mm.then_inc(comb_turned, 1)
                pe.wait_ge(comb_ready, b + 1)


def experts(k):
    nc, i = k.nc, k.i
    H = N // 2
    R = 4
    gate_in, up_in, down_in, share_in = ([k.sem(f"e_{n}{r}") for r in range(R)] for n in (
        "gate_in", "up_in", "down_in", "share_in"))
    hidden_done, gated, scaled, hidden_ready, down_done = (k.sem("e_" + n) for n in (
        "hidden_done", "gated", "scaled", "hidden_ready", "down_done"))
    cleared, added = k.sem("e_cleared"), k.sem("e_added")
    with ExitStack() as local:
        def sb(name, shape, dt=F32):
            return local.enter_context(nc.sbuf_tensor("e" + name, shape, dt))
        wg, wu = sb("wg", [P, R, C, 2, FE]), sb("wu", [P, R, C, 2, FE])
        wd = sb("wd", [P, R, D])
        shares = sb("shares", [P, R, H])
        sg = sb("sg", [P, 2, S])
        sgs = sb("sgs", [P, 2, S])
        hid = sb("hid", [P, 2, S])
        gu = local.enter_context(nc.psum_tensor("egu", [P, 4, 512], F32))
        acc = local.enter_context(nc.psum_tensor("eacc", [P, 4, 512], F32))
        xflat = k.x[:, :, :].rearrange("p t d -> p (t d)")
        xt_flat = k.xt[:, :, :].rearrange("p c n -> p (c n)")
        block = local.enter_context(nc.Block())
        wgr = i["L0_ffn_wg"].rearrange("e (p c) f -> p e c f", c=C)
        wur = i["L0_ffn_wu"].rearrange("e (p c) f -> p e c f", c=C)
        wdr = i["L0_ffn_wd"].rearrange("e f d -> (e f) d")
        sgr = i["L0_ffn_swg"].rearrange("s (p c) (q f) -> p s q c f", c=C, f=FE)
        sur = i["L0_ffn_swu"].rearrange("s (p c) (q f) -> p s q c f", c=C, f=FE)
        sdr = i["L0_ffn_swd"].rearrange("s h d -> (s h) d")
        flat = lambda w, r, c: w[:, r, c, :, :].rearrange("p e f -> p (e f)")

        def fetch(sp, tile, r, use, half, shared=None):
            sp.wait_ge(down_done, use)
            pause(sp, k)
            if shared is None:
                for e in range(2):
                    one = bass.ds(tile * 2 + e, 1)
                    sp.dma_start(wg[:, r, :, e, :], wgr[:, one, :, :].rearrange("p e c f -> p (e c) f")).then_inc(gate_in[r], 16)
                    sp.dma_start(wu[:, r, :, e, :], wur[:, one, :, :].rearrange("p e c f -> p (e c) f")).then_inc(up_in[r], 16)
                sp.dma_start(wd[:, r, :], wdr[bass.ds(tile * P, P), :]).then_inc(down_in[r], 16)
            else:
                s, q = divmod(2 * shared, 4)
                for e in range(2):
                    sp.dma_start(wg[:, r, :, e, :], sgr[:, s, q + e, :, :]).then_inc(gate_in[r], 16)
                    sp.dma_start(wu[:, r, :, e, :], sur[:, s, q + e, :, :]).then_inc(up_in[r], 16)
                sp.dma_start(wd[:, r, :], sdr[shared * P:shared * P + P, :]).then_inc(down_in[r], 16)
            for e in range(2):
                row = tile * 2 + e
                sp.dma_start(shares[e * FE:(e + 1) * FE, r, :],
                             k.shares_dram[bass.ds(row, 1), bass.ds(half * H, H)]
                             .broadcast_to([FE, H])).then_inc(share_in[r], 16)

        @block.sync
        def _(sp):
            with sp.Fori(0, 2) as half:
                with sp.Fori(0, EXPERTS // 2 // R) as m:
                    for r in range(R):
                        fetch(sp, m * R + r, r, half * (2 * HT) + m * (2 * R) + 2 * r + 2, half)
                for r in range(R):
                    t = EXPERTS // 2 + r
                    fetch(sp, t, r, half * (2 * HT) + 2 * t + 2, half, shared=r)

        LAST = 2 * HT

        def down(pe, r, q, t0, use):
            if q == 0:
                pe.wait_ge(down_in[r], use * 16 + 16)
            pe.wait_ge(hidden_ready, t0 * 2 + q + 1)
            for j in range(TB):
                tok = q * TB + j
                mm = pe.matmul(acc[:, tok // 2, (tok % 2) * D:(tok % 2) * D + D], hid[:, q, j * P:(j + 1) * P],
                               wd[:, r, :], start=False, stop=False, skip_group_check=True)
            mm.then_inc(down_done, 1)

        @block.tensor
        def _(pe):
            pe.sem_inc(down_done, 2 * R)
            with pe.Fori(0, 2) as half:
                pe.wait_ge(cleared, half * 4 + 4)
                pause(pe, k)
                with pe.Fori(0, HT // R) as m:
                    for r in range(R):
                        use = half * (HT // R) + m
                        t0 = use * R + r
                        pe.wait_ge(gate_in[r], use * 32 + 32)
                        pe.wait_ge(up_in[r], use * 32 + 32)
                        for q in range(2):
                            pe.wait_ge(scaled, t0 * 2 + q + 1)
                            pause(pe, k)
                            for w, z in ((wg, 0), (wu, 1)):
                                for c in range(C):
                                    mm = pe.matmul(gu[:, 2 * q + z, :],
                                                   flat(w, r, c),
                                                   xt_flat[:, bass.ds(half * H + (q * S + c * N), S)],
                                                   start=c == 0, stop=c == C - 1)
                                mm.then_inc(hidden_done, 1)
                            if q:
                                down(pe, r, 0, t0, use)
                        down(pe, r, 1, t0, use)


        @block.scalar
        def _(act):
            with act.Fori(0, 2 * HT) as t:
                for q in range(2):
                    act.wait_ge(hidden_done, t * 4 + 2 * q + 1)
                    act.wait_ge(scaled, t * 2 + q + 1)
                    act.activation(sg[:, q, :], gu[:, 2 * q, :], ACT.Silu).then_inc(gated, 1)

        @block.vector
        def _(ve):
            ve.sem_inc(scaled, 2)
            with ve.Fori(0, 2) as half:
                for z in range(4):
                    ve.memset(acc[:, z, :], 0.0).then_inc(cleared, 1)
                with ve.Fori(0, HT // R) as m:
                    for r in range(R):
                        use = half * (HT // R) + m
                        t0 = use * R + r
                        ve.wait_ge(share_in[r], use * 32 + 32)
                        for q in range(2):
                            ve.wait_ge(gated, t0 * 2 + q + 1)
                            ve.wait_ge(hidden_done, t0 * 4 + 2 * q + 2)
                            ve.tensor_tensor(sgs[:, q, :], gu[:, 2 * q + 1, :], sg[:, q, :], ALU.mult).then_inc(scaled, 1)
                            ve.wait_ge(scaled, t0 * 2 + q + 3)
                            ve.wait_ge(down_done, t0 * 2 + (q + 2 * R - 1))
                            ve.tensor_tensor(hid[:, q, :], sgs[:, q, :], shares[:, r, q * S:(q + 1) * S],
                                             ALU.mult).then_inc(hidden_ready, 1)
                ve.wait_ge(down_done, half * LAST + LAST + 2 * R)
                for z in range(4):
                    at = half * (N // 2 // P * D) + z * 512
                    ve.tensor_tensor(xflat[:, bass.ds(at, 512)], xflat[:, bass.ds(at, 512)], acc[:, z, :],
                                     ALU.add).then_inc(added, 1)
                ve.wait_ge(added, half * 4 + 4)


ROW0 = 3
SLOTS = ((slice(0, 3), slice(3, 5), slice(5, 6)), (slice(1, 6, 2), slice(2, 5, 2), slice(0, 1)))
PRODUCTS = 6


def turn_weights_once(k):
    nc, i = k.nc, k.i
    loaded, scaled, turned, ready = (k.sem("w_" + n) for n in ("loaded", "scaled", "turned", "ready"))
    with ExitStack() as local:
        def sb(name, shape, dt=F32):
            return local.enter_context(nc.sbuf_tensor("w" + name, shape, dt))
        w1, w2 = sb("w1", [P, D]), sb("w2", [KW, P])
        wqk, wv = sb("wqk", [P, D]), sb("wv", [KW, D])
        wout, wf = sb("wout", [P, C, KW]), sb("wf", [P, C, D])
        wfs, scale = sb("wfs", [P, C, D]), sb("scale", [P, C])
        bank = local.enter_context(nc.psum_tensor("wbank", [P, 8, 512], F32))
        block = local.enter_context(nc.Block())
        wqkv = i["L1_attn_Wqkv"]

        @block.sync
        def _(sp):
            sp.dma_start(w1[:, :], i["L1_attn_W1"]).then_inc(loaded, 16)
            sp.dma_start(w2[:, :], i["L1_attn_W2"]).then_inc(loaded, 16)
            sp.dma_start(wqk[:, :], wqkv[0:P, :]).then_inc(loaded, 16)
            sp.dma_start(wv[:, :], wqkv[P:P + KW, :]).then_inc(loaded, 16)
            sp.dma_start(wout[:, :, :], i["L1_attn_Wout"].rearrange("(o p) n -> p o n", p=P)).then_inc(loaded, 16)
            sp.dma_start(wf[:, :, :], i["L1_ffn_weight"].rearrange("(o p) n -> p o n", p=P)).then_inc(loaded, 16)
            for o in range(2):
                sp.dma_start(scale[:, o:o + 1],
                             column(i["L1_ffn_scale_weight"][o * P:(o + 1) * P])).then_inc(loaded, 16)

        @block.vector
        def _(ve):
            ve.wait_ge(loaded, 128)
            for o in range(2):
                ve.tensor_scalar(wfs[:, o, :], wf[:, o, :], scale[:, o:o + 1], None, ALU.mult).then_inc(scaled, 1)

        odd = lambda w, c: w.rearrange("p (f c) -> p f c", c=C)[:, :, c]
        def turns():
            for c in range(C):
                yield bank[:, 0, c * P:(c + 1) * P], odd(w1[:, :], c), P
                yield bank[:, 1, c * P:(c + 1) * P], odd(wqk[:, :], c), P
                yield bank[:, 2, c * KW:(c + 1) * KW], odd(wv[:, :], c), KW
                yield bank[0:KW, 3, c * P:(c + 1) * P], wout[:, c, :], P
            yield bank[:, 4, 0:KW], w2[:, :], KW
            for o in range(2):
                for c in range(C):
                    yield bank[:, 5 + c, o * P:(o + 1) * P], odd(wfs[:, o, :], c), P

        @block.tensor
        def _(pe):
            pe.wait_ge(loaded, 128)
            pe.wait_ge(scaled, 2)
            for dst, src, rows in turns():
                mm = pe.transpose(dst, src, k.ident[0:rows, 0:rows])
            mm.then_inc(turned, 1)

        @block.scalar
        def _(act):
            act.wait_ge(turned, 1)
            pair = lambda b, n: bank[:, b, 0:C * n].rearrange("p (c n) -> p c n", c=C)
            act.activation(k.w1t[:, :, :], pair(0, P), ACT.Copy).then_inc(ready, 1)
            for z in range(2):
                for c in range(C):
                    for d in range(HD1):
                        at = z * KW
                        act.activation(
                            k.wqkvt[:, c, at:at + KW].rearrange("p (e d g) -> p e d g", e=4, d=HD1)[:, :, d, :],
                            bank[:, 1, c * P + at:c * P + at + KW].rearrange(
                                "p (g e d) -> p e d g", g=G, e=4)[:, :, d, :], ACT.Copy).then_inc(ready, 1)
            act.activation(k.wqkvt[:, :, P:P + KW], pair(2, KW), ACT.Copy).then_inc(ready, 1)
            act.activation(k.woutt[:, :], bank[0:KW, 3, 0:D], ACT.Copy).then_inc(ready, 1)
            act.activation(k.w2t[:, :], bank[:, 4, 0:KW], ACT.Copy).then_inc(ready, 1)
            act.activation(k.wft[:, :, :], bank[:, 5:7, 0:D], ACT.Copy).then_inc(ready, 1)
            act.wait_ge(ready, 13)


def keep_normalised(k):
    nc = k.nc
    normed, added = k.sem("y_normed"), k.sem("y_added")
    with nc.Block() as block:
        @block.vector
        def _(ve):
            xf, yf = (a[:, :, :].rearrange("p t d -> p (t d)") for a in (k.x, k.y))
            with ve.Fori(0, TILES) as t:
                at = bass.ds(t * D, D)
                ve.tensor_scalar(yf[:, at], xf[:, at], k.mean[:, bass.ds(t, 1)], k.rstd[:, bass.ds(t, 1)],
                                 ALU.subtract, ALU.mult).then_inc(normed, 1)
            with ve.Fori(0, TILES // 2) as t:
                at = bass.ds(t * 2 * D, 2 * D)
                ve.wait_ge(normed, TILES)
                ve.tensor_tensor(xf[:, at], xf[:, at], yf[:, at], ALU.add).then_inc(added, 1)
            ve.wait_ge(added, TILES // 2)


def second_projections(k):
    nc, i = k.nc, k.i
    loaded, filled, wiped = k.sem("p_loaded"), k.sem("p_filled"), k.sem("p_wiped")
    normed, turned, xt_ready = k.sem("p_normed"), k.sem("p_turned"), k.sem("p_xt_ready")
    h_done, h_ready, qk_done, qk_ready, v_done, v_ready = (k.sem("p_" + n) for n in (
        "h_done", "h_ready", "qk_done", "qk_ready", "v_done", "v_ready"))
    parted, stored = k.sem("p_parted"), k.sem("p_stored")
    with ExitStack() as local:
        def sb(name, shape, dt=F32):
            return local.enter_context(nc.sbuf_tensor("p" + name, shape, dt))
        gamma, beta, b1, bqk = sb("gamma", [P, C]), sb("beta", [P, C]), sb("b1", [P, 1]), sb("bqk", [KW, 2])
        bv = sb("bv", [P, KW])
        rows, xt = sb("rows", [P, TB, D]), sb("xt", [P, C, S])
        qk = sb("qk", [KW, 2, S])
        rest = sb("rest", [KW, 2, S])
        parts = sb("parts", [KW, 2, PRODUCTS, S], BF16)
        fill = sb("fill", [P, 2, S], BF16)
        bank = local.enter_context(nc.psum_tensor("pbank", [P, 8, 512], F32))
        block = local.enter_context(nc.Block())
        scratch = (k.q_dram, k.k_dram)

        @block.sync
        def _(sp):
            sp.dma_start(gamma[:, :], i["L1_attn_gamma"].rearrange("(p c) -> p c", c=C)).then_inc(loaded, 16)
            sp.dma_start(beta[:, :], i["L1_attn_beta"].rearrange("(p c) -> p c", c=C)).then_inc(loaded, 16)
            sp.dma_start(b1[:, :], column(i["L1_attn_b1"])).then_inc(loaded, 16)
            for z in range(2):
                byhead = i["L1_attn_bqkv"][z * KW:(z + 1) * KW].rearrange("(g c d a) -> c d g a", g=G, c=4, a=1)
                for c in range(4):
                    for d in range(HD1):
                        at = (c * HD1 + d) * G
                        sp.dma_start(bqk[at:at + G, z:z + 1], byhead[c, d], allow_slow_non_contiguous=True).then_inc(loaded, 16)
            sp.dma_start(bv[:, :], everyone(i["L1_attn_bqkv"][2 * KW:3 * KW])).then_inc(loaded, 16)
            sp.wait_ge(filled, 2)
            for z in range(2):
                for b in range(B):
                    sp.dma_start(scratch[z][b], fill[:, z, :].unsqueeze(1).broadcast_to([P, G, S])).then_inc(wiped, 16)
            sp.wait_ge(wiped, 16 * 2 * B)
            with sp.Fori(0, B) as b:
                for z in range(2):
                    sp.wait_ge(parted, b * 8 + 4 * z + 4)
                    pause(sp, k)
                    for c in range(4):
                        at = 32 * c + ROW0
                        rows_of = scratch[z][bass.ds(b, 1), at:at + HD1 * PRODUCTS, :, :].rearrange(
                            "b (m d) g s -> (b d g) m s", d=HD1)
                        sp.dma_start(rows_of, parts[16 * c:16 * c + 16, z, :, :]).then_inc(stored, 16)
                sp.wait_ge(stored, b * (16 * 2 * 4) + 16 * 2 * 4 + 16)
                pause(sp, k)

        @block.gpsimd
        def _(pool):
            pool.memset(fill[:, 0, :], 0.0).then_inc(filled, 1)
            pool.memset(fill[:, 1, :], 1.0).then_inc(filled, 1)

        @block.vector
        def _(ve):
            ve.wait_ge(loaded, 16 * 20)
            ve.sem_inc(stored, 16)
            with ve.Fori(0, B) as b:
                for j in range(TB):
                    normalise_tile(ve, k, k.y, rows, b, j).then_inc(normed, 1)
                ve.wait_ge(h_done, b + 1)
                ve.tensor_scalar(k.hneg[:, bass.ds(b * S, S)], bank[:, 2, :], -1.0, None, ALU.mult).then_inc(h_ready, 1)
                ve.tensor_scalar(k.hplus[:, bass.ds(b * S, S)], bank[:, 2, :], b1[:, 0:1], None, ALU.add).then_inc(h_ready, 1)
                ve.wait_ge(v_done, b + 1)
                ve.tensor_tensor(k.v[:, bass.ds(b * TB, TB), :], bank[:, 3, 0:TB * KW].rearrange("p (t n) -> p t n", t=TB),
                                 bv[:, :].unsqueeze(1).broadcast_to([P, TB, KW]), ALU.add).then_inc(v_ready, 1)
                n = Tally(b, 8)
                ve.wait_ge(stored, b * (16 * 2 * 4) + 16)
                for z in range(2):
                    ve.wait_ge(qk_ready, b * 2 + z + 1)
                    slots = [parts[:, z, at, :] for at in SLOTS[z]]
                    spread = lambda a, slot: a.unsqueeze(1).broadcast_to(list(slot.shape))
                    ve.tensor_copy(slots[0], spread(qk[:, z, :], slots[0])).then_inc(parted, n.up())
                    ve.wait_ge(parted, n.now())
                    ve.tensor_tensor(rest[:, z, :], qk[:, z, :], slots[0][:, 0, :], ALU.subtract).then_inc(parted, n.up())
                    ve.wait_ge(parted, n.now())
                    ve.tensor_copy(slots[1], spread(rest[:, z, :], slots[1])).then_inc(parted, n.up())
                    ve.wait_ge(parted, n.now())
                    ve.tensor_tensor(slots[2][:, 0, :], rest[:, z, :], slots[1][:, 0, :],
                                     ALU.subtract).then_inc(parted, n.up())
                assert n.n == 8

        @block.scalar
        def _(act):
            act.wait_ge(loaded, 16 * 20)
            with act.Fori(0, B) as b:
                for c in range(C):
                    act.wait_ge(turned, b * C + c + 1)
                    act.activation(xt[:, c, :], bank[:, c, :], ACT.Identity, bias=beta[:, c:c + 1],
                                   scale=gamma[:, c:c + 1]).then_inc(xt_ready, 1)
                for z in range(2):
                    act.wait_ge(qk_done, b * 2 + z + 1)
                    act.activation(qk[:, z, :], bank[0:KW, 4 + z, :], ACT.Identity,
                                   bias=bqk[:, z:z + 1]).then_inc(qk_ready, 1)

        @block.tensor
        def _(pe):
            with pe.Fori(0, B) as b:
                pe.wait_ge(normed, b * TB + TB)
                for c in range(C):
                    for j in range(TB):
                        mm = transpose_features(pe, k, bank[:, c, :], rows, j, c)
                    mm.then_inc(turned, 1)
                pe.wait_ge(xt_ready, b * C + C)
                for c in range(C):
                    mm = pe.matmul(bank[:, 2, :], k.w1t[:, c, :], xt[:, c, :], start=c == 0, stop=c == C - 1)
                mm.then_inc(h_done, 1)
                for z in range(2):
                    for c in range(C):
                        mm = pe.matmul(bank[0:KW, 4 + z, :], k.wqkvt[:, c, z * KW:(z + 1) * KW], xt[:, c, :],
                                       start=c == 0, stop=c == C - 1)
                    mm.then_inc(qk_done, 1)
                for j in range(TB):
                    for c in range(C):
                        mm = pe.matmul(bank[:, 3, j * KW:(j + 1) * KW], xt[:, c, j * P:(j + 1) * P],
                                       k.wqkvt[:, c, 2 * KW:3 * KW], start=c == 0, stop=c == C - 1)
                mm.then_inc(v_done, 1)
                pe.wait_ge(h_ready, b * 2 + 2)
                pe.wait_ge(v_ready, b + 1)
                pe.wait_ge(qk_ready, b * 2 + 2)


STEP_I = 8
STEPS = P // STEP_I


def pairwise(k):
    nc, i = k.nc, k.i
    ROUNDS = -(-KEEP // 8)
    assert ROUNDS == STEPS // 2 - 1
    R = 4
    PER = 3 * ROUNDS + 2
    AHEAD1 = 2 * R
    AHEAD2 = 2
    AHEAD3 = R
    loaded, set_up, made = k.sem("s_loaded"), k.sem("s_set_up"), k.sem("s_made")
    shifted, windowed, units, products, hidden, summed, sim_out, search = (k.sem("s_" + n) for n in (
        "shifted", "windowed", "units", "products", "hidden", "summed", "sim_out", "search"))
    with ExitStack() as local:
        def sb(name, shape, dt=F32):
            return local.enter_context(nc.sbuf_tensor("s" + name, shape, dt))
        w3, b2, b3 = sb("w3", [P, 1]), sb("b2", [P, 1]), sb("b3", [P, 1])
        bands = sb("bands", [P, STEPS * 34])
        top = sb("top", [P, 2])
        window = sb("window", [P, R, 32])
        shift = sb("shift", [P, R, 4, 2])
        unit1 = sb("unit1", [P, R, STEP_I, S])
        unit2 = sb("unit2", [P, 2, 4, S])
        offdiag = sb("offdiag", [P, TB, S])
        sim, work = sb("sim", [P, S]), sb("work", [P, S])
        best, cut = sb("best", [P, 8]), sb("cut", [P, 8])
        cap = sb("cap", [P, ROUNDS, 8])
        pre = local.enter_context(nc.psum_tensor("spre", [P, 2, 2, 512], F32))
        simp = local.enter_context(nc.psum_tensor("ssims", [P, 512], F32))
        block = local.enter_context(nc.Block())
        plus = k.hplus[:, :].rearrange("p (n c x) -> p n c x", c=4, x=32)
        maskf = k.mask[:, :, :].rearrange("p t s -> p (t s)")
        capf = cap[:, :, :].rearrange("p r e -> p (r e)")
        offf = offdiag[:, :, :].rearrange("p t s -> p (t s)")

        @block.sync
        def _(sp):
            for z in range(2):
                sp.dma_start(w3[z * KW:(z + 1) * KW, :], i["L1_attn_W3"].rearrange("o (g a) -> (o g) a", a=1)).then_inc(loaded, 16)
                sp.dma_start(b2[z * KW:(z + 1) * KW, :], column(i["L1_attn_b2"])).then_inc(loaded, 16)
            sp.dma_start(b3[:, :], everyone(i["L1_attn_b3"])).then_inc(loaded, 16)

        @block.gpsimd
        def _(pool):
            pool.memset(bands[:, :], 0.0).then_inc(made, 1)
            pool.memset(top[:, :], 1.0).then_inc(made, 1)
            pool.memset(offdiag[:, :, :], 1.0).then_inc(made, 1)
            pool.memset(cap[:, :, :], -GONE).then_inc(made, 1)
            pool.memset(sim[:, :], 0.0).then_inc(set_up, 1)
            pool.wait_ge(made, 4)
            pool.memset(cap[:, ROUNDS - 1, KEEP - 8 * (ROUNDS - 1):8], GONE).then_inc(made, 1)
            for q, n, base in ((0, 1, (TB - 1) * P), (1, TB - 1, 0)):
                part = offdiag[:, q:q + n, :]
                pool.affine_select(out=part, in_=part, compare_op=ALU.not_equal, fill=0.0,
                                   base=base, pattern=[[P, n], [-1, S]], channel_multiplier=1).then_inc(made, 1)
            pool.affine_select(out=top[:, 0:1], in_=top[:, 0:1], compare_op=ALU.is_ge, fill=0.0, base=KW - 1,
                               pattern=[[0, 1]], channel_multiplier=-1).then_inc(made, 1)
            pool.affine_select(out=top[:, 1:2], in_=top[:, 1:2], compare_op=ALU.is_ge, fill=0.0, base=-KW,
                               pattern=[[0, 1]], channel_multiplier=1).then_inc(made, 1)
            pool.wait_ge(made, 9)
            pool.wait_ge(loaded, 80)
            pool.tensor_scalar(bands[:, :].rearrange("p (r x) -> p r x", x=34)[:, :, 0:2],
                               top[:, :].unsqueeze(1).broadcast_to([P, STEPS, 2]), w3[:, 0:1], None,
                               ALU.mult).then_inc(set_up, 1)
            pool.wait_ge(set_up, 2)
            with pool.Fori(0, TILES) as n:
                with pool.Fori(0, STEPS // R) as m:
                    for u in range(R):
                        t = n * STEPS + m * R + u
                        pool.wait_ge(units, t * STEP_I + STEP_I)
                        pause(pool, k)
                        pool.tensor_copy(shift[:, u, :, :].unsqueeze(1),
                                         plus[:, bass.ds(n, 1), :, bass.ds(m * (2 * R) + 2 * u, 2)]).then_inc(shifted, 1)
                        pool.wait_ge(summed, t + 1)
                        pause(pool, k)
                        pool.tensor_copy(window[:, u, :],
                                         bands[:, bass.ds(m * (32 * R) + 32 * u, 32)]).then_inc(windowed, 1)

        def first_layer(ve, b, t, u, extra=None):
            ve.wait_ge(shifted, t + 1)
            ve.wait_ge(products, t * 2 + 2)
            pause(ve, k)
            for j in range(STEP_I):
                ve.tensor_scalar(unit1[:, u, j, :], k.hneg[:, bass.ds(b * S, S)],
                                 shift[:, u, j // 2, j % 2:j % 2 + 1], 0.0, ALU.add, ALU.max).then_inc(units, 1)
                if extra and j in extra:
                    extra[j]()

        def search_round(ve, r, done):
            def top8():
                ve.wait_ge(search, done)
                pause(ve, k)
                ve.max(best[:, :], work[:, :]).then_inc(search, 1)

            def capped():
                ve.wait_ge(search, done + 1)
                ve.tensor_tensor(cut[:, :], best[:, :], capf[:, bass.ds(r * 8, 8)], ALU.min).then_inc(search, 1)

            def taken():
                ve.wait_ge(search, done + 2)
                pause(ve, k)
                ve.match_replace(work[:, :], cut[:, :], work[:, :], GONE).then_inc(search, 1)
            return top8, capped, taken

        def begin_search(ve, n, q):
            ve.wait_ge(sim_out, n + 1)
            ve.wait_ge(search, n * PER + 1)
            pause(ve, k)
            ve.tensor_tensor(work[:, :], sim[:, :], offf[:, bass.ds(q * S, S)], ALU.mult).then_inc(search, 1)

        def end_search(ve, n):
            ve.wait_ge(search, n * PER + PER)
            pause(ve, k)
            ve.tensor_scalar(maskf[:, bass.ds(n * S, S)], work[:, :], GONE, -OFF, ALU.not_equal,
                             ALU.mult).then_inc(search, 1)

        @block.vector
        def _(ve):
            ve.sem_inc(units, R * STEP_I)
            ve.sem_inc(search, 1)
            ve.wait_ge(set_up, 2)
            with ve.Fori(0, B) as b:
                with ve.Fori(0, TB) as q:
                    n = b * TB + q
                    t0, s0 = n * STEPS, n * PER + 2
                    first_layer(ve, b, t0, 0)
                    first_layer(ve, b, t0 + 1, 1)
                    begin_search(ve, n, q)
                    a, c, z = search_round(ve, n * 0, s0)
                    first_layer(ve, b, t0 + 2, 2, {1: a, 5: c})
                    first_layer(ve, b, t0 + 3, 3, {1: z})
                    with ve.Fori(0, STEPS // R - 1) as m:
                        for v in range(2):
                            a, c, z = search_round(ve, m * 2 + 1 + v, s0 + m * 6 + 3 + 3 * v)
                            first_layer(ve, b, t0 + m * R + (R + 2 * v), 2 * v, {1: a, 5: c})
                            first_layer(ve, b, t0 + m * R + (R + 2 * v + 1), 2 * v + 1, {1: z})
                    end_search(ve, n)
            begin_search(ve, TILES, 0)
            for r in range(ROUNDS):
                for part in search_round(ve, r, TILES * PER + 2 + 3 * r):
                    part()
            end_search(ve, TILES)
            ve.wait_ge(search, (TILES + 1) * PER + 1)

        @block.scalar
        def _(act):
            act.sem_inc(hidden, AHEAD2)
            act.sem_inc(sim_out, 1)
            act.wait_ge(loaded, 80)
            with act.Fori(0, TILES) as n:
                with act.Fori(0, STEPS // 2) as m:
                    for v in range(2):
                        t = n * STEPS + m * 2 + v
                        for h in range(2):
                            act.wait_ge(products, t * 2 + h + 1 + AHEAD1)
                            act.wait_ge(summed, t + (AHEAD3 - 1))
                            act.activation(unit2[:, v, 2 * h:2 * h + 2, :], pre[:, h, :, :], ACT.Relu,
                                           bias=b2[:, 0:1]).then_inc(hidden, 1)
                act.wait_ge(summed, n * STEPS + STEPS + AHEAD3)
                act.wait_ge(search, n * PER + 2)
                act.activation(sim[:, :], simp[:, :], ACT.Identity, bias=b3[:, 0:1]).then_inc(sim_out, 1)

        def second_layer(pe, t, u):
            for h in range(2):
                pe.wait_ge(units, t * STEP_I + (R * STEP_I + 4 * h + 4))
                pe.wait_ge(hidden, t * 2 + h + 1)
                for c in range(2 * h, 2 * h + 2):
                    for s in range(2):
                        mm = pe.matmul(pre[s * KW:(s + 1) * KW, h, c % 2, :], k.w2t[:, :], unit1[:, u, 2 * c + s, :],
                                       start=True, stop=True)
                mm.then_inc(products, 1)

        def third_layer(pe, n, t, u, first=False):
            pe.wait_ge(windowed, t + 1)
            pe.wait_ge(hidden, t * 2 + 2 + AHEAD2)
            if first:
                pe.wait_ge(sim_out, n + 1)
            for c in range(4):
                mm = pe.matmul(simp[32 * c:32 * c + 32, :], window[:, u, :], unit2[:, u % 2, c, :], start=first,
                               stop=False, skip_group_check=True)
            mm.then_inc(summed, 1)

        @block.tensor
        def _(pe):
            pe.sem_inc(products, AHEAD1)
            pe.sem_inc(summed, AHEAD3)
            pe.wait_ge(set_up, 2)
            with pe.Fori(0, TILES) as n:
                t0 = n * STEPS
                for u in range(R):
                    second_layer(pe, t0 + u, u)
                    if u:
                        third_layer(pe, n, t0 + u - 1, u - 1, first=u == 1)
                with pe.Fori(0, STEPS // R - 1) as m:
                    for u in range(R):
                        t = t0 + m * R + (R + u)
                        second_layer(pe, t, u)
                        third_layer(pe, n, t - 1, (u - 1) % R)
                third_layer(pe, n, t0 + STEPS - 1, R - 1)


def second_attention(k):
    nc, i = k.nc, k.i
    U = 4 * TB
    loaded, set_up = k.sem("a1_loaded"), k.sem("a1_set_up")
    q_in, k_in = ([k.sem(f"a1_{n}{r}") for r in range(4)] for n in ("q_in", "k_in"))
    v_in = k.sem("a1_v_in")
    mask_in, mask_turned, mask_ready = (k.sem("a1_" + n) for n in ("mask_in", "mask_turned", "mask_ready"))
    scored, peak, split, peaks_turned, q_ready = (k.sem("a1_" + n) for n in (
        "scored", "peak", "split", "peaks_turned", "q_ready"))
    masked, exped, mixed, mixed_ready, mixed_turned, normal = (k.sem("a1_" + n) for n in (
        "masked", "exped", "mixed", "mixed_ready", "mixed_turned", "normal"))
    ao_turned, ao_ready, out_done, out_step = (k.sem("a1_" + n) for n in ("ao_turned", "ao_ready", "out_done", "out_step"))
    SPLIT = 5
    with ExitStack() as local:
        def sb(name, shape, dt=F32):
            return local.enter_context(nc.sbuf_tensor("b" + name, shape, dt))
        R = 4
        qs, ks = sb("qs", [P, R, S], BF16), sb("ks", [P, R, S], BF16)
        qm = sb("qm", [P, 2, S], BF16)
        vg = sb("vg", [P, 2, TB, 4, 32])
        mask_t = sb("mask_t", [P, TB, S], BF16)
        junk = sb("junk", [P, 2, S], BF16)
        peaks = sb("peaks", [P, TB, 4])
        rest = sb("rest", [P, TB, 4])
        neg = sb("neg", [P, TB, 4])
        peak_parts = sb("peak_parts", [P, TB, 4, 32], BF16)
        pt = sb("pt", [P, 2, 4, TB, S])
        mixed_s = sb("mixed_s", [P, S])
        mask_s = sb("mask_s", [P, TB, S], BF16)
        inv = sb("inv", [P, TB, 4])
        ao = sb("ao", [P, TB, KW])
        ao_t = sb("ao_t", [KW, S])
        bout = sb("bout", [P, D])
        tmp = sb("tmp", [P, 2, S])
        s1 = local.enter_context(nc.psum_tensor("bs1", [P, 2, 512], F32))
        s2 = local.enter_context(nc.psum_tensor("bs2", [P, 2, 2, 512], F32))
        om = local.enter_context(nc.psum_tensor("bom", [P, 512], F32))
        misc = local.enter_context(nc.psum_tensor("bmisc", [P, 512], F32))
        miscb = misc[:, :].bitcast(BF16)
        block = local.enter_context(nc.Block())
        xf = k.x[:, :, :].rearrange("p t d -> p (t d)")
        maskf = k.mask[:, :, :].rearrange("p t s -> p (t s)")
        parts_flat = peak_parts[:, :, :, :].rearrange("p q c r -> p q (c r)")

        @block.sync
        def _(sp):
            sp.dma_start(bout[:, :], everyone(i["L1_attn_bout"])).then_inc(loaded, 16)
            with sp.Fori(0, B) as b:
                qd, kd = (a.rearrange("b p g s -> (b p) (g s)")[bass.ds(b * P, P), :] for a in (k.q_dram, k.k_dram))
                for g in range(G):
                    sp.wait_ge(masked, b * (8 * G) + 8 * g + 8)
                    pause(sp, k)
                    u = g % R
                    sp.dma_start(qs[:, u, :], qd[:, g * S:(g + 1) * S]).then_inc(q_in[u], 16)
                    sp.dma_start(ks[:, u, :], kd[:, g * S:(g + 1) * S]).then_inc(k_in[u], 16)

        @block.gpsimd
        def _(pool):
            pool.memset(peak_parts[:, :, :, :], 0.0).then_inc(set_up, 1)
            pool.memset(vg[:, :, :, :, :], 0.0).then_inc(set_up, 1)
            pool.wait_ge(set_up, 2)
            pool.memset(vg[:, :, :, :, 2:3], 1.0).then_inc(set_up, 1)
            vt = k.v[:, :, :].rearrange("p t (g c d) -> p t g c d", c=4, d=2)
            with pool.Fori(0, B) as b:
                for g in range(G):
                    pool.wait_ge(mixed, b * G + g + 1)
                    pause(pool, k)
                    pool.tensor_copy(vg[:, g % 2, :, :, 0:2],
                                     vt[:, bass.ds(b * TB, TB), g, :, :]).then_inc(v_in, 1)

        def scores1(pe, b, it, g, n):
            c, q = divmod(n, TB)
            if n == 0:
                uses = b * (16 * G // R) + (g // R * 16 + 16)
                pe.wait_ge(q_in[g % R], uses)
                pe.wait_ge(k_in[g % R], uses)
            pe.wait_ge(peak, it * U + n + 1)
            pe.matmul(s1[:, n % 2, :], qs[32 * c:32 * c + 32, g % R, q * P:(q + 1) * P],
                      ks[32 * c:32 * c + 32, g % R, :], start=True, stop=True).then_inc(scored, 1)

        def turn_peaks(pe, it):
            pe.wait_ge(split, it * SPLIT + SPLIT + 1)
            pause(pe, k)
            for q in range(TB):
                mm = pe.transpose(miscb[:, q * P:(q + 1) * P], parts_flat[:, q, :], k.identb[:, :])
            mm.then_inc(peaks_turned, 1)

        def scores2(pe, it, g, n):
            c, h = divmod(n, 2)
            if n == 0:
                pe.wait_ge(q_ready, it + 1)
            pe.wait_ge(exped, it * 8 + n + 1)
            for z in range(2):
                j = 2 * h + z
                pe.matmul(s2[:, n % 2, z, :], k.identb[:, :], mask_t[:, j, :], start=True, stop=False)
                mm = pe.matmul(s2[:, n % 2, z, :], ks[32 * c:32 * c + 32, g % R, j * P:(j + 1) * P],
                               qm[32 * c:32 * c + 32, g % 2, :], start=False, stop=True)
            mm.then_inc(masked, 1)

        def mix(pe, it, g):
            pe.wait_ge(exped, it * 8 + 8 + 2)
            pe.wait_ge(v_in, it + 1)
            pe.wait_ge(mixed_ready, it + 1)
            for j in range(TB):
                for c in range(4):
                    mm = pe.matmul(om[32 * c:32 * c + 32, :], vg[:, g % 2, j, c, :], pt[:, g % 2, c, j, :],
                                   start=j == 0, stop=j == TB - 1, skip_group_check=True)
            mm.then_inc(mixed, 1)

        def turn_mixed(pe, it):
            pe.wait_ge(mixed_ready, it + 2)
            pe.wait_ge(q_ready, it + 1)
            for q in range(TB):
                mm = pe.transpose(misc[:, q * P:(q + 1) * P], mixed_s[:, q * P:(q + 1) * P], k.ident[:, :])
            mm.then_inc(mixed_turned, 1)

        @block.tensor
        def _(pe):
            pe.sem_inc(masked, 8 * R)
            pe.sem_inc(mixed, 2)
            pe.sem_inc(mixed_turned, 1)
            pe.sem_inc(peaks_turned, 1)
            pe.wait_ge(set_up, 3)
            with pe.Fori(0, B) as b:
                t0 = b * G
                pe.wait_ge(mask_in, b + 1)
                for j in range(TB):
                    pe.wait_ge(mask_ready, b * TB + j + 1)
                    pe.wait_ge(normal, b * (2 * G) + 1)
                    pause(pe, k)
                    for q in range(TB):
                        mm = pe.transpose(miscb[:, q * P:(q + 1) * P], mask_s[:, q, j * P:(j + 1) * P], k.identb[:, :])
                    mm.then_inc(mask_turned, 1)
                for n in range(U):
                    scores1(pe, b, t0, 0, n)
                pe.wait_ge(mask_ready, b * TB + TB + 1)
                turn_peaks(pe, t0)
                for g in range(G):
                    for n in range(8):
                        scores2(pe, t0 + g, g, n)
                        if g < G - 1:
                            scores1(pe, b, t0 + g + 1, g + 1, 2 * n)
                            scores1(pe, b, t0 + g + 1, g + 1, 2 * n + 1)
                    mix(pe, t0 + g, g)
                    turn_mixed(pe, t0 + g)
                    if g < G - 1:
                        pe.wait_ge(normal, (t0 + g) * 2 + 3)
                        turn_peaks(pe, t0 + g + 1)
                pe.wait_ge(normal, (t0 + G) * 2 + 1)
                pause(pe, k)
                for q in range(TB):
                    mm = pe.transpose(misc[0:KW, q * P:(q + 1) * P], ao[:, q, :], k.ident[:, :])
                mm.then_inc(ao_turned, 1)
                pe.wait_ge(ao_ready, b + 1)
                for q in range(TB):
                    mm = pe.matmul(s1[:, q // 2, (q % 2) * D:(q % 2) * D + D], ao_t[:, q * P:(q + 1) * P],
                                   k.woutt[:, :], start=True, stop=True)
                mm.then_inc(out_done, 1)
                pe.wait_ge(out_step, b * 4 + 2)

        @block.scalar
        def _(act):
            act.sem_inc(exped, 2)
            act.sem_inc(mixed_ready, 1)
            act.sem_inc(mask_ready, 1)
            with act.Fori(0, B) as b:
                t0 = b * G
                for j in range(TB):
                    act.wait_ge(mask_turned, b * TB + j + 1)
                    act.activation(mask_t[:, j, :], miscb[:, 0:S], ACT.Copy).then_inc(mask_ready, 1)
                for g in range(G):
                    for n in range(8):
                        c, h = divmod(n, 2)
                        act.wait_ge(masked, (t0 + g) * 8 + n + 1 + 8 * R)
                        if n == 0:
                            act.wait_ge(mixed, t0 + g + 1)
                        act.activation(pt[:, g % 2, c, 2 * h:2 * h + 2, :], s2[:, n % 2, :, :], ACT.Exp,
                                       scale=HD1 ** -0.5).then_inc(exped, 1)
                    act.wait_ge(mixed, t0 + g + 3)
                    act.wait_ge(mixed_turned, t0 + g + 1)
                    act.activation(mixed_s[:, :], om[:, :], ACT.Copy).then_inc(mixed_ready, 1)
                act.wait_ge(ao_turned, b + 1)
                act.activation(ao_t[:, :], misc[0:KW, :], ACT.Copy).then_inc(ao_ready, 1)

        def find_peaks(ve, b, it, g, n):
            c, q = divmod(n, TB)
            if n == 0:
                ve.wait_ge(split, it * SPLIT + 1)
            ve.wait_ge(scored, it * U + n + 1)
            pause(ve, k)
            ve.tensor_tensor_reduce(junk[:, n % 2, :], s1[:, n % 2, :], mask_s[:, q, :], 1.0, GONE, ALU.add, ALU.max,
                                    peaks[:, q, c:c + 1]).then_inc(peak, 1)

        def split_peaks(ve, it):
            n = Tally(it, SPLIT, 1)
            part = lambda z: peak_parts[:, :, :, z]
            ve.wait_ge(peak, it * U + U + 2)
            ve.wait_ge(peaks_turned, it + 1)
            ve.tensor_scalar(neg[:, :, :], peaks[:, :, :], -1.0, None, ALU.mult).then_inc(split, n.up())
            ve.wait_ge(split, n.now())
            ve.tensor_copy(part(0), neg[:, :, :]).then_inc(split, n.up())
            ve.wait_ge(split, n.now())
            ve.tensor_tensor(rest[:, :, :], neg[:, :, :], part(0), ALU.subtract).then_inc(split, n.up())
            ve.wait_ge(split, n.now())
            ve.tensor_copy(part(1), rest[:, :, :]).then_inc(split, n.up())
            ve.wait_ge(split, n.now())
            ve.tensor_tensor(part(2), rest[:, :, :], part(1), ALU.subtract).then_inc(split, n.up())
            assert n.n == SPLIT

        def add_peaks(ve, it, g):
            ve.wait_ge(peaks_turned, it + 2)
            ve.wait_ge(masked, it * 8 + 8 * R - 8)
            ve.tensor_tensor(qm[:, g % 2, :], miscb[:, 0:S], qs[:, g % R, :], ALU.add).then_inc(q_ready, 1)

        def normalise(ve, it, g):
            ve.wait_ge(mixed_turned, it + 2)
            o = misc[:, :].rearrange("p (q c r) -> p q c r", q=TB, c=4)
            ve.reciprocal(inv[:, :, :], o[:, :, :, 2]).then_inc(normal, 1)
            ve.wait_ge(normal, it * 2 + 2)
            ve.tensor_tensor(ao[:, :, 8 * g:8 * g + 8].rearrange("p q (c d) -> p q c d", c=4), o[:, :, :, 0:2],
                             inv[:, :, :].unsqueeze(3).broadcast_to([P, TB, 4, 2]), ALU.mult).then_inc(normal, 1)

        @block.vector
        def _(ve):
            ve.sem_inc(peak, 2)
            ve.sem_inc(split, 1)
            ve.sem_inc(normal, 1)
            ve.wait_ge(set_up, 3)
            ve.wait_ge(loaded, 16)
            with ve.Fori(0, B) as b:
                t0 = b * G
                ve.tensor_copy(mask_s[:, :, :].rearrange("p t s -> p (t s)"),
                               maskf[:, bass.ds(b * (TB * S) + S, TB * S)]).then_inc(mask_in, 1)
                ve.wait_ge(mask_in, b + 1)
                for n in range(U):
                    find_peaks(ve, b, t0, 0, n)
                split_peaks(ve, t0)
                add_peaks(ve, t0, 0)
                for g in range(G):
                    if g < G - 1:
                        for n in range(U):
                            find_peaks(ve, b, t0 + g + 1, g + 1, n)
                        split_peaks(ve, t0 + g + 1)
                    normalise(ve, t0 + g, g)
                    if g < G - 1:
                        add_peaks(ve, t0 + g + 1, g + 1)
                ve.wait_ge(out_done, b + 1)
                for h in range(2):
                    ve.tensor_tensor(tmp[:, h, :].rearrange("p (t n) -> p t n", t=2),
                                     s1[:, h, :].rearrange("p (t n) -> p t n", t=2),
                                     bout[:, :].unsqueeze(1).broadcast_to([P, 2, D]), ALU.add).then_inc(out_step, 1)
                ve.wait_ge(out_step, b * 4 + 2)
                for h in range(2):
                    at = bass.ds(b * (TB * D) + h * S, S)
                    ve.tensor_tensor(xf[:, at], xf[:, at], tmp[:, h, :], ALU.add).then_inc(out_step, 1)
                ve.wait_ge(out_step, b * 4 + 4)


def last_layer(k):
    nc, i = k.nc, k.i
    loaded, normed, turned, xt_ready, done, step = (k.sem("f_" + n) for n in (
        "loaded", "normed", "turned", "xt_ready", "done", "step"))
    stored = [k.sem(f"f_stored{z}") for z in range(2)]
    with ExitStack() as local:
        def sb(name, shape, dt=F32):
            return local.enter_context(nc.sbuf_tensor("f" + name, shape, dt))
        bias = sb("bias", [P, D])
        rows, xt = sb("rows", [P, 2, TB, D]), sb("xt", [P, 2, C, S])
        tmp = sb("tmp", [P, 2, TB, D])
        bank = local.enter_context(nc.psum_tensor("fbank", [P, 2, 4, 512], F32))
        xf = k.x[:, :, :].rearrange("p t d -> p (t d)")
        outs = k.out.rearrange("b (t p) d -> p b t d", p=P)
        block = local.enter_context(nc.Block())

        @block.sync
        def _(sp):
            sp.dma_start(bias[:, :], everyone(i["L1_ffn_bias"])).then_inc(loaded, 16)
            for b in range(B):
                sp.wait_ge(step, 4 * b + 4)
                sp.dma_start(outs[:, b, :, :], tmp[:, b % 2, :, :]).then_inc(stored[b % 2], 16)
            for z in range(2):
                sp.wait_ge(stored[z], 16 * B // 2)

        @block.vector
        def _(ve):
            ve.wait_ge(loaded, 16)
            for b in range(B + 1):
                if b < B:
                    if b >= 2:
                        ve.wait_ge(turned, 2 * b - 2)
                    for j in range(TB):
                        normalise_tile(ve, k, k.x, rows[:, b % 2, :, :], b, j).then_inc(normed, 1)
                if b:
                    a = b - 1
                    ve.wait_ge(done, a + 1)
                    if a >= 2:
                        ve.wait_ge(stored[a % 2], 16 * (a // 2))
                    for h in range(2):
                        part = tmp[:, a % 2, 2 * h:2 * h + 2, :]
                        ve.tensor_tensor(part, bank[:, a % 2, 2 + h, :].rearrange("p (t n) -> p t n", t=2),
                                         bias[:, :].unsqueeze(1).broadcast_to([P, 2, D]), ALU.add).then_inc(step, 1)
                    ve.wait_ge(step, 4 * a + 2)
                    for h in range(2):
                        part = tmp[:, a % 2, 2 * h:2 * h + 2, :]
                        ve.tensor_tensor(part, part, k.x[:, a * TB + 2 * h:a * TB + 2 * h + 2, :],
                                         ALU.add).then_inc(step, 1)

        @block.scalar
        def _(act):
            for b in range(B):
                for c in range(C):
                    act.wait_ge(turned, b * C + c + 1)
                    if b >= 2:
                        act.wait_ge(done, b - 1)
                    act.activation(xt[:, b % 2, c, :], bank[:, b % 2, c, :], ACT.Copy).then_inc(xt_ready, 1)

        @block.tensor
        def _(pe):
            for b in range(B):
                pe.wait_ge(normed, b * TB + TB)
                if b >= 2:
                    pe.wait_ge(step, 4 * b - 6)
                    pe.wait_ge(xt_ready, 2 * b - 2)
                for c in range(C):
                    for j in range(TB):
                        mm = transpose_features(pe, k, bank[:, b % 2, c, :], rows[:, b % 2, :, :], j, c)
                    mm.then_inc(turned, 1)
                pe.wait_ge(xt_ready, b * C + C)
                for j in range(TB):
                    for c in range(C):
                        mm = pe.matmul(bank[:, b % 2, 2 + j // 2, (j % 2) * D:(j % 2) * D + D],
                                       xt[:, b % 2, c, j * P:(j + 1) * P], k.wft[:, c, :], start=c == 0, stop=c == C - 1)
                mm.then_inc(done, 1)


def build(nc, ins, out):
    with ExitStack() as ctx:
        k = Kernel(nc, ctx, ins, out)

        def sb(name, shape, dt=F32, of=ctx):
            return of.enter_context(nc.sbuf_tensor(name, shape, dt))
        k.x = sb("x", [P, TILES, D])
        k.ident, k.identb = sb("ident", [P, P]), sb("identb", [P, P], BF16)
        k.mean, k.rstd = sb("mean", [P, TILES]), sb("rstd", [P, TILES])
        k.passed = k.sem("passed")
        load_and_constants(k)
        row_statistics(k, "ln0", k.x)
        first_attention(k)
        row_statistics(k, "ln1", k.x)
        with ExitStack() as local:
            k.xt = sb("xt", [P, C, N], of=local)
            k.shares_dram = nc.dram_tensor("shares", (EXPERTS + SHARED // FE, N), F32, kind="Internal").ap()
            router(k)
            experts(k)
        k.w1t, k.wqkvt, k.w2t = sb("w1t", [P, C, P]), sb("wqkvt", [P, C, 3 * KW]), sb("w2t", [P, KW])
        k.woutt, k.wft = sb("woutt", [KW, D]), sb("wft", [P, C, D])
        k.q_dram = nc.dram_tensor("q_parts", (B, P, G, S), BF16, kind="Internal").ap()
        k.k_dram = nc.dram_tensor("k_parts", (B, P, G, S), BF16, kind="Internal").ap()
        k.v = sb("v", [P, TILES, KW])
        k.mask = sb("mask", [P, TILES + 1, S], BF16)
        turn_weights_once(k)
        row_statistics(k, "ln2", k.x)
        with ExitStack() as local:
            k.hneg, k.hplus = sb("hneg", [P, N], of=local), sb("hplus", [P, N], of=local)
            with ExitStack() as inner:
                k.y = sb("y", [P, TILES, D], of=inner)
                keep_normalised(k)
                row_statistics(k, "ln3", k.y)
                second_projections(k)
            pairwise(k)
        second_attention(k)
        row_statistics(k, "ln4", k.x)
        last_layer(k)


INPUTS = ["L0_attn_x", "L0_attn_Wq", "L0_attn_bq", "L0_attn_Wk", "L0_attn_bk", "L0_attn_Wv", "L0_attn_bv",
          "L0_attn_Wo", "L0_attn_bo", "L0_ffn_router_w", "L0_ffn_router_bias", "L0_ffn_wg", "L0_ffn_wu",
          "L0_ffn_wd", "L0_ffn_swg", "L0_ffn_swu", "L0_ffn_swd", "L1_attn_gamma", "L1_attn_beta", "L1_attn_W1",
          "L1_attn_b1", "L1_attn_W2", "L1_attn_b2", "L1_attn_W3", "L1_attn_b3", "L1_attn_Wqkv", "L1_attn_bqkv",
          "L1_attn_Wout", "L1_attn_bout", "L1_ffn_weight", "L1_ffn_scale_weight", "L1_ffn_bias"]


def kernel(**inputs):
    import numpy as np
    import concourse.bacc as bacc
    from concourse.bass_utils import run_bass_kernel_spmd

    nc = bacc.Bacc("TRN2", target_bir_lowering=False, num_devices=1)
    arrays, aps = {}, {}
    for name in INPUTS:
        a = np.ascontiguousarray(inputs[name])
        arrays[name] = a
        aps[name] = nc.dram_tensor(name, a.shape, mybir.dt.from_np(a.dtype), kind="ExternalInput").ap()
    out = nc.dram_tensor("out", (B, S, D), F32, kind="ExternalOutput").ap()
    build(nc, aps, out)
    return run_bass_kernel_spmd(nc, [arrays], core_ids=[0]).results[0]["out"]
```

```python
from collections import namedtuple
from contextlib import ExitStack

import concourse.bass as bass
from concourse import mybir

F32 = mybir.dt.float32
BF16 = mybir.dt.bfloat16
ALU = mybir.AluOpType
ACT = mybir.ActivationFunctionType
AX = mybir.AxisListType

P = 128
B, S, D = 4, 512, 256
N = B * S
TB = S // P
TILES = N // P
C = D // P
EPS = 1e-5
HEADS0, HD0 = 4, 64
EXPERTS, FE, TOPK = 64, 64, 4
SHARED = 512
HT = (EXPERTS * FE + SHARED) // P
HEADS1, HD1, KW = 32, 2, 64
G = HEADS1 // 4
KEEP = int(S * 0.1)
GONE = -3.0e38
OFF = float(2.0 ** 126)


class Tally:

    def __init__(self, t=0, per=0, start=0):
        self.base, self.n = t * per + start, 0

    def up(self):
        self.n += 1
        return 1

    def now(self):
        return self.base + self.n


def pause(eng, k):
    eng.sem_inc(k.passed, 1)


def chunked(ap):
    return ap.rearrange("(p c) n -> p c n", c=C)


def column(ap):
    return ap.rearrange("(p a) -> p a", a=1)


def everyone(ap):
    return ap.partition_broadcast(P)


FirstWeights = namedtuple("FirstWeights", "wq wk wv wo bq bk bv bo")


class Kernel:
    def __init__(self, nc, ctx, ins, out):
        self.nc, self.ctx, self.i, self.out = nc, ctx, ins, out

    def sem(self, name):
        return self.ctx.enter_context(self.nc.semaphore(name))


def load_and_constants(k):
    nc = k.nc
    x_in, ident_step = k.sem("x_in"), k.sem("ident_step")
    i, W = k.i, k.w0
    with nc.Block() as block:
        @block.sync
        def _(sp):
            for t in range(4):
                sp.dma_start(k.x[:, 4 * t:4 * t + 4, :],
                             k.i["L0_attn_x"].rearrange("b (t p) d -> b p t d", p=P)[t]).then_inc(x_in, 16)
            for dst, name in ((W.wq, "Wq"), (W.wk, "Wk"), (W.wv, "Wv")):
                sp.dma_start(dst[:, :, :], chunked(i["L0_attn_" + name])).then_inc(k.w0_loaded, 16)
            sp.dma_start(W.wo[:, :, :], i["L0_attn_Wo"].rearrange("(c p) n -> p c n", p=P)).then_inc(k.w0_loaded, 16)
            for m in range(2):
                sp.dma_start(W.bq[:, m:m + 1], column(i["L0_attn_bq"][m * P:(m + 1) * P])).then_inc(k.w0_loaded, 16)
                sp.dma_start(W.bk[:, m:m + 1], column(i["L0_attn_bk"][m * P:(m + 1) * P])).then_inc(k.w0_loaded, 16)
            sp.dma_start(W.bv[:, :], everyone(i["L0_attn_bv"])).then_inc(k.w0_loaded, 16)
            sp.dma_start(W.bo[:, :], everyone(i["L0_attn_bo"])).then_inc(k.w0_loaded, 16)
            sp.wait_ge(x_in, 64)

        @block.gpsimd
        def _(pool):
            pool.memset(k.ident[:, :], 0.0).then_inc(ident_step, 1)
            pool.memset(k.identb[:, :], 0.0).then_inc(ident_step, 1)
            pool.wait_ge(ident_step, 2)
            for m in (k.ident, k.identb):
                pool.affine_select(out=m[:, :], in_=m[:, :], compare_op=ALU.not_equal, fill=1.0, base=0,
                                   pattern=[[-1, P]], channel_multiplier=1).then_inc(ident_step, 1)
            pool.wait_ge(ident_step, 4)


def row_statistics(k, tag, src):
    nc = k.nc
    tile_done, step, root = k.sem(tag + "_tile_done"), k.sem(tag + "_step"), k.sem(tag + "_root")
    with ExitStack() as local:
        def sb(name, shape, dt=F32):
            return local.enter_context(nc.sbuf_tensor(tag + name, shape, dt))
        stats = sb("stats", [P, TILES, 6])
        half, spread, var, std, r0, r1 = (sb(n, [P, TILES]) for n in ("half", "spread", "var", "std", "r0", "r1"))
        block = local.enter_context(nc.Block())
        flat = src[:, :, :].rearrange("p t d -> p (t d)")
        sflat = stats[:, :, :].rearrange("p t d -> p (t d)")

        @block.vector
        def _(ve):
            with ve.Fori(0, TILES) as t:
                ve.bn_stats(sflat[:, bass.ds(t * 6, 6)], flat[:, bass.ds(t * D, D)]).then_inc(tile_done, 1)
            ve.wait_ge(tile_done, TILES)
            n = Tally()
            ve.tensor_tensor(k.mean[:, :], stats[:, :, 1], stats[:, :, 4], ALU.add).then_inc(step, n.up())
            ve.tensor_tensor(half[:, :], stats[:, :, 1], stats[:, :, 4], ALU.subtract).then_inc(step, n.up())
            ve.tensor_tensor(spread[:, :], stats[:, :, 2], stats[:, :, 5], ALU.add).then_inc(step, n.up())
            ve.wait_ge(step, n.now())
            ve.tensor_scalar(k.mean[:, :], k.mean[:, :], 0.5, None, ALU.mult).then_inc(step, n.up())
            ve.scalar_tensor_tensor(out=half[:, :], in0=half[:, :], scalar=0.25, in1=half[:, :],
                                    op0=ALU.mult, op1=ALU.mult).then_inc(step, n.up())
            ve.tensor_scalar(spread[:, :], spread[:, :], 1.0 / D, EPS, ALU.mult, ALU.add).then_inc(step, n.up())
            ve.wait_ge(step, n.now())
            ve.tensor_tensor(var[:, :], half[:, :], spread[:, :], ALU.add).then_inc(step, n.up())
            ve.wait_ge(root, 1)
            ve.reciprocal(r0[:, :], std[:, :]).then_inc(step, n.up())
            ve.wait_ge(step, n.now())
            ve.tensor_tensor(r1[:, :], r0[:, :], r0[:, :], ALU.mult).then_inc(step, n.up())
            ve.wait_ge(step, n.now())
            ve.tensor_tensor(r1[:, :], r1[:, :], var[:, :], ALU.mult).then_inc(step, n.up())
            ve.wait_ge(step, n.now())
            ve.tensor_scalar(r1[:, :], r1[:, :], -0.5, 1.5, ALU.mult, ALU.add).then_inc(step, n.up())
            ve.wait_ge(step, n.now())
            ve.tensor_tensor(k.rstd[:, :], r0[:, :], r1[:, :], ALU.mult).then_inc(step, n.up())
            ve.wait_ge(step, n.now())

        @block.scalar
        def _(act):
            act.wait_ge(step, 7)
            act.activation(std[:, :], var[:, :], ACT.Sqrt).then_inc(root, 1)


def normalise_tile(ve, k, src, dst, b, i):
    t = b * TB + i
    flat = src[:, :, :].rearrange("p t d -> p (t d)")
    return ve.tensor_scalar(dst[:, i, :], flat[:, bass.ds(t * D, D)], k.mean[:, bass.ds(t, 1)],
                            k.rstd[:, bass.ds(t, 1)], ALU.subtract, ALU.mult)


def transpose_features(pe, k, psum, rows, i, c):
    picked = rows[:, i, :].rearrange("p (f c) -> p f c", c=C)[:, :, c]
    return pe.transpose(psum[:, i * P:(i + 1) * P], picked, k.ident[:, :])


def first_attention(k):
    nc = k.nc
    UNITS = HEADS0 * TB
    LAG = 3
    WSLOTS = LAG + 1
    END = B * UNITS
    LAST = END + 2 * TB + LAG
    normed, scored, peak, exped, inverse, weighted, turned, turned_kept = (k.sem("a0_" + n) for n in (
        "normed", "scored", "peak", "exped", "inverse", "weighted", "turned", "turned_kept"))
    mixed, mixed_kept, projected, out_step, halved = (k.sem("a0_" + n) for n in (
        "mixed", "mixed_kept", "projected", "out_step", "halved"))
    filled, taken = ([k.sem(f"a0_{n}{r}") for r in range(2)] for n in ("filled", "taken"))

    WINDOW = {0: ("x", 0), 1: ("x", 1), 2: ("qk", 0), 7: ("qk", 2), 8: ("out", 0), 9: ("out", 1),
              10: ("qk", 1), 11: ("v", 0), 13: ("v", 1), 15: ("qk", 3)}
    FIRST = [("x", 0), ("x", 1), ("qk", 0), ("qk", 2), ("v", 0), ("v", 1), ("qk", 1), ("qk", 3)]

    def piece(slot):
        b, u = divmod(slot, UNITS)
        kind, m = WINDOW.get(u, (None, 0))
        of = b - 1 if kind == "out" else b + 1
        return (kind, of, m) if kind and 0 <= of < B else None

    order = [(kind, 0, m) for kind, m in FIRST] + [p for s in range(END + UNITS) if (p := piece(s))]
    use_of = {p: (n % 2, n // 2) for n, p in enumerate(order)}
    kept_by_scalar = [p for p in order if p[0] in ("x", "qk")]
    kept_count = {p: n + 1 for n, p in enumerate(kept_by_scalar)}

    with ExitStack() as local:
        def sb(name, shape, dt=F32):
            return local.enter_context(nc.sbuf_tensor("a0" + name, shape, dt))
        half_bq = sb("half_bq", [P, 2])
        rows = sb("rows", [P, TB, D])
        xt = sb("xt", [P, C, S])
        qk = sb("qk", [P, 2, 4, S])
        v = sb("v", [P, 2, TB, D])
        negpeak, total, inv = (sb(n, [P, END]) for n in ("negpeak", "total", "inv"))
        w = sb("w", [P, WSLOTS, S])
        wt = sb("wt", [P, 4, TB, S])
        ft = sb("ft", [P, 2, S])
        tmp = sb("tmp", [P, 2, S])
        scores = local.enter_context(nc.psum_tensor("a0scores", [P, 3, 512], F32))
        turn = local.enter_context(nc.psum_tensor("a0turn", [P, 2, 512], F32))
        mix = local.enter_context(nc.psum_tensor("a0mix", [P, 512], F32))
        prod = local.enter_context(nc.psum_tensor("a0prod", [P, 2, 512], F32))
        block = local.enter_context(nc.Block())
        W = k.w0

        def mixes(slot):
            pair, j = divmod(slot - LAG - 2 * TB, 2 * TB)
            return (pair, j) if j < TB and 0 <= pair < 2 * B else None

        def normalise_rows(ve, b):
            for j in range(TB):
                if b:
                    ve.wait_ge(filled[use_of["x", b - 1, 1][0]], use_of["x", b - 1, 1][1] + 1)
                t = b * TB + j
                ve.tensor_scalar(rows[:, j, :], k.x[:, t, :], k.mean[:, t:t + 1], k.rstd[:, t:t + 1],
                                 ALU.subtract, ALU.mult).then_inc(normed, 1)

        def weigh(ve, u):
            ve.wait_ge(exped, u + 1)
            ve.reciprocal(inv[:, u:u + 1], total[:, u:u + 1]).then_inc(inverse, 1)
            ve.wait_ge(inverse, u + 1)
            ve.tensor_scalar(w[:, u % WSLOTS, :], w[:, u % WSLOTS, :], inv[:, u:u + 1], None,
                             ALU.mult).then_inc(weighted, 1)

        def take_on_vector(ve, p):
            kind, b, h = p
            if kind not in ("v", "out"):
                return
            bank, use = use_of[p]
            ve.wait_ge(filled[bank], use + 1)
            src = prod[:, bank, :].rearrange("p (t n) -> p t n", t=2)
            if kind == "v":
                if b >= 2:
                    ve.wait_ge(mixed, 2 * (b - 2) + 2)
                ve.tensor_tensor(v[:, b % 2, 2 * h:2 * h + 2, :], src,
                                 W.bv[:, :].unsqueeze(1).broadcast_to([P, 2, D]), ALU.add).then_inc(taken[bank], 1)
            else:
                x = k.x[:, b * TB + 2 * h:b * TB + 2 * h + 2, :]
                if b:
                    ve.wait_ge(out_step, 2 * (b - 1) + h + 1)
                ve.tensor_tensor(tmp[:, h, :].rearrange("p (t n) -> p t n", t=2), src,
                                 W.bo[:, :].unsqueeze(1).broadcast_to([P, 2, D]), ALU.add).then_inc(taken[bank], 1)
                ve.wait_ge(taken[bank], use + 1)
                ve.tensor_tensor(x, x, tmp[:, h, :].rearrange("p (t n) -> p t n", t=2),
                                 ALU.add).then_inc(out_step, 1)

        @block.vector
        def _(ve):
            ve.wait_ge(k.w0_loaded, k.W0_LOADED)
            ve.tensor_scalar(half_bq[:, :], W.bq[:, :], 0.5, None, ALU.mult).then_inc(halved, 1)
            normalise_rows(ve, 0)
            for kind, m in FIRST:
                take_on_vector(ve, (kind, 0, m))
            normalise_rows(ve, 1)
            for s in range(LAST):
                if s < END:
                    ve.wait_ge(scored, s + 1)
                    ve.tensor_reduce(negpeak[:, s:s + 1], scores[:, s % 3, :], AX.X, ALU.max,
                                     negate=True).then_inc(peak, 1)
                if 0 < s <= END:
                    weigh(ve, s - 1)
                if piece(s):
                    take_on_vector(ve, piece(s))
                b, u = divmod(s, UNITS)
                if u == 3 and b + 2 < B:
                    normalise_rows(ve, b + 2)
            ve.wait_ge(out_step, 2 * B)

        def take_on_scalar(act, p):
            kind, b, m = p
            if kind not in ("x", "qk"):
                return
            bank, use = use_of[p]
            act.wait_ge(filled[bank], use + 1)
            if kind == "x":
                if b:
                    last = max(("v", b - 1, 1), ("qk", b - 1, 3), key=order.index)
                    act.wait_ge(filled[use_of[last][0]], use_of[last][1] + 1)
                act.activation(xt[:, m, :], prod[:, bank, :], ACT.Copy).then_inc(taken[bank], 1)
            else:
                if b >= 2:
                    act.wait_ge(scored, (b - 1) * UNITS)
                if m < 2:
                    act.activation(qk[:, b % 2, m, :], prod[:, bank, :], ACT.Identity, bias=half_bq[:, m:m + 1],
                                   scale=0.5).then_inc(taken[bank], 1)
                else:
                    act.activation(qk[:, b % 2, m, :], prod[:, bank, :], ACT.Identity,
                                   bias=W.bk[:, m - 2:m - 1]).then_inc(taken[bank], 1)

        @block.scalar
        def _(act):
            act.wait_ge(halved, 1)
            act.wait_ge(k.w0_loaded, k.W0_LOADED)
            for kind, m in FIRST:
                take_on_scalar(act, (kind, 0, m))
            for s in range(LAST):
                if 0 <= s - LAG < END:
                    u = s - LAG
                    h, q = divmod(u, TB)
                    act.wait_ge(turned, u + 1)
                    if h >= 4:
                        act.wait_ge(mixed, h // 2 - 1)
                    act.activation(wt[:, h % 4, :, q * P:(q + 1) * P],
                                   turn[:, u % 2, :].rearrange("p (j s) -> p j s", j=TB), ACT.Copy).then_inc(turned_kept, 1)
                if s < END:
                    act.wait_ge(peak, s + 1)
                    if s >= WSLOTS:
                        act.wait_ge(turned, s - WSLOTS + 1)
                    act.activation(w[:, s % WSLOTS, :], scores[:, s % 3, :], ACT.Exp, bias=negpeak[:, s:s + 1],
                                   accum_out=total[:, s:s + 1]).then_inc(exped, 1)
                if piece(s):
                    take_on_scalar(act, piece(s))
                if mixes(s) and mixes(s)[1] == TB - 1:
                    pair = mixes(s)[0]
                    act.wait_ge(mixed, pair + 1)
                    if pair >= 2:
                        bank, use = use_of["out", pair // 2 - 1, 1]
                        act.wait_ge(filled[bank], use + 1)
                    act.activation(ft[:, pair % 2, :], mix[:, :], ACT.Copy).then_inc(mixed_kept, 1)

        def make(pe, p):
            kind, b, m = p
            bank, use = use_of[p]
            if use:
                pe.wait_ge(taken[bank], use)
            out = prod[:, bank, :]

            def kept(*what):
                other, its_use = use_of[what]
                pe.wait_ge(taken[other], its_use + 1)

            if kind == "x":
                pe.wait_ge(normed, b * TB + TB)
                for j in range(TB):
                    mm = transpose_features(pe, k, out, rows, j, m)
            elif kind == "qk":
                kept("x", b, 0)
                kept("x", b, 1)
                wts = W.wq if m < 2 else W.wk
                for c in range(C):
                    mm = pe.matmul(out, wts[:, c, (m % 2) * P:(m % 2) * P + P], xt[:, c, :], start=c == 0, stop=c == C - 1)
            elif kind == "v":
                kept("x", b, 0)
                kept("x", b, 1)
                for j in range(2):
                    for c in range(C):
                        mm = pe.matmul(out[:, j * D:(j + 1) * D], xt[:, c, (2 * m + j) * P:(2 * m + j + 1) * P],
                                       W.wv[:, c, :], start=c == 0, stop=c == C - 1)
            else:
                pe.wait_ge(mixed_kept, 2 * b + 2)
                for j in range(2):
                    for c in range(2):
                        mm = pe.matmul(out[:, j * D:(j + 1) * D], ft[:, c, (2 * m + j) * P:(2 * m + j + 1) * P],
                                       W.wo[:, c, :], start=c == 0, stop=c == 1)
            mm.then_inc(filled[bank], 1)

        @block.tensor
        def _(pe):
            pe.wait_ge(k.w0_loaded, k.W0_LOADED)
            for kind, m in FIRST:
                make(pe, (kind, 0, m))
            for s in range(LAST):
                if s < END:
                    b, u = divmod(s, UNITS)
                    h, q = divmod(u, TB)
                    if s >= 3:
                        pe.wait_ge(exped, s - 2)
                    if q == 0 and h % 2 == 0:
                        for m in (h // 2, 2 + h // 2):
                            bank, use = use_of["qk", b, m]
                            pe.wait_ge(taken[bank], use + 1)
                    r = HD0 * (h % 2)
                    pe.matmul(scores[:, s % 3, :], qk[r:r + HD0, b % 2, h // 2, q * P:(q + 1) * P],
                              qk[r:r + HD0, b % 2, 2 + h // 2, :], start=True, stop=True).then_inc(scored, 1)
                if 0 <= s - LAG < END:
                    u = s - LAG
                    pe.wait_ge(weighted, u + 1)
                    if u >= 2:
                        pe.wait_ge(turned_kept, u - 1)
                    for j in range(TB):
                        mm = pe.transpose(turn[:, u % 2, j * P:(j + 1) * P], w[:, u % WSLOTS, j * P:(j + 1) * P],
                                          k.ident[:, :])
                    mm.then_inc(turned, 1)
                if piece(s):
                    make(pe, piece(s))
                if mixes(s):
                    pair, j = mixes(s)
                    b, p2 = divmod(pair, 2)
                    if j == 0:
                        pe.wait_ge(turned_kept, (pair + 1) * 2 * TB)
                        bank, use = use_of["v", b, 1]
                        pe.wait_ge(taken[bank], use + 1)
                        bank, use = use_of["v", b, 0]
                        pe.wait_ge(taken[bank], use + 1)
                        if pair:
                            pe.wait_ge(mixed_kept, pair)
                    for e in range(2):
                        h = 2 * p2 + e
                        mm = pe.matmul(mix[e * HD0:(e + 1) * HD0, :], v[:, b % 2, j, h * HD0:(h + 1) * HD0],
                                       wt[:, (2 * pair + e) % 4, j, :], start=j == 0, stop=j == TB - 1,
                                       skip_group_check=True)
                    if j == TB - 1:
                        mm.then_inc(mixed, 1)


def router(k):
    nc, i = k.nc, k.i
    loaded, set_up = k.sem("r_loaded"), k.sem("r_set_up")
    normed, turned, xt_ready = k.sem("r_normed"), k.sem("r_turned"), k.sem("r_xt_ready")
    logit_done, logit_ready, logit_turned = k.sem("r_logit_done"), k.sem("r_logit_ready"), k.sem("r_logit_turned")
    step, exped, comb_turned, comb_ready, stored = (k.sem("r_" + n) for n in (
        "step", "exped", "comb_turned", "comb_ready", "stored"))
    PAD = EXPERTS + 8
    with ExitStack() as local:
        def sb(name, shape, dt=F32):
            return local.enter_context(nc.sbuf_tensor("r" + name, shape, dt))
        wr, bias = sb("wr", [P, C, EXPERTS]), sb("bias", [P, EXPERTS])
        rows = sb("rows", [P, TB, D])
        logit_t = sb("logit_t", [EXPERTS, S])
        logit = sb("logit", [P, TB, EXPERTS])
        ranked = sb("ranked", [P, TB, PAD])
        best, cap = sb("best", [P, TB, 8]), sb("cap", [P, 8])
        negpeak, total, inv = sb("negpeak", [P, TB]), sb("total", [P, TB]), sb("inv", [P, TB])
        picked, inv2 = sb("picked", [P, TB]), sb("inv2", [P, TB])
        share = sb("share", [P, TB, EXPERTS])
        comb_t = sb("comb_t", [EXPERTS, S])
        ones = sb("ones", [SHARED // FE, N])
        bank = local.enter_context(nc.psum_tensor("rbank", [P, 8, 512], F32))
        block = local.enter_context(nc.Block())
        xt_flat = k.xt[:, :, :].rearrange("p c n -> p (c n)")

        @block.sync
        def _(sp):
            sp.dma_start(wr[:, :, :], chunked(i["L0_ffn_router_w"])).then_inc(loaded, 16)
            sp.dma_start(bias[:, :], everyone(i["L0_ffn_router_bias"])).then_inc(loaded, 16)
            sp.wait_ge(set_up, 3)
            sp.dma_start(k.shares_dram[EXPERTS:, :], ones[:, :]).then_inc(stored, 16)
            with sp.Fori(0, B) as b:
                sp.wait_ge(comb_ready, b + 1)
                pause(sp, k)
                sp.dma_start(k.shares_dram[0:EXPERTS, bass.ds(b * S, S)], comb_t[:, :]).then_inc(stored, 16)
                sp.wait_ge(stored, b * 16 + 32)
                pause(sp, k)

        @block.gpsimd
        def _(pool):
            pool.memset(cap[:, 0:TOPK], -GONE).then_inc(set_up, 1)
            pool.memset(cap[:, TOPK:8], GONE).then_inc(set_up, 1)
            pool.memset(ones[:, :], 1.0).then_inc(set_up, 1)

        @block.vector
        def _(ve):
            ve.wait_ge(loaded, 32)
            ve.wait_ge(set_up, 3)
            with ve.Fori(0, B) as b:
                for j in range(TB):
                    normalise_tile(ve, k, k.x, rows, b, j).then_inc(normed, 1)
                n = Tally(b, 4 * TB + 9)
                ve.wait_ge(logit_turned, b + 1)
                turned_logits = bank[:, 3, 0:TB * EXPERTS].rearrange("p (t e) -> p t e", t=TB)
                ve.tensor_copy(logit[:, :, :], turned_logits).then_inc(step, n.up())
                ve.memset(ranked[:, :, EXPERTS:PAD], GONE).then_inc(step, n.up())
                ve.wait_ge(step, n.now())
                ve.tensor_reduce(negpeak[:, :], logit[:, :, :], AX.X, ALU.max, negate=True).then_inc(step, n.up())
                ve.tensor_tensor(ranked[:, :, 0:EXPERTS], logit[:, :, :],
                                 bias[:, :].unsqueeze(1).broadcast_to([P, TB, EXPERTS]), ALU.add).then_inc(step, n.up())
                ve.wait_ge(step, n.now())
                pause(ve, k)
                for j in range(TB):
                    ve.max(best[:, j, :], ranked[:, j, :]).then_inc(step, n.up())
                ve.wait_ge(step, n.now())
                ve.tensor_tensor(best[:, :, :], best[:, :, :], cap[:, :].unsqueeze(1).broadcast_to([P, TB, 8]),
                                 ALU.min).then_inc(step, n.up())
                ve.wait_ge(step, n.now())
                pause(ve, k)
                for j in range(TB):
                    ve.match_replace(ranked[:, j, :], best[:, j, :], ranked[:, j, :], GONE).then_inc(step, n.up())
                ve.wait_ge(exped, b * TB + TB)
                ve.reciprocal(inv[:, :], total[:, :]).then_inc(step, n.up())
                ve.wait_ge(step, n.now())
                for j in range(TB):
                    ve.tensor_scalar(share[:, j, :], share[:, j, :], inv[:, j:j + 1], None, ALU.mult).then_inc(step, n.up())
                ve.wait_ge(step, n.now())
                for j in range(TB):
                    ve.scalar_tensor_tensor(out=share[:, j, :], in0=ranked[:, j, 0:EXPERTS], scalar=GONE,
                                            in1=share[:, j, :], op0=ALU.is_equal, op1=ALU.mult).then_inc(step, n.up())
                ve.wait_ge(step, n.now())
                ve.tensor_reduce(picked[:, :], share[:, :, :], AX.X, ALU.add).then_inc(step, n.up())
                ve.wait_ge(step, n.now())
                ve.reciprocal(inv2[:, :], picked[:, :]).then_inc(step, n.up())
                ve.wait_ge(step, n.now())
                ve.tensor_tensor(share[:, :, :], share[:, :, :],
                                 inv2[:, :].unsqueeze(2).broadcast_to([P, TB, EXPERTS]), ALU.mult).then_inc(step, n.up())
                assert n.n == 4 * TB + 9, n.n

        @block.scalar
        def _(act):
            with act.Fori(0, B) as b:
                for c in range(C):
                    act.wait_ge(turned, b * C + c + 1)
                    act.activation(xt_flat[:, bass.ds(b * S + c * N, S)], bank[:, c, :], ACT.Copy).then_inc(xt_ready, 1)
                act.wait_ge(logit_done, b + 1)
                act.activation(logit_t[:, :], bank[0:EXPERTS, 2, :], ACT.Copy).then_inc(logit_ready, 1)
                act.wait_ge(step, b * (4 * TB + 9) + 3)
                for j in range(TB):
                    act.activation(share[:, j, :], logit[:, j, :], ACT.Exp, bias=negpeak[:, j:j + 1],
                                   accum_out=total[:, j:j + 1]).then_inc(exped, 1)
                act.wait_ge(comb_turned, b + 1)
                act.wait_ge(stored, b * 16 + 16)
                act.activation(comb_t[:, :], bank[0:EXPERTS, 4, :], ACT.Copy).then_inc(comb_ready, 1)

        @block.tensor
        def _(pe):
            pe.wait_ge(loaded, 32)
            with pe.Fori(0, B) as b:
                pe.wait_ge(normed, b * TB + TB)
                for c in range(C):
                    for j in range(TB):
                        mm = transpose_features(pe, k, bank[:, c, :], rows, j, c)
                    mm.then_inc(turned, 1)
                pe.wait_ge(xt_ready, b * C + C)
                pause(pe, k)
                for c in range(C):
                    mm = pe.matmul(bank[0:EXPERTS, 2, :], wr[:, c, :], xt_flat[:, bass.ds(b * S + c * N, S)],
                                   start=c == 0, stop=c == C - 1)
                mm.then_inc(logit_done, 1)
                pe.wait_ge(logit_ready, b + 1)
                pause(pe, k)
                for j in range(TB):
                    mm = pe.transpose(bank[:, 3, j * EXPERTS:(j + 1) * EXPERTS], logit_t[:, j * P:(j + 1) * P],
                                      k.ident[0:EXPERTS, 0:EXPERTS])
                mm.then_inc(logit_turned, 1)
                pe.wait_ge(step, b * (4 * TB + 9) + 4 * TB + 9)
                pause(pe, k)
                for j in range(TB):
                    mm = pe.transpose(bank[0:EXPERTS, 4, j * P:(j + 1) * P], share[:, j, :], k.ident[:, :])
                mm.then_inc(comb_turned, 1)
                pe.wait_ge(comb_ready, b + 1)


def experts(k):
    nc, i = k.nc, k.i
    H = N // 2
    R = 4
    gate_in, up_in, down_in, share_in = ([k.sem(f"e_{n}{r}") for r in range(R)] for n in (
        "gate_in", "up_in", "down_in", "share_in"))
    hidden_done, gated, scaled, hidden_ready, down_done = (k.sem("e_" + n) for n in (
        "hidden_done", "gated", "scaled", "hidden_ready", "down_done"))
    cleared, added = k.sem("e_cleared"), k.sem("e_added")
    with ExitStack() as local:
        def sb(name, shape, dt=F32):
            return local.enter_context(nc.sbuf_tensor("e" + name, shape, dt))
        wg, wu = sb("wg", [P, R, C, 2, FE]), sb("wu", [P, R, C, 2, FE])
        wd = sb("wd", [P, R, D])
        shares = sb("shares", [P, R, H])
        sg = sb("sg", [P, 2, S])
        sgs = sb("sgs", [P, 2, S])
        hid = sb("hid", [P, 2, S])
        gu = local.enter_context(nc.psum_tensor("egu", [P, 4, 512], F32))
        acc = local.enter_context(nc.psum_tensor("eacc", [P, 4, 512], F32))
        xflat = k.x[:, :, :].rearrange("p t d -> p (t d)")
        xt_flat = k.xt[:, :, :].rearrange("p c n -> p (c n)")
        block = local.enter_context(nc.Block())
        wgr = i["L0_ffn_wg"].rearrange("e (p c) f -> p e c f", c=C)
        wur = i["L0_ffn_wu"].rearrange("e (p c) f -> p e c f", c=C)
        wdr = i["L0_ffn_wd"].rearrange("e f d -> (e f) d")
        sgr = i["L0_ffn_swg"].rearrange("s (p c) (q f) -> p s q c f", c=C, f=FE)
        sur = i["L0_ffn_swu"].rearrange("s (p c) (q f) -> p s q c f", c=C, f=FE)
        sdr = i["L0_ffn_swd"].rearrange("s h d -> (s h) d")
        flat = lambda w, r, c: w[:, r, c, :, :].rearrange("p e f -> p (e f)")

        def fetch(sp, tile, r, use, half, shared=None):
            sp.wait_ge(down_done, use)
            pause(sp, k)
            if shared is None:
                for e in range(2):
                    one = bass.ds(tile * 2 + e, 1)
                    sp.dma_start(wg[:, r, :, e, :], wgr[:, one, :, :].rearrange("p e c f -> p (e c) f")).then_inc(gate_in[r], 16)
                    sp.dma_start(wu[:, r, :, e, :], wur[:, one, :, :].rearrange("p e c f -> p (e c) f")).then_inc(up_in[r], 16)
                sp.dma_start(wd[:, r, :], wdr[bass.ds(tile * P, P), :]).then_inc(down_in[r], 16)
            else:
                s, q = divmod(2 * shared, 4)
                for e in range(2):
                    sp.dma_start(wg[:, r, :, e, :], sgr[:, s, q + e, :, :]).then_inc(gate_in[r], 16)
                    sp.dma_start(wu[:, r, :, e, :], sur[:, s, q + e, :, :]).then_inc(up_in[r], 16)
                sp.dma_start(wd[:, r, :], sdr[shared * P:shared * P + P, :]).then_inc(down_in[r], 16)
            for e in range(2):
                row = tile * 2 + e
                sp.dma_start(shares[e * FE:(e + 1) * FE, r, :],
                             k.shares_dram[bass.ds(row, 1), bass.ds(half * H, H)]
                             .broadcast_to([FE, H])).then_inc(share_in[r], 16)

        @block.sync
        def _(sp):
            with sp.Fori(0, 2) as half:
                with sp.Fori(0, EXPERTS // 2 // R) as m:
                    for r in range(R):
                        fetch(sp, m * R + r, r, half * (2 * HT) + m * (2 * R) + 2 * r + 2, half)
                for r in range(R):
                    t = EXPERTS // 2 + r
                    fetch(sp, t, r, half * (2 * HT) + 2 * t + 2, half, shared=r)

        LAST = 2 * HT

        def down(pe, r, q, t0, use):
            if q == 0:
                pe.wait_ge(down_in[r], use * 16 + 16)
            pe.wait_ge(hidden_ready, t0 * 2 + q + 1)
            for j in range(TB):
                tok = q * TB + j
                mm = pe.matmul(acc[:, tok // 2, (tok % 2) * D:(tok % 2) * D + D], hid[:, q, j * P:(j + 1) * P],
                               wd[:, r, :], start=False, stop=False, skip_group_check=True)
            mm.then_inc(down_done, 1)

        @block.tensor
        def _(pe):
            pe.sem_inc(down_done, 2 * R)
            with pe.Fori(0, 2) as half:
                pe.wait_ge(cleared, half * 4 + 4)
                pause(pe, k)
                with pe.Fori(0, HT // R) as m:
                    for r in range(R):
                        use = half * (HT // R) + m
                        t0 = use * R + r
                        pe.wait_ge(gate_in[r], use * 32 + 32)
                        pe.wait_ge(up_in[r], use * 32 + 32)
                        for q in range(2):
                            pe.wait_ge(scaled, t0 * 2 + q + 1)
                            pause(pe, k)
                            for w, z in ((wg, 0), (wu, 1)):
                                for c in range(C):
                                    mm = pe.matmul(gu[:, 2 * q + z, :],
                                                   flat(w, r, c),
                                                   xt_flat[:, bass.ds(half * H + (q * S + c * N), S)],
                                                   start=c == 0, stop=c == C - 1)
                                mm.then_inc(hidden_done, 1)
                            if q:
                                down(pe, r, 0, t0, use)
                        down(pe, r, 1, t0, use)


        @block.scalar
        def _(act):
            with act.Fori(0, 2 * HT) as t:
                for q in range(2):
                    act.wait_ge(hidden_done, t * 4 + 2 * q + 1)
                    act.wait_ge(scaled, t * 2 + q + 1)
                    act.activation(sg[:, q, :], gu[:, 2 * q, :], ACT.Silu).then_inc(gated, 1)

        @block.vector
        def _(ve):
            ve.sem_inc(scaled, 2)
            with ve.Fori(0, 2) as half:
                for z in range(4):
                    ve.memset(acc[:, z, :], 0.0).then_inc(cleared, 1)
                with ve.Fori(0, HT // R) as m:
                    for r in range(R):
                        use = half * (HT // R) + m
                        t0 = use * R + r
                        ve.wait_ge(share_in[r], use * 32 + 32)
                        for q in range(2):
                            ve.wait_ge(gated, t0 * 2 + q + 1)
                            ve.wait_ge(hidden_done, t0 * 4 + 2 * q + 2)
                            ve.tensor_tensor(sgs[:, q, :], gu[:, 2 * q + 1, :], sg[:, q, :], ALU.mult).then_inc(scaled, 1)
                            ve.wait_ge(scaled, t0 * 2 + q + 3)
                            ve.wait_ge(down_done, t0 * 2 + (q + 2 * R - 1))
                            ve.tensor_tensor(hid[:, q, :], sgs[:, q, :], shares[:, r, q * S:(q + 1) * S],
                                             ALU.mult).then_inc(hidden_ready, 1)
                ve.wait_ge(down_done, half * LAST + LAST + 2 * R)
                for z in range(4):
                    at = half * (N // 2 // P * D) + z * 512
                    ve.tensor_tensor(xflat[:, bass.ds(at, 512)], xflat[:, bass.ds(at, 512)], acc[:, z, :],
                                     ALU.add).then_inc(added, 1)
                ve.wait_ge(added, half * 4 + 4)


ROW0 = 3
SLOTS = ((slice(0, 3), slice(3, 5), slice(5, 6)), (slice(1, 6, 2), slice(2, 5, 2), slice(0, 1)))
PRODUCTS = 6


def turn_weights_once(k):
    nc, i = k.nc, k.i
    loaded, scaled, turned, ready = (k.sem("w_" + n) for n in ("loaded", "scaled", "turned", "ready"))
    with ExitStack() as local:
        def sb(name, shape, dt=F32):
            return local.enter_context(nc.sbuf_tensor("w" + name, shape, dt))
        w1, w2 = sb("w1", [P, D]), sb("w2", [KW, P])
        wqk, wv = sb("wqk", [P, D]), sb("wv", [KW, D])
        wout, wf = sb("wout", [P, C, KW]), sb("wf", [P, C, D])
        wfs, scale = sb("wfs", [P, C, D]), sb("scale", [P, C])
        bank = local.enter_context(nc.psum_tensor("wbank", [P, 8, 512], F32))
        block = local.enter_context(nc.Block())
        wqkv = i["L1_attn_Wqkv"]

        @block.sync
        def _(sp):
            sp.dma_start(w1[:, :], i["L1_attn_W1"]).then_inc(loaded, 16)
            sp.dma_start(w2[:, :], i["L1_attn_W2"]).then_inc(loaded, 16)
            sp.dma_start(wqk[:, :], wqkv[0:P, :]).then_inc(loaded, 16)
            sp.dma_start(wv[:, :], wqkv[P:P + KW, :]).then_inc(loaded, 16)
            sp.dma_start(wout[:, :, :], i["L1_attn_Wout"].rearrange("(o p) n -> p o n", p=P)).then_inc(loaded, 16)
            sp.dma_start(wf[:, :, :], i["L1_ffn_weight"].rearrange("(o p) n -> p o n", p=P)).then_inc(loaded, 16)
            for o in range(2):
                sp.dma_start(scale[:, o:o + 1],
                             column(i["L1_ffn_scale_weight"][o * P:(o + 1) * P])).then_inc(loaded, 16)

        @block.vector
        def _(ve):
            ve.wait_ge(loaded, 128)
            for o in range(2):
                ve.tensor_scalar(wfs[:, o, :], wf[:, o, :], scale[:, o:o + 1], None, ALU.mult).then_inc(scaled, 1)

        odd = lambda w, c: w.rearrange("p (f c) -> p f c", c=C)[:, :, c]
        def turns():
            for c in range(C):
                yield bank[:, 0, c * P:(c + 1) * P], odd(w1[:, :], c), P
                yield bank[:, 1, c * P:(c + 1) * P], odd(wqk[:, :], c), P
                yield bank[:, 2, c * KW:(c + 1) * KW], odd(wv[:, :], c), KW
                yield bank[0:KW, 3, c * P:(c + 1) * P], wout[:, c, :], P
            yield bank[:, 4, 0:KW], w2[:, :], KW
            for o in range(2):
                for c in range(C):
                    yield bank[:, 5 + c, o * P:(o + 1) * P], odd(wfs[:, o, :], c), P

        @block.tensor
        def _(pe):
            pe.wait_ge(loaded, 128)
            pe.wait_ge(scaled, 2)
            for dst, src, rows in turns():
                mm = pe.transpose(dst, src, k.ident[0:rows, 0:rows])
            mm.then_inc(turned, 1)

        @block.scalar
        def _(act):
            act.wait_ge(turned, 1)
            pair = lambda b, n: bank[:, b, 0:C * n].rearrange("p (c n) -> p c n", c=C)
            act.activation(k.w1t[:, :, :], pair(0, P), ACT.Copy).then_inc(ready, 1)
            for z in range(2):
                for c in range(C):
                    for d in range(HD1):
                        at = z * KW
                        act.activation(
                            k.wqkvt[:, c, at:at + KW].rearrange("p (e d g) -> p e d g", e=4, d=HD1)[:, :, d, :],
                            bank[:, 1, c * P + at:c * P + at + KW].rearrange(
                                "p (g e d) -> p e d g", g=G, e=4)[:, :, d, :], ACT.Copy).then_inc(ready, 1)
            act.activation(k.wqkvt[:, :, P:P + KW], pair(2, KW), ACT.Copy).then_inc(ready, 1)
            act.activation(k.woutt[:, :], bank[0:KW, 3, 0:D], ACT.Copy).then_inc(ready, 1)
            act.activation(k.w2t[:, :], bank[:, 4, 0:KW], ACT.Copy).then_inc(ready, 1)
            act.activation(k.wft[:, :, :], bank[:, 5:7, 0:D], ACT.Copy).then_inc(ready, 1)
            act.wait_ge(ready, 13)


def keep_normalised(k):
    nc = k.nc
    normed, added = k.sem("y_normed"), k.sem("y_added")
    with nc.Block() as block:
        @block.vector
        def _(ve):
            xf, yf = (a[:, :, :].rearrange("p t d -> p (t d)") for a in (k.x, k.y))
            with ve.Fori(0, TILES) as t:
                at = bass.ds(t * D, D)
                ve.tensor_scalar(yf[:, at], xf[:, at], k.mean[:, bass.ds(t, 1)], k.rstd[:, bass.ds(t, 1)],
                                 ALU.subtract, ALU.mult).then_inc(normed, 1)
            with ve.Fori(0, TILES // 2) as t:
                at = bass.ds(t * 2 * D, 2 * D)
                ve.wait_ge(normed, TILES)
                ve.tensor_tensor(xf[:, at], xf[:, at], yf[:, at], ALU.add).then_inc(added, 1)
            ve.wait_ge(added, TILES // 2)


def second_projections(k):
    nc, i = k.nc, k.i
    loaded, filled, wiped = k.sem("p_loaded"), k.sem("p_filled"), k.sem("p_wiped")
    normed, turned, xt_ready = k.sem("p_normed"), k.sem("p_turned"), k.sem("p_xt_ready")
    h_done, h_ready, qk_done, qk_ready, v_done, v_ready = (k.sem("p_" + n) for n in (
        "h_done", "h_ready", "qk_done", "qk_ready", "v_done", "v_ready"))
    parted, stored = k.sem("p_parted"), k.sem("p_stored")
    with ExitStack() as local:
        def sb(name, shape, dt=F32):
            return local.enter_context(nc.sbuf_tensor("p" + name, shape, dt))
        gamma, beta, b1, bqk = sb("gamma", [P, C]), sb("beta", [P, C]), sb("b1", [P, 1]), sb("bqk", [KW, 2])
        bv = sb("bv", [P, KW])
        rows, xt = sb("rows", [P, TB, D]), sb("xt", [P, C, S])
        qk = sb("qk", [KW, 2, S])
        rest = sb("rest", [KW, 2, S])
        parts = sb("parts", [KW, 2, PRODUCTS, S], BF16)
        fill = sb("fill", [P, 2, S], BF16)
        bank = local.enter_context(nc.psum_tensor("pbank", [P, 8, 512], F32))
        block = local.enter_context(nc.Block())
        scratch = (k.q_dram, k.k_dram)

        @block.sync
        def _(sp):
            sp.dma_start(gamma[:, :], i["L1_attn_gamma"].rearrange("(p c) -> p c", c=C)).then_inc(loaded, 16)
            sp.dma_start(beta[:, :], i["L1_attn_beta"].rearrange("(p c) -> p c", c=C)).then_inc(loaded, 16)
            sp.dma_start(b1[:, :], column(i["L1_attn_b1"])).then_inc(loaded, 16)
            for z in range(2):
                byhead = i["L1_attn_bqkv"][z * KW:(z + 1) * KW].rearrange("(g c d a) -> c d g a", g=G, c=4, a=1)
                for c in range(4):
                    for d in range(HD1):
                        at = (c * HD1 + d) * G
                        sp.dma_start(bqk[at:at + G, z:z + 1], byhead[c, d], allow_slow_non_contiguous=True).then_inc(loaded, 16)
            sp.dma_start(bv[:, :], everyone(i["L1_attn_bqkv"][2 * KW:3 * KW])).then_inc(loaded, 16)
            sp.wait_ge(filled, 2)
            for z in range(2):
                for b in range(B):
                    sp.dma_start(scratch[z][b], fill[:, z, :].unsqueeze(1).broadcast_to([P, G, S])).then_inc(wiped, 16)
            sp.wait_ge(wiped, 16 * 2 * B)
            with sp.Fori(0, B) as b:
                for z in range(2):
                    sp.wait_ge(parted, b * 8 + 4 * z + 4)
                    pause(sp, k)
                    for c in range(4):
                        at = 32 * c + ROW0
                        rows_of = scratch[z][bass.ds(b, 1), at:at + HD1 * PRODUCTS, :, :].rearrange(
                            "b (m d) g s -> (b d g) m s", d=HD1)
                        sp.dma_start(rows_of, parts[16 * c:16 * c + 16, z, :, :]).then_inc(stored, 16)
                sp.wait_ge(stored, b * (16 * 2 * 4) + 16 * 2 * 4 + 16)
                pause(sp, k)

        @block.gpsimd
        def _(pool):
            pool.memset(fill[:, 0, :], 0.0).then_inc(filled, 1)
            pool.memset(fill[:, 1, :], 1.0).then_inc(filled, 1)

        @block.vector
        def _(ve):
            ve.wait_ge(loaded, 16 * 20)
            ve.sem_inc(stored, 16)
            with ve.Fori(0, B) as b:
                for j in range(TB):
                    normalise_tile(ve, k, k.y, rows, b, j).then_inc(normed, 1)
                ve.wait_ge(h_done, b + 1)
                ve.tensor_scalar(k.hneg[:, bass.ds(b * S, S)], bank[:, 2, :], -1.0, None, ALU.mult).then_inc(h_ready, 1)
                ve.tensor_scalar(k.hplus[:, bass.ds(b * S, S)], bank[:, 2, :], b1[:, 0:1], None, ALU.add).then_inc(h_ready, 1)
                ve.wait_ge(v_done, b + 1)
                ve.tensor_tensor(k.v[:, bass.ds(b * TB, TB), :], bank[:, 3, 0:TB * KW].rearrange("p (t n) -> p t n", t=TB),
                                 bv[:, :].unsqueeze(1).broadcast_to([P, TB, KW]), ALU.add).then_inc(v_ready, 1)
                n = Tally(b, 8)
                ve.wait_ge(stored, b * (16 * 2 * 4) + 16)
                for z in range(2):
                    ve.wait_ge(qk_ready, b * 2 + z + 1)
                    slots = [parts[:, z, at, :] for at in SLOTS[z]]
                    spread = lambda a, slot: a.unsqueeze(1).broadcast_to(list(slot.shape))
                    ve.tensor_copy(slots[0], spread(qk[:, z, :], slots[0])).then_inc(parted, n.up())
                    ve.wait_ge(parted, n.now())
                    ve.tensor_tensor(rest[:, z, :], qk[:, z, :], slots[0][:, 0, :], ALU.subtract).then_inc(parted, n.up())
                    ve.wait_ge(parted, n.now())
                    ve.tensor_copy(slots[1], spread(rest[:, z, :], slots[1])).then_inc(parted, n.up())
                    ve.wait_ge(parted, n.now())
                    ve.tensor_tensor(slots[2][:, 0, :], rest[:, z, :], slots[1][:, 0, :],
                                     ALU.subtract).then_inc(parted, n.up())
                assert n.n == 8

        @block.scalar
        def _(act):
            act.wait_ge(loaded, 16 * 20)
            with act.Fori(0, B) as b:
                for c in range(C):
                    act.wait_ge(turned, b * C + c + 1)
                    act.activation(xt[:, c, :], bank[:, c, :], ACT.Identity, bias=beta[:, c:c + 1],
                                   scale=gamma[:, c:c + 1]).then_inc(xt_ready, 1)
                for z in range(2):
                    act.wait_ge(qk_done, b * 2 + z + 1)
                    act.activation(qk[:, z, :], bank[0:KW, 4 + z, :], ACT.Identity,
                                   bias=bqk[:, z:z + 1]).then_inc(qk_ready, 1)

        @block.tensor
        def _(pe):
            with pe.Fori(0, B) as b:
                pe.wait_ge(normed, b * TB + TB)
                for c in range(C):
                    for j in range(TB):
                        mm = transpose_features(pe, k, bank[:, c, :], rows, j, c)
                    mm.then_inc(turned, 1)
                pe.wait_ge(xt_ready, b * C + C)
                for c in range(C):
                    mm = pe.matmul(bank[:, 2, :], k.w1t[:, c, :], xt[:, c, :], start=c == 0, stop=c == C - 1)
                mm.then_inc(h_done, 1)
                for z in range(2):
                    for c in range(C):
                        mm = pe.matmul(bank[0:KW, 4 + z, :], k.wqkvt[:, c, z * KW:(z + 1) * KW], xt[:, c, :],
                                       start=c == 0, stop=c == C - 1)
                    mm.then_inc(qk_done, 1)
                for j in range(TB):
                    for c in range(C):
                        mm = pe.matmul(bank[:, 3, j * KW:(j + 1) * KW], xt[:, c, j * P:(j + 1) * P],
                                       k.wqkvt[:, c, 2 * KW:3 * KW], start=c == 0, stop=c == C - 1)
                mm.then_inc(v_done, 1)
                pe.wait_ge(h_ready, b * 2 + 2)
                pe.wait_ge(v_ready, b + 1)
                pe.wait_ge(qk_ready, b * 2 + 2)


STEP_I = 8
STEPS = P // STEP_I


def pairwise(k):
    nc, i = k.nc, k.i
    ROUNDS = -(-KEEP // 8)
    assert ROUNDS == STEPS // 2 - 1
    R = 4
    PER = 3 * ROUNDS + 2
    AHEAD1 = 2 * R
    AHEAD2 = 2
    AHEAD3 = R
    loaded, set_up, made = k.sem("s_loaded"), k.sem("s_set_up"), k.sem("s_made")
    shifted, windowed, units, products, hidden, summed, sim_out, search = (k.sem("s_" + n) for n in (
        "shifted", "windowed", "units", "products", "hidden", "summed", "sim_out", "search"))
    mask_made, mask_turned, mask_kept = k.sem("s_mask_made"), k.sem("s_mask_turned"), k.sem("s_mask_kept")
    with ExitStack() as local:
        def sb(name, shape, dt=F32):
            return local.enter_context(nc.sbuf_tensor("s" + name, shape, dt))
        w3, b2, b3 = sb("w3", [P, 1]), sb("b2", [P, 1]), sb("b3", [P, 1])
        bands = sb("bands", [P, STEPS * 34])
        top = sb("top", [P, 2])
        window = sb("window", [P, R, 32])
        shift = sb("shift", [P, R, 4, 2])
        unit1 = sb("unit1", [P, R, STEP_I, S])
        unit2 = sb("unit2", [P, 2, 4, S])
        offdiag = sb("offdiag", [P, TB, S])
        sim, work = sb("sim", [P, S]), sb("work", [P, S])
        best, cut = sb("best", [P, 8]), sb("cut", [P, 8])
        cap = sb("cap", [P, ROUNDS, 8])
        mask_now = sb("mask_now", [P, S], BF16)
        turned = local.enter_context(nc.psum_tensor("sturned", [P, 1024], BF16))
        pre = local.enter_context(nc.psum_tensor("spre", [P, 2, 2, 512], F32))
        simp = local.enter_context(nc.psum_tensor("ssims", [P, 512], F32))
        block = local.enter_context(nc.Block())
        plus = k.hplus[:, :].rearrange("p (n c x) -> p n c x", c=4, x=32)
        maskf = k.mask[:, :, :].rearrange("p t s -> p (t s)")
        capf = cap[:, :, :].rearrange("p r e -> p (r e)")
        offf = offdiag[:, :, :].rearrange("p t s -> p (t s)")

        @block.sync
        def _(sp):
            for z in range(2):
                sp.dma_start(w3[z * KW:(z + 1) * KW, :], i["L1_attn_W3"].rearrange("o (g a) -> (o g) a", a=1)).then_inc(loaded, 16)
                sp.dma_start(b2[z * KW:(z + 1) * KW, :], column(i["L1_attn_b2"])).then_inc(loaded, 16)
            sp.dma_start(b3[:, :], everyone(i["L1_attn_b3"])).then_inc(loaded, 16)

        @block.gpsimd
        def _(pool):
            pool.memset(bands[:, :], 0.0).then_inc(made, 1)
            pool.memset(top[:, :], 1.0).then_inc(made, 1)
            pool.memset(offdiag[:, :, :], 1.0).then_inc(made, 1)
            pool.memset(cap[:, :, :], -GONE).then_inc(made, 1)
            pool.memset(sim[:, :], 0.0).then_inc(set_up, 1)
            pool.wait_ge(made, 4)
            pool.memset(cap[:, ROUNDS - 1, KEEP - 8 * (ROUNDS - 1):8], GONE).then_inc(made, 1)
            for q, n, base in ((0, 1, (TB - 1) * P), (1, TB - 1, 0)):
                part = offdiag[:, q:q + n, :]
                pool.affine_select(out=part, in_=part, compare_op=ALU.not_equal, fill=0.0,
                                   base=base, pattern=[[P, n], [-1, S]], channel_multiplier=1).then_inc(made, 1)
            pool.affine_select(out=top[:, 0:1], in_=top[:, 0:1], compare_op=ALU.is_ge, fill=0.0, base=KW - 1,
                               pattern=[[0, 1]], channel_multiplier=-1).then_inc(made, 1)
            pool.affine_select(out=top[:, 1:2], in_=top[:, 1:2], compare_op=ALU.is_ge, fill=0.0, base=-KW,
                               pattern=[[0, 1]], channel_multiplier=1).then_inc(made, 1)
            pool.wait_ge(made, 9)
            pool.wait_ge(loaded, 80)
            pool.tensor_scalar(bands[:, :].rearrange("p (r x) -> p r x", x=34)[:, :, 0:2],
                               top[:, :].unsqueeze(1).broadcast_to([P, STEPS, 2]), w3[:, 0:1], None,
                               ALU.mult).then_inc(set_up, 1)
            pool.wait_ge(set_up, 2)
            with pool.Fori(0, TILES) as n:
                with pool.Fori(0, STEPS // R) as m:
                    for u in range(R):
                        t = n * STEPS + m * R + u
                        pool.wait_ge(units, t * STEP_I + STEP_I)
                        pause(pool, k)
                        pool.tensor_copy(shift[:, u, :, :].unsqueeze(1),
                                         plus[:, bass.ds(n, 1), :, bass.ds(m * (2 * R) + 2 * u, 2)]).then_inc(shifted, 1)
                        pool.wait_ge(summed, t + 1)
                        pause(pool, k)
                        pool.tensor_copy(window[:, u, :],
                                         bands[:, bass.ds(m * (32 * R) + 32 * u, 32)]).then_inc(windowed, 1)

        def first_layer(ve, b, t, u, extra=None):
            ve.wait_ge(shifted, t + 1)
            ve.wait_ge(products, t * 2 + 2)
            pause(ve, k)
            for j in range(STEP_I):
                ve.tensor_scalar(unit1[:, u, j, :], k.hneg[:, bass.ds(b * S, S)],
                                 shift[:, u, j // 2, j % 2:j % 2 + 1], 0.0, ALU.add, ALU.max).then_inc(units, 1)
                if extra and j in extra:
                    extra[j]()

        def search_round(ve, r, done):
            def top8():
                ve.wait_ge(search, done)
                pause(ve, k)
                ve.max(best[:, :], work[:, :]).then_inc(search, 1)

            def capped():
                ve.wait_ge(search, done + 1)
                ve.tensor_tensor(cut[:, :], best[:, :], capf[:, bass.ds(r * 8, 8)], ALU.min).then_inc(search, 1)

            def taken():
                ve.wait_ge(search, done + 2)
                pause(ve, k)
                ve.match_replace(work[:, :], cut[:, :], work[:, :], GONE).then_inc(search, 1)
            return top8, capped, taken

        def begin_search(ve, n, q):
            ve.wait_ge(sim_out, n + 1)
            ve.wait_ge(search, n * PER + 1)
            pause(ve, k)
            ve.tensor_tensor(work[:, :], sim[:, :], offf[:, bass.ds(q * S, S)], ALU.mult).then_inc(search, 1)

        def end_search(ve, n):
            ve.wait_ge(search, n * PER + PER)
            pause(ve, k)
            ve.tensor_scalar(maskf[:, bass.ds(n * S, S)], work[:, :], GONE, -OFF, ALU.not_equal,
                             ALU.mult).then_inc(search, 1)
            ve.wait_ge(mask_turned, n + 1)
            ve.tensor_scalar(mask_now[:, :], work[:, :], GONE, -OFF, ALU.not_equal, ALU.mult).then_inc(mask_made, 1)

        @block.vector
        def _(ve):
            ve.sem_inc(units, R * STEP_I)
            ve.sem_inc(search, 1)
            ve.wait_ge(set_up, 2)
            with ve.Fori(0, B) as b:
                with ve.Fori(0, TB) as q:
                    n = b * TB + q
                    t0, s0 = n * STEPS, n * PER + 2
                    first_layer(ve, b, t0, 0)
                    first_layer(ve, b, t0 + 1, 1)
                    begin_search(ve, n, q)
                    a, c, z = search_round(ve, n * 0, s0)
                    first_layer(ve, b, t0 + 2, 2, {1: a, 5: c})
                    first_layer(ve, b, t0 + 3, 3, {1: z})
                    with ve.Fori(0, STEPS // R - 1) as m:
                        for v in range(2):
                            a, c, z = search_round(ve, m * 2 + 1 + v, s0 + m * 6 + 3 + 3 * v)
                            first_layer(ve, b, t0 + m * R + (R + 2 * v), 2 * v, {1: a, 5: c})
                            first_layer(ve, b, t0 + m * R + (R + 2 * v + 1), 2 * v + 1, {1: z})
                    end_search(ve, n)
            begin_search(ve, TILES, 0)
            for r in range(ROUNDS):
                for part in search_round(ve, r, TILES * PER + 2 + 3 * r):
                    part()
            end_search(ve, TILES)
            ve.wait_ge(search, (TILES + 1) * PER + 1)
            ve.wait_ge(mask_made, TILES + 1)

        mask_tf = k.mask_t[:, :, :, :].rearrange("p t j s -> p (t j s)")

        def keep_mask(act, n):
            act.wait_ge(mask_turned, n + 2)
            act.activation(mask_tf[:, bass.ds(n * S, S)], turned[:, 0:S], ACT.Copy).then_inc(mask_kept, 1)

        @block.scalar
        def _(act):
            act.sem_inc(hidden, AHEAD2)
            act.sem_inc(sim_out, 1)
            act.sem_inc(mask_kept, 1)
            act.wait_ge(loaded, 80)
            with act.Fori(0, TILES) as n:
                with act.Fori(0, STEPS // 2) as m:
                    for v in range(2):
                        t = n * STEPS + m * 2 + v
                        for h in range(2):
                            act.wait_ge(products, t * 2 + h + 1 + AHEAD1)
                            act.wait_ge(summed, t + (AHEAD3 - 1))
                            act.activation(unit2[:, v, 2 * h:2 * h + 2, :], pre[:, h, :, :], ACT.Relu,
                                           bias=b2[:, 0:1]).then_inc(hidden, 1)
                act.wait_ge(summed, n * STEPS + STEPS + AHEAD3)
                act.wait_ge(search, n * PER + 2)
                act.activation(sim[:, :], simp[:, :], ACT.Identity, bias=b3[:, 0:1]).then_inc(sim_out, 1)
                keep_mask(act, n)
            keep_mask(act, TILES)

        def second_layer(pe, t, u):
            for h in range(2):
                pe.wait_ge(units, t * STEP_I + (R * STEP_I + 4 * h + 4))
                pe.wait_ge(hidden, t * 2 + h + 1)
                for c in range(2 * h, 2 * h + 2):
                    for s in range(2):
                        mm = pe.matmul(pre[s * KW:(s + 1) * KW, h, c % 2, :], k.w2t[:, :], unit1[:, u, 2 * c + s, :],
                                       start=True, stop=True)
                mm.then_inc(products, 1)

        def third_layer(pe, n, t, u, first=False):
            pe.wait_ge(windowed, t + 1)
            pe.wait_ge(hidden, t * 2 + 2 + AHEAD2)
            if first:
                pe.wait_ge(sim_out, n + 1)
            for c in range(4):
                mm = pe.matmul(simp[32 * c:32 * c + 32, :], window[:, u, :], unit2[:, u % 2, c, :], start=first,
                               stop=False, skip_group_check=True)
            mm.then_inc(summed, 1)

        def turn_mask(pe, n):
            pe.wait_ge(mask_made, n + 1)
            pe.wait_ge(mask_kept, n + 1)
            for j in range(TB):
                mm = pe.transpose(turned[:, j * P:(j + 1) * P], mask_now[:, j * P:(j + 1) * P], k.identb[:, :])
            mm.then_inc(mask_turned, 1)

        def tile(pe, n, more):
            t0 = n * STEPS
            for u in range(1, R):
                second_layer(pe, t0 + u, u)
                third_layer(pe, n, t0 + u - 1, u - 1, first=u == 1)
            with pe.Fori(0, STEPS // R - 1) as m:
                for u in range(R):
                    t = t0 + m * R + (R + u)
                    second_layer(pe, t, u)
                    third_layer(pe, n, t - 1, (u - 1) % R)
            if more:
                second_layer(pe, t0 + STEPS, 0)
            turn_mask(pe, n)
            third_layer(pe, n, t0 + STEPS - 1, R - 1)

        @block.tensor
        def _(pe):
            pe.sem_inc(products, AHEAD1)
            pe.sem_inc(summed, AHEAD3)
            pe.sem_inc(mask_turned, 1)
            pe.wait_ge(set_up, 2)
            second_layer(pe, 0, 0)
            with pe.Fori(0, TILES - 1) as n:
                tile(pe, n, True)
            tile(pe, TILES - 1, False)
            turn_mask(pe, TILES)


def second_attention(k):
    nc = k.nc
    U = 4 * TB
    R = 4
    set_up = k.sem("a1_set_up")
    q_in, k_in = ([k.sem(f"a1_{n}{r}") for r in range(R)] for n in ("q_in", "k_in"))
    v_in, mask_in = k.sem("a1_v_in"), k.sem("a1_mask_in")
    scored, peak, split, peaks_turned, q_ready = (k.sem("a1_" + n) for n in (
        "scored", "peak", "split", "peaks_turned", "q_ready"))
    masked, exped, mixed, mixed_ready, mixed_turned, normal = (k.sem("a1_" + n) for n in (
        "masked", "exped", "mixed", "mixed_ready", "mixed_turned", "normal"))
    SPLIT = 5
    LASTG = B * G - 1
    UNITS_AT = (3, 2, 3, 2, 3, 3, 0, 0)
    assert sum(UNITS_AT) == U
    NORMAL_AT = sum(UNITS_AT[:4])
    with ExitStack() as local:
        def sb(name, shape, dt=F32):
            return local.enter_context(nc.sbuf_tensor("b" + name, shape, dt))
        qs, ks = sb("qs", [P, R, S], BF16), sb("ks", [P, R, S], BF16)
        qm = sb("qm", [P, 2, S], BF16)
        vg = sb("vg", [P, 2, TB, 4, 32])
        junk = sb("junk", [P, 2, S], BF16)
        peaks = sb("peaks", [P, TB, 4])
        rest = sb("rest", [P, TB, 4])
        neg = sb("neg", [P, TB, 4])
        peak_parts = sb("peak_parts", [P, TB, 4, 32], BF16)
        pt = sb("pt", [P, 2, 4, TB, S])
        mixed_s = sb("mixed_s", [P, S])
        inv = sb("inv", [P, TB, 4])
        mask_s = sb("mask_s", [P, TB, S], BF16)
        s1 = local.enter_context(nc.psum_tensor("bs1", [P, 2, 512], F32))
        s2 = local.enter_context(nc.psum_tensor("bs2", [P, 2, 2, 512], F32))
        om = local.enter_context(nc.psum_tensor("bom", [P, 512], F32))
        misc = local.enter_context(nc.psum_tensor("bmisc", [P, 512], F32))
        miscb = misc[:, :].bitcast(BF16)
        block = local.enter_context(nc.Block())
        maskf = k.mask[:, :, :].rearrange("p t s -> p (t s)")
        mask_t = k.mask_t[:, :, :, :].rearrange("p t j s -> p j t s")
        parts_flat = peak_parts[:, :, :, :].rearrange("p q c r -> p q (c r)")
        ao_groups = k.ao[:, :, :].rearrange("p t (g c d) -> p t g c d", c=4, d=HD1)

        @block.sync
        def _(sp):
            with sp.Fori(0, B) as b:
                qd, kd = (a.rearrange("b p g s -> (b p) (g s)")[bass.ds(b * P, P), :] for a in (k.q_dram, k.k_dram))
                for g in range(G):
                    sp.wait_ge(masked, b * (8 * G) + 8 * g + 8)
                    pause(sp, k)
                    u = g % R
                    sp.dma_start(qs[:, u, :], qd[:, g * S:(g + 1) * S]).then_inc(q_in[u], 16)
                    sp.dma_start(ks[:, u, :], kd[:, g * S:(g + 1) * S]).then_inc(k_in[u], 16)

        @block.gpsimd
        def _(pool):
            pool.memset(peak_parts[:, :, :, :], 0.0).then_inc(set_up, 1)
            pool.memset(vg[:, :, :, :, :], 0.0).then_inc(set_up, 1)
            pool.wait_ge(set_up, 2)
            pool.memset(vg[:, :, :, :, 2:3], 1.0).then_inc(set_up, 1)
            vt = k.v[:, :, :].rearrange("p t (g c d) -> p t g c d", c=4, d=2)
            with pool.Fori(0, B) as b:
                for g in range(G):
                    pool.wait_ge(mixed, b * G + g + 1)
                    pause(pool, k)
                    pool.tensor_copy(vg[:, g % 2, :, :, 0:2],
                                     vt[:, bass.ds(b * TB, TB), g, :, :]).then_inc(v_in, 1)


        def scores1(pe, it, g, n):
            c, q = divmod(n, TB)
            if n == 0:
                uses = (it - g % R) * (16 // R) + 16
                pe.wait_ge(q_in[g % R], uses)
                pe.wait_ge(k_in[g % R], uses)
            pe.wait_ge(peak, it * U + n + 1)
            pe.matmul(s1[:, n % 2, :], qs[32 * c:32 * c + 32, g % R, q * P:(q + 1) * P],
                      ks[32 * c:32 * c + 32, g % R, :], start=True, stop=True).then_inc(scored, 1)

        def turn_peaks(pe, it):
            pe.wait_ge(split, it * SPLIT + SPLIT + 1)
            pause(pe, k)
            for q in range(TB):
                mm = pe.transpose(miscb[:, q * P:(q + 1) * P], parts_flat[:, q, :], k.identb[:, :])
            mm.then_inc(peaks_turned, 1)

        def scores2(pe, b, it, g, n, z):
            c, h = divmod(n, 2)
            j = 2 * h + z
            if z == 0:
                if n == 0:
                    pe.wait_ge(q_ready, it + 1)
                pe.wait_ge(exped, it * 8 + n + 1)
            pe.matmul(s2[:, n % 2, z, :], ks[32 * c:32 * c + 32, g % R, j * P:(j + 1) * P],
                      qm[32 * c:32 * c + 32, g % 2, :], start=True, stop=False)
            mm = pe.matmul(s2[:, n % 2, z, :].rearrange("p (t s) -> p t s", t=TB), k.identb[:, :],
                           mask_t[:, j, bass.ds(b * TB + 1, TB), :], start=False, stop=True)
            if z:
                mm.then_inc(masked, 1)

        def mix(pe, it, g, j):
            if j == 0:
                pe.wait_ge(v_in, it + 1)
                pe.wait_ge(mixed_ready, it + 1)
            pe.wait_ge(exped, it * 8 + (7 if j < 2 else 8) + 2)
            for c in range(4):
                mm = pe.matmul(om[32 * c:32 * c + 32, :], vg[:, g % 2, j, c, :], pt[:, g % 2, c, j, :],
                               start=j == 0, stop=j == TB - 1, skip_group_check=True)
            if j == TB - 1:
                mm.then_inc(mixed, 1)

        def turn_mixed(pe, it, peaks_added):
            pe.wait_ge(mixed_ready, it + 2)
            pe.wait_ge(q_ready, peaks_added)
            for q in range(TB):
                mm = pe.transpose(misc[:, q * P:(q + 1) * P], mixed_s[:, q * P:(q + 1) * P], k.ident[:, :])
            mm.then_inc(mixed_turned, 1)

        def group_on_tensor(pe, b, g, age=2, last=False):
            it = b * G + g
            n1 = 0

            def next_unit():
                nonlocal n1
                if n1 < sum(UNITS_AT[:n + 1]) and not last:
                    scores1(pe, it + 1, (g + 1) % G, n1)
                    n1 += 1

            for n in range(8):
                if n == 7 and not last:
                    if age:
                        pe.wait_ge(normal, it * 2 - 1)
                    turn_peaks(pe, it + 1)
                for z in range(2):
                    scores2(pe, b, it, g, n, z)
                    next_unit()
                if n % 2 == 0 and age:
                    mix(pe, it - 1, (g - 1) % G, n // 2)
                next_unit()
                if n == 2 and age == 2:
                    turn_mixed(pe, it - 2, it + 1)

        @block.tensor
        def _(pe):
            pe.sem_inc(masked, 8 * R)
            pe.sem_inc(mixed, 2)
            pe.sem_inc(mixed_turned, 1)
            pe.sem_inc(peaks_turned, 1)
            pe.wait_ge(set_up, 3)
            for n in range(U):
                scores1(pe, 0, 0, n)
            turn_peaks(pe, 0)
            for g in range(G):
                group_on_tensor(pe, 0, g, age=min(g, 2))
            with pe.Fori(1, B - 1) as b:
                for g in range(G):
                    group_on_tensor(pe, b, g)
            for g in range(G):
                group_on_tensor(pe, B - 1, g, last=g == G - 1)
            pe.wait_ge(normal, LASTG * 2 - 1)
            turn_mixed(pe, LASTG - 1, B * G)
            for j in range(TB):
                mix(pe, LASTG, G - 1, j)
            pe.wait_ge(normal, LASTG * 2 + 1)
            turn_mixed(pe, LASTG, B * G)

        def group_on_scalar(act, b, g, first):
            it = b * G + g
            for n in range(8):
                c, h = divmod(n, 2)
                act.wait_ge(masked, it * 8 + n + 1 + 8 * R)
                if n == 0:
                    act.wait_ge(mixed, it + 1)
                act.activation(pt[:, g % 2, c, 2 * h:2 * h + 2, :], s2[:, n % 2, :, :], ACT.Exp,
                               scale=HD1 ** -0.5).then_inc(exped, 1)
                if n == 6 and not first:
                    take_mixed(act, it - 1)

        def take_mixed(act, it):
            act.wait_ge(mixed, it + 3)
            act.wait_ge(mixed_turned, it + 1)
            act.activation(mixed_s[:, :], om[:, :], ACT.Copy).then_inc(mixed_ready, 1)

        @block.scalar
        def _(act):
            act.sem_inc(exped, 2)
            act.sem_inc(mixed_ready, 1)
            for g in range(G):
                group_on_scalar(act, 0, g, g == 0)
            with act.Fori(1, B) as b:
                for g in range(G):
                    group_on_scalar(act, b, g, False)
            take_mixed(act, LASTG)

        def fetch_masks(ve, b):
            ve.wait_ge(peak, b * (G * U) + 2)
            ve.tensor_copy(mask_s[:, :, :].rearrange("p t s -> p (t s)"),
                           maskf[:, bass.ds(b * (TB * S) + S, TB * S)]).then_inc(mask_in, 1)
            ve.wait_ge(mask_in, b + 1)

        def find_peak(ve, it, n):
            c, q = divmod(n, TB)
            if n == 0:
                ve.wait_ge(split, it * SPLIT + 1)
            ve.wait_ge(scored, it * U + n + 1)
            ve.wait_ge(peak, it * U + n + 1)
            pause(ve, k)
            ve.tensor_tensor_reduce(junk[:, n % 2, :], s1[:, n % 2, :], mask_s[:, q, :],
                                    1.0, GONE, ALU.add, ALU.max, peaks[:, q, c:c + 1]).then_inc(peak, 1)

        def split_peaks(ve, it):
            n = Tally(it, SPLIT, 1)
            part = lambda z: peak_parts[:, :, :, z]
            ve.wait_ge(peak, it * U + U + 2)
            ve.wait_ge(peaks_turned, it + 1)
            ve.tensor_scalar(neg[:, :, :], peaks[:, :, :], -1.0, None, ALU.mult).then_inc(split, n.up())
            ve.wait_ge(split, n.now())
            ve.tensor_copy(part(0), neg[:, :, :]).then_inc(split, n.up())
            ve.wait_ge(split, n.now())
            ve.tensor_tensor(rest[:, :, :], neg[:, :, :], part(0), ALU.subtract).then_inc(split, n.up())
            ve.wait_ge(split, n.now())
            ve.tensor_copy(part(1), rest[:, :, :]).then_inc(split, n.up())
            ve.wait_ge(split, n.now())
            ve.tensor_tensor(part(2), rest[:, :, :], part(1), ALU.subtract).then_inc(split, n.up())
            assert n.n == SPLIT

        def add_peaks(ve, it, g):
            ve.wait_ge(peaks_turned, it + 2)
            ve.wait_ge(masked, it * 8 + 8 * R - 8)
            ve.tensor_tensor(qm[:, g % 2, :], miscb[:, 0:S], qs[:, g % R, :], ALU.add).then_inc(q_ready, 1)

        def normalise(ve, b, it, g):
            ve.wait_ge(mixed_turned, it + 2)
            o = misc[:, :].rearrange("p (q c r) -> p q c r", q=TB, c=4)
            ve.wait_ge(normal, it * 2 + 1)
            ve.reciprocal(inv[:, :, :], o[:, :, :, 2]).then_inc(normal, 1)
            ve.wait_ge(normal, it * 2 + 2)
            ve.tensor_tensor(ao_groups[:, bass.ds(b * TB, TB), g, :, :], o[:, :, :, 0:2],
                             inv[:, :, :].unsqueeze(3).broadcast_to([P, TB, 4, HD1]), ALU.mult).then_inc(normal, 1)

        def group_on_vector(ve, b, g, age=2, last=False):
            it = b * G + g
            done_b, done_g = (b, g - 2) if g >= 2 else (b - 1, g + G - 2)
            next_b, next_g = (b, g + 1) if g < G - 1 else (b + 1, 0)
            if g == G - 1 and not last:
                fetch_masks(ve, next_b)
            for n in range(U + 1):
                if n == NORMAL_AT and age == 2:
                    normalise(ve, done_b, it - 2, done_g)
                if n < U and not last:
                    find_peak(ve, it + 1, n)
            if not last:
                split_peaks(ve, it + 1)
                add_peaks(ve, it + 1, next_g)

        @block.vector
        def _(ve):
            ve.sem_inc(peak, 2)
            ve.sem_inc(split, 1)
            ve.sem_inc(normal, 1)
            ve.wait_ge(set_up, 3)
            fetch_masks(ve, 0)
            for n in range(U):
                find_peak(ve, 0, n)
            split_peaks(ve, 0)
            add_peaks(ve, 0, 0)
            for g in range(G):
                group_on_vector(ve, 0, g, age=min(g, 2))
            with ve.Fori(1, B - 1) as b:
                for g in range(G):
                    group_on_vector(ve, b, g)
            for g in range(G):
                group_on_vector(ve, B - 1, g, last=g == G - 1)
            for g in range(G - 2, G):
                normalise(ve, B - 1, (B - 1) * G + g, g)
            ve.wait_ge(normal, B * G * 2 + 1)


def second_output(k):
    nc = k.nc
    loaded, ao_turned, ao_ready, out_done, step = (k.sem("o_" + n) for n in (
        "loaded", "ao_turned", "ao_ready", "out_done", "step"))
    with ExitStack() as local:
        ao_t = local.enter_context(nc.sbuf_tensor("oao_t", [KW, 2, S], F32))
        bout = local.enter_context(nc.sbuf_tensor("obout", [P, D], F32))
        tmp = local.enter_context(nc.sbuf_tensor("otmp", [P, 2, 2, S], F32))
        turned = local.enter_context(nc.psum_tensor("oturned", [P, 2, 512], F32))
        out = local.enter_context(nc.psum_tensor("oout", [P, 2, 2, 512], F32))
        block = local.enter_context(nc.Block())

        @block.sync
        def _(sp):
            sp.dma_start(bout[:, :], everyone(k.i["L1_attn_bout"])).then_inc(loaded, 16)

        @block.tensor
        def _(pe):
            for b in range(B + 1):
                if b < B:
                    if b >= 2:
                        pe.wait_ge(ao_ready, b - 1)
                    for q in range(TB):
                        mm = pe.transpose(turned[0:KW, b % 2, q * P:(q + 1) * P], k.ao[:, b * TB + q, :], k.ident[:, :])
                    mm.then_inc(ao_turned, 1)
                if b:
                    pe.wait_ge(ao_ready, b)
                    if b >= 3:
                        pe.wait_ge(step, 4 * (b - 3) + 2)
                    for q in range(TB):
                        mm = pe.matmul(out[:, (b - 1) % 2, q // 2, (q % 2) * D:(q % 2) * D + D],
                                       ao_t[:, (b - 1) % 2, q * P:(q + 1) * P], k.woutt[:, :], start=True, stop=True)
                    mm.then_inc(out_done, 1)

        @block.scalar
        def _(act):
            for b in range(B):
                act.wait_ge(ao_turned, b + 1)
                if b >= 2:
                    act.wait_ge(out_done, b - 1)
                act.activation(ao_t[:, b % 2, :], turned[0:KW, b % 2, :], ACT.Copy).then_inc(ao_ready, 1)

        @block.vector
        def _(ve):
            ve.wait_ge(loaded, 16)
            for b in range(B):
                ve.wait_ge(out_done, b + 1)
                ve.wait_ge(step, 4 * b)
                for h in range(2):
                    ve.tensor_tensor(tmp[:, b % 2, h, :].rearrange("p (t n) -> p t n", t=2),
                                     out[:, b % 2, h, :].rearrange("p (t n) -> p t n", t=2),
                                     bout[:, :].unsqueeze(1).broadcast_to([P, 2, D]), ALU.add).then_inc(step, 1)
                ve.wait_ge(step, 4 * b + 2)
                for h in range(2):
                    x = k.x[:, b * TB + 2 * h:b * TB + 2 * h + 2, :].rearrange("p t d -> p (t d)")
                    ve.tensor_tensor(x, x, tmp[:, b % 2, h, :], ALU.add).then_inc(step, 1)
            ve.wait_ge(step, 4 * B)


def last_layer(k):
    nc, i = k.nc, k.i
    loaded, normed, turned, xt_ready, done, step = (k.sem("f_" + n) for n in (
        "loaded", "normed", "turned", "xt_ready", "done", "step"))
    stored = [k.sem(f"f_stored{z}") for z in range(2)]
    with ExitStack() as local:
        def sb(name, shape, dt=F32):
            return local.enter_context(nc.sbuf_tensor("f" + name, shape, dt))
        bias = sb("bias", [P, D])
        rows, xt = sb("rows", [P, 2, TB, D]), sb("xt", [P, 2, C, S])
        tmp = sb("tmp", [P, 2, TB, D])
        bank = local.enter_context(nc.psum_tensor("fbank", [P, 2, 4, 512], F32))
        xf = k.x[:, :, :].rearrange("p t d -> p (t d)")
        outs = k.out.rearrange("b (t p) d -> p b t d", p=P)
        block = local.enter_context(nc.Block())

        @block.sync
        def _(sp):
            sp.dma_start(bias[:, :], everyone(i["L1_ffn_bias"])).then_inc(loaded, 16)
            for b in range(B):
                sp.wait_ge(step, 4 * b + 4)
                sp.dma_start(outs[:, b, :, :], tmp[:, b % 2, :, :]).then_inc(stored[b % 2], 16)
            for z in range(2):
                sp.wait_ge(stored[z], 16 * B // 2)

        @block.vector
        def _(ve):
            ve.wait_ge(loaded, 16)
            for b in range(B + 1):
                if b < B:
                    if b >= 2:
                        ve.wait_ge(turned, 2 * b - 2)
                    for j in range(TB):
                        normalise_tile(ve, k, k.x, rows[:, b % 2, :, :], b, j).then_inc(normed, 1)
                if b:
                    a = b - 1
                    ve.wait_ge(done, a + 1)
                    if a >= 2:
                        ve.wait_ge(stored[a % 2], 16 * (a // 2))
                    for h in range(2):
                        part = tmp[:, a % 2, 2 * h:2 * h + 2, :]
                        ve.tensor_tensor(part, bank[:, a % 2, 2 + h, :].rearrange("p (t n) -> p t n", t=2),
                                         bias[:, :].unsqueeze(1).broadcast_to([P, 2, D]), ALU.add).then_inc(step, 1)
                    ve.wait_ge(step, 4 * a + 2)
                    for h in range(2):
                        part = tmp[:, a % 2, 2 * h:2 * h + 2, :]
                        ve.tensor_tensor(part, part, k.x[:, a * TB + 2 * h:a * TB + 2 * h + 2, :],
                                         ALU.add).then_inc(step, 1)

        @block.scalar
        def _(act):
            for b in range(B):
                for c in range(C):
                    act.wait_ge(turned, b * C + c + 1)
                    if b >= 2:
                        act.wait_ge(done, b - 1)
                    act.activation(xt[:, b % 2, c, :], bank[:, b % 2, c, :], ACT.Copy).then_inc(xt_ready, 1)

        @block.tensor
        def _(pe):
            for b in range(B):
                pe.wait_ge(normed, b * TB + TB)
                if b >= 2:
                    pe.wait_ge(step, 4 * b - 6)
                    pe.wait_ge(xt_ready, 2 * b - 2)
                for c in range(C):
                    for j in range(TB):
                        mm = transpose_features(pe, k, bank[:, b % 2, c, :], rows[:, b % 2, :, :], j, c)
                    mm.then_inc(turned, 1)
                pe.wait_ge(xt_ready, b * C + C)
                for j in range(TB):
                    for c in range(C):
                        mm = pe.matmul(bank[:, b % 2, 2 + j // 2, (j % 2) * D:(j % 2) * D + D],
                                       xt[:, b % 2, c, j * P:(j + 1) * P], k.wft[:, c, :], start=c == 0, stop=c == C - 1)
                mm.then_inc(done, 1)


def build(nc, ins, out):
    with ExitStack() as ctx:
        k = Kernel(nc, ctx, ins, out)

        def sb(name, shape, dt=F32, of=ctx):
            return of.enter_context(nc.sbuf_tensor(name, shape, dt))
        k.x = sb("x", [P, TILES, D])
        k.ident, k.identb = sb("ident", [P, P]), sb("identb", [P, P], BF16)
        k.mean, k.rstd = sb("mean", [P, TILES]), sb("rstd", [P, TILES])
        k.passed = k.sem("passed")
        k.w0_loaded, k.W0_LOADED = k.sem("w0_loaded"), 16 * 10
        with ExitStack() as local:
            wq, wk, wv, wo = (sb("a0" + name, [P, C, D], of=local) for name in ("wq", "wk", "wv", "wo"))
            bq, bk = sb("a0bq", [P, 2], of=local), sb("a0bk", [P, 2], of=local)
            bv, bo = sb("a0bv", [P, D], of=local), sb("a0bo", [P, D], of=local)
            k.w0 = FirstWeights(wq, wk, wv, wo, bq, bk, bv, bo)
            load_and_constants(k)
            row_statistics(k, "ln0", k.x)
            first_attention(k)
        row_statistics(k, "ln1", k.x)
        with ExitStack() as local:
            k.xt = sb("xt", [P, C, N], of=local)
            k.shares_dram = nc.dram_tensor("shares", (EXPERTS + SHARED // FE, N), F32, kind="Internal").ap()
            router(k)
            experts(k)
        k.w1t, k.wqkvt, k.w2t = sb("w1t", [P, C, P]), sb("wqkvt", [P, C, 3 * KW]), sb("w2t", [P, KW])
        k.woutt, k.wft = sb("woutt", [KW, D]), sb("wft", [P, C, D])
        k.q_dram = nc.dram_tensor("q_parts", (B, P, G, S), BF16, kind="Internal").ap()
        k.k_dram = nc.dram_tensor("k_parts", (B, P, G, S), BF16, kind="Internal").ap()
        k.v = sb("v", [P, TILES, KW])
        k.mask = sb("mask", [P, TILES + 1, S], BF16)
        k.mask_t = sb("mask_t", [P, TILES + 1, TB, P], BF16)
        k.ao = sb("ao", [P, TILES, KW])
        turn_weights_once(k)
        row_statistics(k, "ln2", k.x)
        with ExitStack() as local:
            k.hneg, k.hplus = sb("hneg", [P, N], of=local), sb("hplus", [P, N], of=local)
            with ExitStack() as inner:
                k.y = sb("y", [P, TILES, D], of=inner)
                keep_normalised(k)
                row_statistics(k, "ln3", k.y)
                second_projections(k)
            pairwise(k)
        second_attention(k)
        second_output(k)
        row_statistics(k, "ln4", k.x)
        last_layer(k)


INPUTS = ["L0_attn_x", "L0_attn_Wq", "L0_attn_bq", "L0_attn_Wk", "L0_attn_bk", "L0_attn_Wv", "L0_attn_bv",
          "L0_attn_Wo", "L0_attn_bo", "L0_ffn_router_w", "L0_ffn_router_bias", "L0_ffn_wg", "L0_ffn_wu",
          "L0_ffn_wd", "L0_ffn_swg", "L0_ffn_swu", "L0_ffn_swd", "L1_attn_gamma", "L1_attn_beta", "L1_attn_W1",
          "L1_attn_b1", "L1_attn_W2", "L1_attn_b2", "L1_attn_W3", "L1_attn_b3", "L1_attn_Wqkv", "L1_attn_bqkv",
          "L1_attn_Wout", "L1_attn_bout", "L1_ffn_weight", "L1_ffn_scale_weight", "L1_ffn_bias"]


def kernel(**inputs):
    import numpy as np
    import concourse.bacc as bacc
    from concourse.bass_utils import run_bass_kernel_spmd

    nc = bacc.Bacc("TRN2", target_bir_lowering=False, num_devices=1)
    arrays, aps = {}, {}
    for name in INPUTS:
        a = np.ascontiguousarray(inputs[name])
        arrays[name] = a
        aps[name] = nc.dram_tensor(name, a.shape, mybir.dt.from_np(a.dtype), kind="ExternalInput").ap()
    out = nc.dram_tensor("out", (B, S, D), F32, kind="ExternalOutput").ap()
    build(nc, aps, out)
    return run_bass_kernel_spmd(nc, [arrays], core_ids=[0]).results[0]["out"]
```

```python
from collections import namedtuple
from contextlib import ExitStack

import concourse.bass as bass
from concourse import mybir

F32 = mybir.dt.float32
BF16 = mybir.dt.bfloat16
ALU = mybir.AluOpType
ACT = mybir.ActivationFunctionType
AX = mybir.AxisListType

P = 128
B, S, D = 4, 512, 256
N = B * S
TB = S // P
TILES = N // P
C = D // P
EPS = 1e-5
HEADS0, HD0 = 4, 64
EXPERTS, FE, TOPK = 64, 64, 4
SHARED = 512
HT = (EXPERTS * FE + SHARED) // P
HEADS1, HD1, KW = 32, 2, 64
G = HEADS1 // 4
KEEP = int(S * 0.1)
GONE = -3.0e38
OFF = float(2.0 ** 126)


class Tally:

    def __init__(self, t=0, per=0, start=0):
        self.base, self.n = t * per + start, 0

    def up(self):
        self.n += 1
        return 1

    def now(self):
        return self.base + self.n


def pause(eng, k):
    eng.sem_inc(k.passed, 1)


def chunked(ap):
    return ap.rearrange("(p c) n -> p c n", c=C)


def column(ap):
    return ap.rearrange("(p a) -> p a", a=1)


def everyone(ap):
    return ap.partition_broadcast(P)


FirstWeights = namedtuple("FirstWeights", "wq wk wv wo bq bk bv bo")
ExpertSlots = namedtuple("ExpertSlots", "wg wu wd gate_in up_in down_in")
EXPERT_SLOTS = 4
Small = namedtuple("Small", "gamma beta b1 bqk bv w3 b2 b3 bout bias")
Network = namedtuple("Network", "bands top offdiag cap sim work best cut mask_now")
RawWeights = namedtuple("RawWeights", "w1 w2 wqk wv wout wf scale")


class Kernel:
    def __init__(self, nc, ctx, ins, out):
        self.nc, self.ctx, self.i, self.out = nc, ctx, ins, out

    def sem(self, name):
        return self.ctx.enter_context(self.nc.semaphore(name))


class Statistics:

    def __init__(self, k, tag, local):
        def sb(name, shape):
            return local.enter_context(k.nc.sbuf_tensor(tag + name, shape, F32))
        self.tile_done, self.step, self.root = k.sem(tag + "_tile_done"), k.sem(tag + "_step"), k.sem(tag + "_root")
        self.stats = sb("stats", [P, TILES, 6])
        self.half, self.spread, self.var, self.std, self.r0, self.r1 = (
            sb(n, [P, TILES]) for n in ("half", "spread", "var", "std", "r0", "r1"))


ROOT_AT, STAT_STEPS = 7, 12


def finish_statistics(ve, k, s, turn=0):
    step = s.step
    ve.wait_ge(s.tile_done, (turn + 1) * TILES)
    n = Tally(turn, STAT_STEPS)
    if turn:
        ve.wait_ge(step, n.now())
    ve.tensor_tensor(k.mean[:, :], s.stats[:, :, 1], s.stats[:, :, 4], ALU.add).then_inc(step, n.up())
    ve.tensor_tensor(s.half[:, :], s.stats[:, :, 1], s.stats[:, :, 4], ALU.subtract).then_inc(step, n.up())
    ve.tensor_tensor(s.spread[:, :], s.stats[:, :, 2], s.stats[:, :, 5], ALU.add).then_inc(step, n.up())
    ve.wait_ge(step, n.now())
    ve.tensor_scalar(k.mean[:, :], k.mean[:, :], 0.5, None, ALU.mult).then_inc(step, n.up())
    ve.scalar_tensor_tensor(out=s.half[:, :], in0=s.half[:, :], scalar=0.25, in1=s.half[:, :],
                            op0=ALU.mult, op1=ALU.mult).then_inc(step, n.up())
    ve.tensor_scalar(s.spread[:, :], s.spread[:, :], 1.0 / D, EPS, ALU.mult, ALU.add).then_inc(step, n.up())
    ve.wait_ge(step, n.now())
    ve.tensor_tensor(s.var[:, :], s.half[:, :], s.spread[:, :], ALU.add).then_inc(step, n.up())
    assert n.n == ROOT_AT
    ve.wait_ge(s.root, turn + 1)
    ve.reciprocal(s.r0[:, :], s.std[:, :]).then_inc(step, n.up())
    ve.wait_ge(step, n.now())
    ve.tensor_tensor(s.r1[:, :], s.r0[:, :], s.r0[:, :], ALU.mult).then_inc(step, n.up())
    ve.wait_ge(step, n.now())
    ve.tensor_tensor(s.r1[:, :], s.r1[:, :], s.var[:, :], ALU.mult).then_inc(step, n.up())
    ve.wait_ge(step, n.now())
    ve.tensor_scalar(s.r1[:, :], s.r1[:, :], -0.5, 1.5, ALU.mult, ALU.add).then_inc(step, n.up())
    ve.wait_ge(step, n.now())
    ve.tensor_tensor(k.rstd[:, :], s.r0[:, :], s.r1[:, :], ALU.mult).then_inc(step, n.up())
    assert n.n == STAT_STEPS
    ve.wait_ge(step, n.now())


def take_root(act, s, turn=0):
    act.wait_ge(s.step, turn * STAT_STEPS + ROOT_AT)
    act.activation(s.std[:, :], s.var[:, :], ACT.Sqrt).then_inc(s.root, 1)


def load_and_constants(k):
    nc = k.nc
    x_in, ident_step = [k.sem(f"x_in{b}") for b in range(B)], k.sem("ident_step")
    i, W = k.i, k.w0
    with ExitStack() as local:
        s = Statistics(k, "ln0", local)
        block = local.enter_context(nc.Block())

        @block.sync
        def _(sp):
            for b in range(B):
                sp.dma_start(k.x[:, b * TB:b * TB + TB, :],
                             k.i["L0_attn_x"].rearrange("b (t p) d -> b p t d", p=P)[b]).then_inc(x_in[b], 16)
            for dst, name in ((W.wq, "Wq"), (W.wk, "Wk"), (W.wv, "Wv")):
                sp.dma_start(dst[:, :, :], chunked(i["L0_attn_" + name])).then_inc(k.w0_loaded, 16)
            sp.dma_start(W.wo[:, :, :], i["L0_attn_Wo"].rearrange("(c p) n -> p c n", p=P)).then_inc(k.w0_loaded, 16)
            for m in range(2):
                sp.dma_start(W.bq[:, m:m + 1], column(i["L0_attn_bq"][m * P:(m + 1) * P])).then_inc(k.w0_loaded, 16)
                sp.dma_start(W.bk[:, m:m + 1], column(i["L0_attn_bk"][m * P:(m + 1) * P])).then_inc(k.w0_loaded, 16)
            sp.dma_start(W.bv[:, :], everyone(i["L0_attn_bv"])).then_inc(k.w0_loaded, 16)
            sp.dma_start(W.bo[:, :], everyone(i["L0_attn_bo"])).then_inc(k.w0_loaded, 16)

        @block.vector
        def _(ve):
            for t in range(TILES):
                ve.wait_ge(x_in[t // TB], 16)
                ve.bn_stats(s.stats[:, t, :], k.x[:, t, :]).then_inc(s.tile_done, 1)
            finish_statistics(ve, k, s)

        @block.scalar
        def _(act):
            take_root(act, s)

        @block.gpsimd
        def _(pool):
            pool.memset(k.ident[:, :], 0.0).then_inc(ident_step, 1)
            pool.memset(k.identb[:, :], 0.0).then_inc(ident_step, 1)
            pool.wait_ge(ident_step, 2)
            for m in (k.ident, k.identb):
                pool.affine_select(out=m[:, :], in_=m[:, :], compare_op=ALU.not_equal, fill=1.0, base=0,
                                   pattern=[[-1, P]], channel_multiplier=1).then_inc(ident_step, 1)
            pool.wait_ge(ident_step, 4)


def normalise_tile(ve, k, src, dst, b, i):
    t = b * TB + i
    flat = src[:, :, :].rearrange("p t d -> p (t d)")
    return ve.tensor_scalar(dst[:, i, :], flat[:, bass.ds(t * D, D)], k.mean[:, bass.ds(t, 1)],
                            k.rstd[:, bass.ds(t, 1)], ALU.subtract, ALU.mult)


def transpose_features(pe, k, psum, rows, i, c):
    picked = rows[:, i, :].rearrange("p (f c) -> p f c", c=C)[:, :, c]
    return pe.transpose(psum[:, i * P:(i + 1) * P], picked, k.ident[:, :])


def first_attention(k):
    nc = k.nc
    UNITS = HEADS0 * TB
    LAG = 3
    WSLOTS = LAG + 1
    END = B * UNITS
    LAST = END + 2 * TB + LAG
    normed, scored, peak, exped, inverse, weighted, turned, turned_kept = (k.sem("a0_" + n) for n in (
        "normed", "scored", "peak", "exped", "inverse", "weighted", "turned", "turned_kept"))
    mixed, mixed_kept, out_step, halved = (k.sem("a0_" + n) for n in ("mixed", "mixed_kept", "out_step", "halved"))
    filled, taken = ([k.sem(f"a0_{n}{r}") for r in range(2)] for n in ("filled", "taken"))

    WINDOW = {0: ("x", 0), 1: ("x", 1), 2: ("qk", 0), 7: ("qk", 2), 8: ("out", 0), 9: ("out", 1),
              10: ("qk", 1), 11: ("v", 0), 13: ("v", 1), 15: ("qk", 3)}
    FIRST = [("x", 0), ("x", 1), ("qk", 0), ("qk", 2), ("v", 0), ("v", 1), ("qk", 1), ("qk", 3)]

    def piece(slot):
        b, u = divmod(slot, UNITS)
        kind, m = WINDOW.get(u, (None, 0))
        of = b - 1 if kind == "out" else b + 1
        return (kind, of, m) if kind and 0 <= of < B else None

    order = [(kind, 0, m) for kind, m in FIRST] + [p for s in range(END + UNITS) if (p := piece(s))]
    use_of = {p: (n % 2, n // 2) for n, p in enumerate(order)}

    with ExitStack() as local:
        def sb(name, shape, dt=F32):
            return local.enter_context(nc.sbuf_tensor("a0" + name, shape, dt))
        stat = Statistics(k, "ln1", local)
        half_bq = sb("half_bq", [P, 2])
        rows = sb("rows", [P, TB, D])
        xt = sb("xt", [P, C, S])
        qk = sb("qk", [P, 2, 4, S])
        v = sb("v", [P, 2, TB, D])
        negpeak, total, inv = (sb(n, [P, END]) for n in ("negpeak", "total", "inv"))
        w = sb("w", [P, WSLOTS, S])
        wt = sb("wt", [P, 4, TB, S])
        ft = sb("ft", [P, 2, S])
        tmp = sb("tmp", [P, 2, S])
        scores = local.enter_context(nc.psum_tensor("a0scores", [P, 3, 512], F32))
        turn = local.enter_context(nc.psum_tensor("a0turn", [P, 2, 512], F32))
        mix = local.enter_context(nc.psum_tensor("a0mix", [P, 512], F32))
        prod = local.enter_context(nc.psum_tensor("a0prod", [P, 2, 512], F32))
        block = local.enter_context(nc.Block())
        W = k.w0

        def mixes(slot):
            pair, j = divmod(slot - LAG - 2 * TB, 2 * TB)
            return (pair, j) if j < TB and 0 <= pair < 2 * B else None

        @block.sync
        def _(sp):
            i, M = k.i, k.small
            R, wqkv = k.raw, i["L1_attn_Wqkv"]
            sp.dma_start(R.w1[:, :], i["L1_attn_W1"]).then_inc(k.raw_loaded, 16)
            sp.dma_start(R.w2[:, :], i["L1_attn_W2"]).then_inc(k.raw_loaded, 16)
            sp.dma_start(R.wqk[:, :], wqkv[0:P, :]).then_inc(k.raw_loaded, 16)
            sp.dma_start(R.wv[:, :], wqkv[P:P + KW, :]).then_inc(k.raw_loaded, 16)
            sp.dma_start(R.wout[:, :, :], i["L1_attn_Wout"].rearrange("(o p) n -> p o n", p=P)).then_inc(k.raw_loaded, 16)
            sp.dma_start(R.wf[:, :, :], i["L1_ffn_weight"].rearrange("(o p) n -> p o n", p=P)).then_inc(k.raw_loaded, 16)
            for o in range(2):
                sp.dma_start(R.scale[:, o:o + 1],
                             column(i["L1_ffn_scale_weight"][o * P:(o + 1) * P])).then_inc(k.raw_loaded, 16)
            sp.dma_start(M.gamma[:, :], i["L1_attn_gamma"].rearrange("(p c) -> p c", c=C)).then_inc(k.small_loaded, 16)
            sp.dma_start(M.beta[:, :], i["L1_attn_beta"].rearrange("(p c) -> p c", c=C)).then_inc(k.small_loaded, 16)
            sp.dma_start(M.b1[:, :], column(i["L1_attn_b1"])).then_inc(k.small_loaded, 16)
            sp.dma_start(M.bv[:, :], everyone(i["L1_attn_bqkv"][2 * KW:3 * KW])).then_inc(k.small_loaded, 16)
            for z in range(2):
                byhead = i["L1_attn_bqkv"][z * KW:(z + 1) * KW].rearrange("(g c d a) -> c d g a", g=G, c=4, a=1)
                for c in range(4):
                    for d in range(HD1):
                        at = (c * HD1 + d) * G
                        sp.dma_start(M.bqk[at:at + G, z:z + 1], byhead[c, d],
                                     allow_slow_non_contiguous=True).then_inc(k.small_loaded, 16)
            for z in range(2):
                half = slice(z * KW, (z + 1) * KW)
                sp.dma_start(M.w3[half, :], i["L1_attn_W3"].rearrange("o (g a) -> (o g) a", a=1)).then_inc(k.small_loaded, 16)
                sp.dma_start(M.b2[half, :], column(i["L1_attn_b2"])).then_inc(k.small_loaded, 16)
            sp.dma_start(M.b3[:, :], everyone(i["L1_attn_b3"])).then_inc(k.small_loaded, 16)
            sp.dma_start(M.bout[:, :], everyone(i["L1_attn_bout"])).then_inc(k.small_loaded, 16)
            sp.dma_start(M.bias[:, :], everyone(i["L1_ffn_bias"])).then_inc(k.small_loaded, 16)

        def normalise_rows(ve, b):
            for j in range(TB):
                if b:
                    ve.wait_ge(filled[use_of["x", b - 1, 1][0]], use_of["x", b - 1, 1][1] + 1)
                t = b * TB + j
                ve.tensor_scalar(rows[:, j, :], k.x[:, t, :], k.mean[:, t:t + 1], k.rstd[:, t:t + 1],
                                 ALU.subtract, ALU.mult).then_inc(normed, 1)

        def weigh(ve, u):
            ve.wait_ge(exped, u + 1)
            ve.reciprocal(inv[:, u:u + 1], total[:, u:u + 1]).then_inc(inverse, 1)
            ve.wait_ge(inverse, u + 1)
            ve.tensor_scalar(w[:, u % WSLOTS, :], w[:, u % WSLOTS, :], inv[:, u:u + 1], None,
                             ALU.mult).then_inc(weighted, 1)

        def take_on_vector(ve, p):
            kind, b, h = p
            if kind not in ("v", "out"):
                return
            bank, use = use_of[p]
            ve.wait_ge(filled[bank], use + 1)
            src = prod[:, bank, :].rearrange("p (t n) -> p t n", t=2)
            if kind == "v":
                if b >= 2:
                    ve.wait_ge(mixed, 2 * (b - 2) + 2)
                ve.tensor_tensor(v[:, b % 2, 2 * h:2 * h + 2, :], src,
                                 W.bv[:, :].unsqueeze(1).broadcast_to([P, 2, D]), ALU.add).then_inc(taken[bank], 1)
            else:
                x = k.x[:, b * TB + 2 * h:b * TB + 2 * h + 2, :]
                if b:
                    ve.wait_ge(out_step, 2 * (b - 1) + h + 1)
                ve.tensor_tensor(tmp[:, h, :].rearrange("p (t n) -> p t n", t=2), src,
                                 W.bo[:, :].unsqueeze(1).broadcast_to([P, 2, D]), ALU.add).then_inc(taken[bank], 1)
                ve.wait_ge(taken[bank], use + 1)
                ve.tensor_tensor(x, x, tmp[:, h, :].rearrange("p (t n) -> p t n", t=2),
                                 ALU.add).then_inc(out_step, 1)
                ve.wait_ge(out_step, 2 * b + h + 1)
                for t in range(b * TB + 2 * h, b * TB + 2 * h + 2):
                    ve.bn_stats(stat.stats[:, t, :], k.x[:, t, :]).then_inc(stat.tile_done, 1)

        @block.vector
        def _(ve):
            ve.wait_ge(k.w0_loaded, k.W0_LOADED)
            ve.tensor_scalar(half_bq[:, :], W.bq[:, :], 0.5, None, ALU.mult).then_inc(halved, 1)
            normalise_rows(ve, 0)
            for kind, m in FIRST:
                take_on_vector(ve, (kind, 0, m))
            normalise_rows(ve, 1)
            for s in range(LAST):
                if s < END:
                    ve.wait_ge(scored, s + 1)
                    ve.tensor_reduce(negpeak[:, s:s + 1], scores[:, s % 3, :], AX.X, ALU.max,
                                     negate=True).then_inc(peak, 1)
                if 0 < s <= END:
                    weigh(ve, s - 1)
                if piece(s):
                    take_on_vector(ve, piece(s))
                b, u = divmod(s, UNITS)
                if u == 3 and b + 2 < B:
                    normalise_rows(ve, b + 2)
            finish_statistics(ve, k, stat)

        def take_on_scalar(act, p):
            kind, b, m = p
            if kind not in ("x", "qk"):
                return
            bank, use = use_of[p]
            act.wait_ge(filled[bank], use + 1)
            if kind == "x":
                if b:
                    last = max(("v", b - 1, 1), ("qk", b - 1, 3), key=order.index)
                    act.wait_ge(filled[use_of[last][0]], use_of[last][1] + 1)
                act.activation(xt[:, m, :], prod[:, bank, :], ACT.Copy).then_inc(taken[bank], 1)
            else:
                if b >= 2:
                    act.wait_ge(scored, (b - 1) * UNITS)
                if m < 2:
                    act.activation(qk[:, b % 2, m, :], prod[:, bank, :], ACT.Identity, bias=half_bq[:, m:m + 1],
                                   scale=0.5).then_inc(taken[bank], 1)
                else:
                    act.activation(qk[:, b % 2, m, :], prod[:, bank, :], ACT.Identity,
                                   bias=W.bk[:, m - 2:m - 1]).then_inc(taken[bank], 1)

        @block.scalar
        def _(act):
            act.wait_ge(halved, 1)
            act.wait_ge(k.w0_loaded, k.W0_LOADED)
            for kind, m in FIRST:
                take_on_scalar(act, (kind, 0, m))
            for s in range(LAST):
                if 0 <= s - LAG < END:
                    u = s - LAG
                    h, q = divmod(u, TB)
                    act.wait_ge(turned, u + 1)
                    if h >= 4:
                        act.wait_ge(mixed, h // 2 - 1)
                    act.activation(wt[:, h % 4, :, q * P:(q + 1) * P],
                                   turn[:, u % 2, :].rearrange("p (j s) -> p j s", j=TB), ACT.Copy).then_inc(turned_kept, 1)
                if s < END:
                    act.wait_ge(peak, s + 1)
                    if s >= WSLOTS:
                        act.wait_ge(turned, s - WSLOTS + 1)
                    act.activation(w[:, s % WSLOTS, :], scores[:, s % 3, :], ACT.Exp, bias=negpeak[:, s:s + 1],
                                   accum_out=total[:, s:s + 1]).then_inc(exped, 1)
                if piece(s):
                    take_on_scalar(act, piece(s))
                if mixes(s) and mixes(s)[1] == TB - 1:
                    pair = mixes(s)[0]
                    act.wait_ge(mixed, pair + 1)
                    if pair >= 2:
                        bank, use = use_of["out", pair // 2 - 1, 1]
                        act.wait_ge(filled[bank], use + 1)
                    act.activation(ft[:, pair % 2, :], mix[:, :], ACT.Copy).then_inc(mixed_kept, 1)
            take_root(act, stat)

        def make(pe, p):
            kind, b, m = p
            bank, use = use_of[p]
            if use:
                pe.wait_ge(taken[bank], use)
            out = prod[:, bank, :]

            def kept(*what):
                other, its_use = use_of[what]
                pe.wait_ge(taken[other], its_use + 1)

            if kind == "x":
                pe.wait_ge(normed, b * TB + TB)
                for j in range(TB):
                    mm = transpose_features(pe, k, out, rows, j, m)
            elif kind == "qk":
                kept("x", b, 0)
                kept("x", b, 1)
                wts = W.wq if m < 2 else W.wk
                for c in range(C):
                    mm = pe.matmul(out, wts[:, c, (m % 2) * P:(m % 2) * P + P], xt[:, c, :], start=c == 0, stop=c == C - 1)
            elif kind == "v":
                kept("x", b, 0)
                kept("x", b, 1)
                for j in range(2):
                    for c in range(C):
                        mm = pe.matmul(out[:, j * D:(j + 1) * D], xt[:, c, (2 * m + j) * P:(2 * m + j + 1) * P],
                                       W.wv[:, c, :], start=c == 0, stop=c == C - 1)
            else:
                pe.wait_ge(mixed_kept, 2 * b + 2)
                for j in range(2):
                    for c in range(2):
                        mm = pe.matmul(out[:, j * D:(j + 1) * D], ft[:, c, (2 * m + j) * P:(2 * m + j + 1) * P],
                                       W.wo[:, c, :], start=c == 0, stop=c == 1)
            mm.then_inc(filled[bank], 1)

        @block.tensor
        def _(pe):
            pe.wait_ge(k.w0_loaded, k.W0_LOADED)
            for kind, m in FIRST:
                make(pe, (kind, 0, m))
            for s in range(LAST):
                if s < END:
                    b, u = divmod(s, UNITS)
                    h, q = divmod(u, TB)
                    if s >= 3:
                        pe.wait_ge(exped, s - 2)
                    if q == 0 and h % 2 == 0:
                        for m in (h // 2, 2 + h // 2):
                            bank, use = use_of["qk", b, m]
                            pe.wait_ge(taken[bank], use + 1)
                    r = HD0 * (h % 2)
                    pe.matmul(scores[:, s % 3, :], qk[r:r + HD0, b % 2, h // 2, q * P:(q + 1) * P],
                              qk[r:r + HD0, b % 2, 2 + h // 2, :], start=True, stop=True).then_inc(scored, 1)
                if 0 <= s - LAG < END:
                    u = s - LAG
                    pe.wait_ge(weighted, u + 1)
                    if u >= 2:
                        pe.wait_ge(turned_kept, u - 1)
                    for j in range(TB):
                        mm = pe.transpose(turn[:, u % 2, j * P:(j + 1) * P], w[:, u % WSLOTS, j * P:(j + 1) * P],
                                          k.ident[:, :])
                    mm.then_inc(turned, 1)
                if piece(s):
                    make(pe, piece(s))
                if mixes(s):
                    pair, j = mixes(s)
                    b, p2 = divmod(pair, 2)
                    if j == 0:
                        pe.wait_ge(turned_kept, (pair + 1) * 2 * TB)
                        bank, use = use_of["v", b, 1]
                        pe.wait_ge(taken[bank], use + 1)
                        bank, use = use_of["v", b, 0]
                        pe.wait_ge(taken[bank], use + 1)
                        if pair:
                            pe.wait_ge(mixed_kept, pair)
                    for e in range(2):
                        h = 2 * p2 + e
                        mm = pe.matmul(mix[e * HD0:(e + 1) * HD0, :], v[:, b % 2, j, h * HD0:(h + 1) * HD0],
                                       wt[:, (2 * pair + e) % 4, j, :], start=j == 0, stop=j == TB - 1,
                                       skip_group_check=True)
                    if j == TB - 1:
                        mm.then_inc(mixed, 1)


def router(k):
    nc, i = k.nc, k.i
    loaded, set_up = k.sem("r_loaded"), k.sem("r_set_up")
    normed, turned, xt_ready = k.sem("r_normed"), k.sem("r_turned"), k.sem("r_xt_ready")
    logit_done, logit_ready, logit_turned = k.sem("r_logit_done"), k.sem("r_logit_ready"), k.sem("r_logit_turned")
    step, exped, comb_turned, comb_ready, stored = (k.sem("r_" + n) for n in (
        "step", "exped", "comb_turned", "comb_ready", "stored"))
    PAD = EXPERTS + 8
    PEAKED, ROUTED = 4, 2 * TILES + 15
    with ExitStack() as local:
        def sb(name, shape, dt=F32):
            return local.enter_context(nc.sbuf_tensor("r" + name, shape, dt))
        wr, bias = sb("wr", [P, C, EXPERTS]), sb("bias", [P, EXPERTS])
        rows = sb("rows", [P, 2, TB, D])
        logit_t = sb("logit_t", [EXPERTS, 2, S])
        logit = sb("logit", [P, TILES, EXPERTS])
        ranked = sb("ranked", [P, TILES, PAD])
        best, cap = sb("best", [P, TILES, 8]), sb("cap", [P, 8])
        negpeak, total, inv = sb("negpeak", [P, TILES]), sb("total", [P, TILES]), sb("inv", [P, TILES])
        picked, inv2 = sb("picked", [P, TILES]), sb("inv2", [P, TILES])
        share = sb("share", [P, TILES, EXPERTS])
        comb_t = sb("comb_t", [EXPERTS, N])
        ones = sb("ones", [SHARED // FE, N])
        bank = local.enter_context(nc.psum_tensor("rbank", [P, 8, 512], F32))
        block = local.enter_context(nc.Block())

        @block.sync
        def _(sp):
            sp.dma_start(wr[:, :, :], chunked(i["L0_ffn_router_w"])).then_inc(loaded, 16)
            sp.dma_start(bias[:, :], everyone(i["L0_ffn_router_bias"])).then_inc(loaded, 16)
            for r in range(EXPERT_SLOTS):
                fetch_weights(sp, k, r, r)
            sp.wait_ge(set_up, 3)
            sp.dma_start(k.shares_dram[EXPERTS:, :], ones[:, :]).then_inc(stored, 16)
            for b in range(B):
                seq = slice(b * S, (b + 1) * S)
                sp.wait_ge(comb_ready, b + 1)
                sp.dma_start(k.shares_dram[0:EXPERTS, seq], comb_t[:, seq]).then_inc(stored, 16)
            sp.wait_ge(stored, 16 * (B + 1))

        @block.gpsimd
        def _(pool):
            pool.memset(cap[:, 0:TOPK], -GONE).then_inc(set_up, 1)
            pool.memset(cap[:, TOPK:8], GONE).then_inc(set_up, 1)
            pool.memset(ones[:, :], 1.0).then_inc(set_up, 1)

        @block.vector
        def _(ve):
            n = Tally()
            wide = [P, TILES, EXPERTS]
            for b in range(B):
                if b >= 2:
                    ve.wait_ge(turned, (b - 2) * C + C)
                for j in range(TB):
                    t = b * TB + j
                    ve.tensor_scalar(rows[:, b % 2, j, :], k.x[:, t, :], k.mean[:, t:t + 1], k.rstd[:, t:t + 1],
                                     ALU.subtract, ALU.mult).then_inc(normed, 1)
            ve.memset(ranked[:, :, EXPERTS:PAD], GONE).then_inc(step, n.up())
            ve.wait_ge(loaded, 32)
            for h in range(2):
                ve.wait_ge(logit_turned, 2 * h + 2)
                ve.tensor_copy(logit[:, 8 * h:8 * h + 8, :],
                               bank[:, 4 + h, :].rearrange("p (t e) -> p t e", e=EXPERTS)).then_inc(step, n.up())
            ve.wait_ge(step, n.now())
            ve.tensor_reduce(negpeak[:, :], logit[:, :, :], AX.X, ALU.max, negate=True).then_inc(step, n.up())
            PEAKS = n.now()
            ve.tensor_tensor(ranked[:, :, 0:EXPERTS], logit[:, :, :],
                             bias[:, :].unsqueeze(1).broadcast_to(wide), ALU.add).then_inc(step, n.up())
            ve.wait_ge(step, n.now())
            for t in range(TILES):
                ve.max(best[:, t, :], ranked[:, t, :]).then_inc(step, n.up())
            ve.wait_ge(set_up, 3)
            ve.wait_ge(step, n.now())
            ve.tensor_tensor(best[:, :, :], best[:, :, :], cap[:, :].unsqueeze(1).broadcast_to([P, TILES, 8]),
                             ALU.min).then_inc(step, n.up())
            ve.wait_ge(step, n.now())
            for t in range(TILES):
                ve.match_replace(ranked[:, t, :], best[:, t, :], ranked[:, t, :], GONE).then_inc(step, n.up())
            ve.wait_ge(exped, TILES)
            ve.reciprocal(inv[:, :], total[:, :]).then_inc(step, n.up())
            ve.wait_ge(step, n.now())
            ve.tensor_tensor(share[:, :, :], share[:, :, :], inv[:, :].unsqueeze(2).broadcast_to(wide),
                             ALU.mult).then_inc(step, n.up())
            ve.wait_ge(step, n.now())
            ve.scalar_tensor_tensor(out=share[:, :, :], in0=ranked[:, :, 0:EXPERTS], scalar=GONE,
                                    in1=share[:, :, :], op0=ALU.is_equal, op1=ALU.mult).then_inc(step, n.up())
            ve.wait_ge(step, n.now())
            ve.tensor_reduce(picked[:, :], share[:, :, :], AX.X, ALU.add).then_inc(step, n.up())
            ve.wait_ge(step, n.now())
            ve.reciprocal(inv2[:, :], picked[:, :]).then_inc(step, n.up())
            ve.wait_ge(step, n.now())
            for b in range(B):
                part = share[:, b * TB:b * TB + TB, :]
                ve.tensor_tensor(part, part, inv2[:, b * TB:b * TB + TB].unsqueeze(2).broadcast_to([P, TB, EXPERTS]),
                                 ALU.mult).then_inc(step, n.up())
            assert (PEAKS, n.now()) == (PEAKED, ROUTED)

        @block.scalar
        def _(act):
            for b in range(B):
                for c in range(C):
                    act.wait_ge(turned, b * C + c + 1)
                    act.activation(k.xt[:, c, b * S:(b + 1) * S], bank[:, c, :], ACT.Copy).then_inc(xt_ready, 1)
                act.wait_ge(logit_done, b + 1)
                if b >= 2:
                    act.wait_ge(logit_turned, b - 1)
                act.activation(logit_t[:, b % 2, :], bank[0:EXPERTS, 2 + b % 2, :], ACT.Copy).then_inc(logit_ready, 1)
            act.wait_ge(step, PEAKED)
            for t in range(TILES):
                act.activation(share[:, t, :], logit[:, t, :], ACT.Exp, bias=negpeak[:, t:t + 1],
                               accum_out=total[:, t:t + 1]).then_inc(exped, 1)
            for b in range(B):
                act.wait_ge(comb_turned, b + 1)
                act.activation(comb_t[:, b * S:(b + 1) * S], bank[0:EXPERTS, 6 + b % 2, :],
                               ACT.Copy).then_inc(comb_ready, 1)

        @block.tensor
        def _(pe):
            def turn_rows(b):
                pe.wait_ge(normed, b * TB + TB)
                if b:
                    pe.wait_ge(xt_ready, b * C)
                for c in range(C):
                    for j in range(TB):
                        mm = transpose_features(pe, k, bank[:, c, :], rows[:, b % 2, :, :], j, c)
                    mm.then_inc(turned, 1)
            turn_rows(0)
            pe.wait_ge(loaded, 32)
            for b in range(B):
                pe.wait_ge(xt_ready, b * C + C)
                if b >= 2:
                    pe.wait_ge(logit_ready, b - 1)
                for c in range(C):
                    mm = pe.matmul(bank[0:EXPERTS, 2 + b % 2, :], wr[:, c, :], k.xt[:, c, b * S:(b + 1) * S],
                                   start=c == 0, stop=c == C - 1)
                mm.then_inc(logit_done, 1)
                if b + 1 < B:
                    turn_rows(b + 1)
                pe.wait_ge(logit_ready, b + 1)
                for j in range(TB):
                    at = (b % 2 * TB + j) * EXPERTS
                    mm = pe.transpose(bank[:, 4 + b // 2, at:at + EXPERTS], logit_t[:, b % 2, j * P:(j + 1) * P],
                                      k.ident[0:EXPERTS, 0:EXPERTS])
                mm.then_inc(logit_turned, 1)
            for b in range(B):
                pe.wait_ge(step, ROUTED - (B - 1 - b))
                if b >= 2:
                    pe.wait_ge(comb_ready, b - 1)
                for j in range(TB):
                    mm = pe.transpose(bank[0:EXPERTS, 6 + b % 2, j * P:(j + 1) * P],
                                      share[:, b * TB + j, :], k.ident[:, :])
                mm.then_inc(comb_turned, 1)


def fetch_weights(sp, k, tile, r):
    i, E = k.i, k.expert_slots
    for e in range(2):
        one = bass.ds(tile * 2 + e, 1)
        for name, dst, here in (("wg", E.wg, E.gate_in), ("wu", E.wu, E.up_in)):
            src = i["L0_ffn_" + name].rearrange("e (p c) f -> p e c f", c=C)[:, one, :, :]
            sp.dma_start(dst[:, r, :, e, :], src.rearrange("p e c f -> p (e c) f")).then_inc(here[r], 16)
    sp.dma_start(E.wd[:, r, :], i["L0_ffn_wd"].rearrange("e f d -> (e f) d")[bass.ds(tile * P, P), :]).then_inc(
        E.down_in[r], 16)


def experts(k):
    nc, i = k.nc, k.i
    H = N // 2
    R = EXPERT_SLOTS
    wg, wu, wd, gate_in, up_in, down_in = k.expert_slots
    share_in = [k.sem(f"e_share_in{r}") for r in range(R)]
    hidden_done, gated, scaled, hidden_ready, down_done = (k.sem("e_" + n) for n in (
        "hidden_done", "gated", "scaled", "hidden_ready", "down_done"))
    cleared, added = k.sem("e_cleared"), k.sem("e_added")
    with ExitStack() as local:
        def sb(name, shape, dt=F32):
            return local.enter_context(nc.sbuf_tensor("e" + name, shape, dt))
        shares = sb("shares", [P, R, H])
        sg = sb("sg", [P, 2, S])
        sgs = sb("sgs", [P, 2, S])
        hid = sb("hid", [P, 2, S])
        gu = local.enter_context(nc.psum_tensor("egu", [P, 4, 512], F32))
        acc = local.enter_context(nc.psum_tensor("eacc", [P, 4, 512], F32))
        xflat = k.x[:, :, :].rearrange("p t d -> p (t d)")
        xt_flat = k.xt[:, :, :].rearrange("p c n -> p (c n)")
        block = local.enter_context(nc.Block())
        sgr = i["L0_ffn_swg"].rearrange("s (p c) (q f) -> p s q c f", c=C, f=FE)
        sur = i["L0_ffn_swu"].rearrange("s (p c) (q f) -> p s q c f", c=C, f=FE)
        sdr = i["L0_ffn_swd"].rearrange("s h d -> (s h) d")
        flat = lambda w, r, c: w[:, r, c, :, :].rearrange("p e f -> p (e f)")

        def fetch_shares(sp, tile, r, half):
            for e in range(2):
                row = tile * 2 + e
                sp.dma_start(shares[e * FE:(e + 1) * FE, r, :],
                             k.shares_dram[bass.ds(row, 1), bass.ds(half * H, H)]
                             .broadcast_to([FE, H])).then_inc(share_in[r], 16)

        def fetch(sp, tile, r, use, half, shared=None):
            sp.wait_ge(down_done, use)
            pause(sp, k)
            if shared is None:
                fetch_weights(sp, k, tile, r)
            else:
                s, q = divmod(2 * shared, 4)
                for e in range(2):
                    sp.dma_start(wg[:, r, :, e, :], sgr[:, s, q + e, :, :]).then_inc(gate_in[r], 16)
                    sp.dma_start(wu[:, r, :, e, :], sur[:, s, q + e, :, :]).then_inc(up_in[r], 16)
                sp.dma_start(wd[:, r, :], sdr[shared * P:shared * P + P, :]).then_inc(down_in[r], 16)
            fetch_shares(sp, tile, r, half)

        def fetch_half(sp, half, first):
            with sp.Fori(first // R, EXPERTS // 2 // R) as m:
                for r in range(R):
                    fetch(sp, m * R + r, r, m * (2 * R) + (half * (2 * HT) + 2 * r + 2), half)
            for r in range(R):
                t = EXPERTS // 2 + r
                fetch(sp, t, r, half * (2 * HT) + 2 * t + 2, half, shared=r)

        @block.sync
        def _(sp):
            for r in range(R):
                fetch_shares(sp, r, r, 0)
            fetch_half(sp, 0, R)
            fetch_half(sp, 1, 0)

        LAST = 2 * HT

        def down(pe, r, q, t0, use):
            if q == 0:
                pe.wait_ge(down_in[r], use * 16 + 16)
            pe.wait_ge(hidden_ready, t0 * 2 + q + 1)
            for j in range(TB):
                tok = q * TB + j
                mm = pe.matmul(acc[:, tok // 2, (tok % 2) * D:(tok % 2) * D + D], hid[:, q, j * P:(j + 1) * P],
                               wd[:, r, :], start=False, stop=False, skip_group_check=True)
            mm.then_inc(down_done, 1)

        @block.tensor
        def _(pe):
            pe.sem_inc(down_done, 2 * R)
            with pe.Fori(0, 2) as half:
                with pe.Fori(0, HT // R) as m:
                    for r in range(R):
                        use = half * (HT // R) + m
                        t0 = use * R + r
                        pe.wait_ge(gate_in[r], use * 32 + 32)
                        pe.wait_ge(up_in[r], use * 32 + 32)
                        for q in range(2):
                            pe.wait_ge(scaled, t0 * 2 + q + 1)
                            pause(pe, k)
                            for w, z in ((wg, 0), (wu, 1)):
                                for c in range(C):
                                    mm = pe.matmul(gu[:, 2 * q + z, :],
                                                   flat(w, r, c),
                                                   xt_flat[:, bass.ds(half * H + (q * S + c * N), S)],
                                                   start=c == 0, stop=c == C - 1)
                                mm.then_inc(hidden_done, 1)
                            if q:
                                if r == 0:
                                    pe.wait_ge(cleared, half * 4 + 4)
                                    pause(pe, k)
                                down(pe, r, 0, t0, use)
                            elif r:
                                down(pe, r - 1, 1, t0 - 1, use)
                    down(pe, R - 1, 1, t0, use)


        @block.scalar
        def _(act):
            with act.Fori(0, 2 * HT) as t:
                for q in range(2):
                    act.wait_ge(hidden_done, t * 4 + 2 * q + 1)
                    act.wait_ge(scaled, t * 2 + q + 1)
                    act.activation(sg[:, q, :], gu[:, 2 * q, :], ACT.Silu).then_inc(gated, 1)

        @block.vector
        def _(ve):
            ve.sem_inc(scaled, 2)
            with ve.Fori(0, 2) as half:
                for z in range(4):
                    ve.memset(acc[:, z, :], 0.0).then_inc(cleared, 1)
                with ve.Fori(0, HT // R) as m:
                    for r in range(R):
                        use = half * (HT // R) + m
                        t0 = use * R + r
                        ve.wait_ge(share_in[r], use * 32 + 32)
                        for q in range(2):
                            ve.wait_ge(gated, t0 * 2 + q + 1)
                            ve.wait_ge(hidden_done, t0 * 4 + 2 * q + 2)
                            ve.tensor_tensor(sgs[:, q, :], gu[:, 2 * q + 1, :], sg[:, q, :], ALU.mult).then_inc(scaled, 1)
                            ve.wait_ge(scaled, t0 * 2 + q + 3)
                            ve.wait_ge(down_done, t0 * 2 + (q + 2 * R - 1))
                            ve.tensor_tensor(hid[:, q, :], sgs[:, q, :], shares[:, r, q * S:(q + 1) * S],
                                             ALU.mult).then_inc(hidden_ready, 1)
                ve.wait_ge(down_done, half * LAST + LAST + 2 * R)
                for z in range(4):
                    at = half * (N // 2 // P * D) + z * 512
                    ve.tensor_tensor(xflat[:, bass.ds(at, 512)], xflat[:, bass.ds(at, 512)], acc[:, z, :],
                                     ALU.add).then_inc(added, 1)
                ve.wait_ge(added, half * 4 + 4)


ROW0 = 3
SLOTS = ((slice(0, 3), slice(3, 5), slice(5, 6)), (slice(1, 6, 2), slice(2, 5, 2), slice(0, 1)))
PRODUCTS = 6


def normalise_and_turn_weights(k):
    nc = k.nc
    scaled, turned, ready, normed = (k.sem("w_" + n) for n in ("scaled", "turned", "ready", "normed"))
    R = k.raw
    with ExitStack() as local:
        s = Statistics(k, "ln2", local)
        wfs = local.enter_context(nc.sbuf_tensor("wwfs", [P, C, D], F32))
        bank = local.enter_context(nc.psum_tensor("wbank", [P, 8, 512], F32))
        block = local.enter_context(nc.Block())

        @block.vector
        def _(ve):
            ve.wait_ge(k.raw_loaded, k.RAW_LOADED)
            for o in range(2):
                ve.tensor_scalar(wfs[:, o, :], R.wf[:, o, :], R.scale[:, o:o + 1], None, ALU.mult).then_inc(scaled, 1)
            for t in range(TILES):
                ve.bn_stats(s.stats[:, t, :], k.x[:, t, :]).then_inc(s.tile_done, 1)
            finish_statistics(ve, k, s)
            for t in range(TILES):
                ve.tensor_scalar(k.y[:, t, :], k.x[:, t, :], k.mean[:, t:t + 1], k.rstd[:, t:t + 1],
                                 ALU.subtract, ALU.mult).then_inc(normed, 1)
            for t in range(TILES):
                ve.wait_ge(normed, t + 1)
                ve.bn_stats(s.stats[:, t, :], k.y[:, t, :]).then_inc(s.tile_done, 1)
            ve.wait_ge(normed, TILES)
            finish_statistics(ve, k, s, turn=1)

        odd = lambda w, c: w.rearrange("p (f c) -> p f c", c=C)[:, :, c]
        def turns():
            for c in range(C):
                yield bank[:, 0, c * P:(c + 1) * P], odd(R.w1[:, :], c), P
                yield bank[:, 1, c * P:(c + 1) * P], odd(R.wqk[:, :], c), P
                yield bank[:, 2, c * KW:(c + 1) * KW], odd(R.wv[:, :], c), KW
                yield bank[0:KW, 3, c * P:(c + 1) * P], R.wout[:, c, :], P
            yield bank[:, 4, 0:KW], R.w2[:, :], KW
            for o in range(2):
                for c in range(C):
                    yield bank[:, 5 + c, o * P:(o + 1) * P], odd(wfs[:, o, :], c), P

        @block.tensor
        def _(pe):
            pe.wait_ge(k.raw_loaded, k.RAW_LOADED)
            pe.wait_ge(scaled, 2)
            for dst, src, rows in turns():
                mm = pe.transpose(dst, src, k.ident[0:rows, 0:rows])
            mm.then_inc(turned, 1)

        @block.scalar
        def _(act):
            act.wait_ge(turned, 1)
            pair = lambda b, n: bank[:, b, 0:C * n].rearrange("p (c n) -> p c n", c=C)
            act.activation(k.w1t[:, :, :], pair(0, P), ACT.Copy).then_inc(ready, 1)
            take_root(act, s)
            for z in range(2):
                for c in range(C):
                    for d in range(HD1):
                        at = z * KW
                        act.activation(
                            k.wqkvt[:, c, at:at + KW].rearrange("p (e d g) -> p e d g", e=4, d=HD1)[:, :, d, :],
                            bank[:, 1, c * P + at:c * P + at + KW].rearrange(
                                "p (g e d) -> p e d g", g=G, e=4)[:, :, d, :], ACT.Copy).then_inc(ready, 1)
            act.activation(k.wqkvt[:, :, P:P + KW], pair(2, KW), ACT.Copy).then_inc(ready, 1)
            act.activation(k.woutt[:, :], bank[0:KW, 3, 0:D], ACT.Copy).then_inc(ready, 1)
            act.activation(k.w2t[:, :], bank[:, 4, 0:KW], ACT.Copy).then_inc(ready, 1)
            act.activation(k.wft[:, :, :], bank[:, 5:7, 0:D], ACT.Copy).then_inc(ready, 1)
            take_root(act, s, turn=1)
            act.wait_ge(ready, 13)


def second_projections(k):
    nc = k.nc
    filled, wiped = k.sem("p_filled"), k.sem("p_wiped")
    normed, turned, xt_ready = k.sem("p_normed"), k.sem("p_turned"), k.sem("p_xt_ready")
    h_done, h_ready, qk_done, qk_ready, v_done, v_ready = (k.sem("p_" + n) for n in (
        "h_done", "h_ready", "qk_done", "qk_ready", "v_done", "v_ready"))
    rounded, split = k.sem("p_rounded"), k.sem("p_split")
    added = k.sem("p_added")
    stored = [k.sem(f"p_stored{r}") for r in range(2)]
    SPLIT = 6
    with ExitStack() as local:
        def sb(name, shape, dt=F32):
            return local.enter_context(nc.sbuf_tensor("p" + name, shape, dt))
        gamma, beta, b1, bqk, bv = k.small[:5]
        rows, xt = sb("rows", [P, 2, TB, D]), sb("xt", [P, 2, C, S])
        qk = sb("qk", [KW, 2, 2, S])
        rest = sb("rest", [KW, 2, S])
        parts = sb("parts", [KW, 2, 2, PRODUCTS, S], BF16)
        fill = sb("fill", [P, 2, S], BF16)
        bank = local.enter_context(nc.psum_tensor("pbank", [P, 8, 512], F32))
        block = local.enter_context(nc.Block())
        scratch = (k.q_dram, k.k_dram)

        @block.sync
        def _(sp):
            sp.wait_ge(filled, 2)
            for z in range(2):
                for b in range(B):
                    sp.dma_start(scratch[z][b], fill[:, z, :].unsqueeze(1).broadcast_to([P, G, S])).then_inc(wiped, 16)
            sp.wait_ge(wiped, 16 * 2 * B)
            for b in range(B):
                for z in range(2):
                    sp.wait_ge(rounded, (2 * b + z) * 2 + 2)
                    sp.wait_ge(split, b * SPLIT + (4 if z == 0 else 6))
                    for c in range(4):
                        at = 32 * c + ROW0
                        rows_of = scratch[z][b, at:at + HD1 * PRODUCTS, :, :].rearrange(
                            "(m d) g s -> (d g) m s", d=HD1)
                        sp.dma_start(rows_of, parts[16 * c:16 * c + 16, b % 2, z, :, :]).then_inc(stored[b % 2], 16)
            for r in range(2):
                sp.wait_ge(stored[r], 16 * 8 * (B // 2))

        @block.gpsimd
        def _(pool):
            pool.memset(fill[:, 0, :], 0.0).then_inc(filled, 1)
            pool.memset(fill[:, 1, :], 1.0).then_inc(filled, 1)
            set_network_up(k, pool)
            for t in range(0, TILES, 4):
                x = k.x[:, t:t + 4, :]
                pool.tensor_tensor(x, x, k.y[:, t:t + 4, :], ALU.add).then_inc(added, 1)
            pool.wait_ge(added, TILES // 4)

        def parts_of(b, z, n):
            return parts[:, b % 2, z, SLOTS[z][n], :]

        def spread(a, slot):
            return a.unsqueeze(1).broadcast_to(list(slot.shape))

        @block.vector
        def _(ve):
            def rows_of(b):
                if b >= 2:
                    ve.wait_ge(turned, (b - 2) * C + C)
                for j in range(TB):
                    t = b * TB + j
                    ve.tensor_scalar(rows[:, b % 2, j, :], k.y[:, t, :], k.mean[:, t:t + 1], k.rstd[:, t:t + 1],
                                     ALU.subtract, ALU.mult).then_inc(normed, 1)
            rows_of(0)
            rows_of(1)
            ve.wait_ge(k.small_loaded, k.SMALL_LOADED)
            for b in range(B):
                n = Tally(b, SPLIT)
                if b + 2 < B:
                    rows_of(b + 2)
                if b:
                    ve.wait_ge(split, b * SPLIT)
                for z in range(2):
                    ve.wait_ge(rounded, (2 * b + z) * 2 + 1)
                    ve.tensor_tensor(rest[:, z, :], qk[:, b % 2, z, :], parts_of(b, z, 0)[:, 0, :],
                                     ALU.subtract).then_inc(split, n.up())
                for z in range(2):
                    if z == 0:
                        ve.wait_ge(split, n.now())
                    ve.tensor_copy(parts_of(b, z, 1), spread(rest[:, z, :], parts_of(b, z, 1))).then_inc(split, n.up())
                    ve.wait_ge(split, n.now())
                    ve.tensor_tensor(parts_of(b, z, 2)[:, 0, :], rest[:, z, :], parts_of(b, z, 1)[:, 0, :],
                                     ALU.subtract).then_inc(split, n.up())
                ve.wait_ge(v_done, b + 1)
                ve.tensor_tensor(k.v[:, b * TB:b * TB + TB, :], bank[:, 6, 0:TB * KW].rearrange("p (t n) -> p t n", t=TB),
                                 bv[:, :].unsqueeze(1).broadcast_to([P, TB, KW]), ALU.add).then_inc(v_ready, 1)
                assert n.n == SPLIT

        @block.scalar
        def _(act):
            act.wait_ge(k.small_loaded, k.SMALL_LOADED)
            def take_xt(b):
                for c in range(C):
                    act.wait_ge(turned, b * C + c + 1)
                    if b >= 2:
                        act.wait_ge(v_done, b - 1)
                    act.activation(xt[:, b % 2, c, :], bank[:, c, :], ACT.Identity, bias=beta[:, c:c + 1],
                                   scale=gamma[:, c:c + 1]).then_inc(xt_ready, 1)
            take_xt(0)
            for b in range(B):
                seq = slice(b * S, (b + 1) * S)
                for z in range(2):
                    act.wait_ge(qk_done, b * 2 + z + 1)
                    if b >= 2:
                        act.wait_ge(split, (b - 1) * SPLIT)
                    act.activation(qk[:, b % 2, z, :], bank[0:KW, 4 + z, :], ACT.Identity,
                                   bias=bqk[:, z:z + 1]).then_inc(qk_ready, 1)
                for z in range(2):
                    act.wait_ge(qk_ready, b * 2 + z + 1)
                    if b >= 2:
                        act.wait_ge(stored[b % 2], 16 * 8 * (b // 2))
                    first = parts_of(b, z, 0)
                    act.activation(first[:, 0, :], qk[:, b % 2, z, :], ACT.Copy).then_inc(rounded, 1)
                    act.activation(first[:, 1:3, :], spread(qk[:, b % 2, z, :], first[:, 1:3, :]),
                                   ACT.Copy).then_inc(rounded, 1)
                if b + 1 < B:
                    take_xt(b + 1)
                act.wait_ge(h_done, b + 1)
                act.activation(k.hneg[:, seq], bank[:, 2 + b % 2, :], ACT.Copy, scale=-1.0).then_inc(h_ready, 1)
                act.activation(k.hplus[:, seq], bank[:, 2 + b % 2, :], ACT.Identity, bias=b1[:, 0:1]).then_inc(h_ready, 1)
            act.wait_ge(h_ready, 2 * B)

        @block.tensor
        def _(pe):
            def turn_rows(b):
                pe.wait_ge(normed, b * TB + TB)
                if b:
                    pe.wait_ge(xt_ready, b * C)
                for c in range(C):
                    for j in range(TB):
                        mm = transpose_features(pe, k, bank[:, c, :], rows[:, b % 2, :, :], j, c)
                    mm.then_inc(turned, 1)
            turn_rows(0)
            for b in range(B):
                pe.wait_ge(xt_ready, b * C + C)
                if b:
                    pe.wait_ge(qk_ready, 2 * b)
                for z in range(2):
                    for c in range(C):
                        mm = pe.matmul(bank[0:KW, 4 + z, :], k.wqkvt[:, c, z * KW:(z + 1) * KW], xt[:, b % 2, c, :],
                                       start=c == 0, stop=c == C - 1)
                    mm.then_inc(qk_done, 1)
                if b + 1 < B:
                    turn_rows(b + 1)
                if b >= 2:
                    pe.wait_ge(h_ready, 2 * (b - 1))
                for c in range(C):
                    mm = pe.matmul(bank[:, 2 + b % 2, :], k.w1t[:, c, :], xt[:, b % 2, c, :], start=c == 0, stop=c == C - 1)
                mm.then_inc(h_done, 1)
                if b:
                    pe.wait_ge(v_ready, b)
                for j in range(TB):
                    for c in range(C):
                        mm = pe.matmul(bank[:, 6, j * KW:(j + 1) * KW], xt[:, b % 2, c, j * P:(j + 1) * P],
                                       k.wqkvt[:, c, 2 * KW:3 * KW], start=c == 0, stop=c == C - 1)
                mm.then_inc(v_done, 1)


STEP_I = 8
STEPS = P // STEP_I


ROUNDS = -(-KEEP // 8)


def set_network_up(k, pool):
    bands, top, offdiag, cap, sim = k.network[:5]
    made, set_up = k.sem("s_made"), k.network_set_up
    pool.memset(bands[:, :], 0.0).then_inc(made, 1)
    pool.memset(top[:, :], 1.0).then_inc(made, 1)
    pool.memset(offdiag[:, :, :], 1.0).then_inc(made, 1)
    pool.memset(cap[:, :, :], -GONE).then_inc(made, 1)
    pool.memset(sim[:, :], 0.0).then_inc(set_up, 1)
    pool.wait_ge(made, 4)
    pool.memset(cap[:, ROUNDS - 1, KEEP - 8 * (ROUNDS - 1):8], GONE).then_inc(made, 1)
    for q, n, base in ((0, 1, (TB - 1) * P), (1, TB - 1, 0)):
        part = offdiag[:, q:q + n, :]
        pool.affine_select(out=part, in_=part, compare_op=ALU.not_equal, fill=0.0,
                           base=base, pattern=[[P, n], [-1, S]], channel_multiplier=1).then_inc(made, 1)
    pool.affine_select(out=top[:, 0:1], in_=top[:, 0:1], compare_op=ALU.is_ge, fill=0.0, base=KW - 1,
                       pattern=[[0, 1]], channel_multiplier=-1).then_inc(made, 1)
    pool.affine_select(out=top[:, 1:2], in_=top[:, 1:2], compare_op=ALU.is_ge, fill=0.0, base=-KW,
                       pattern=[[0, 1]], channel_multiplier=1).then_inc(made, 1)
    pool.wait_ge(made, 9)
    pool.wait_ge(k.small_loaded, k.SMALL_LOADED)
    pool.tensor_scalar(bands[:, :].rearrange("p (r x) -> p r x", x=34)[:, :, 0:2],
                       top[:, :].unsqueeze(1).broadcast_to([P, STEPS, 2]), k.small.w3[:, 0:1], None,
                       ALU.mult).then_inc(set_up, 1)
    pool.wait_ge(set_up, 2)


def pairwise(k):
    nc = k.nc
    assert ROUNDS == STEPS // 2 - 1
    R = 4
    PER = 3 * ROUNDS + 2
    AHEAD1 = 2 * R
    AHEAD2 = 2
    AHEAD3 = R
    shifted, windowed, units, products, hidden, summed, sim_out, search = (k.sem("s_" + n) for n in (
        "shifted", "windowed", "units", "products", "hidden", "summed", "sim_out", "search"))
    mask_made, mask_turned, mask_kept = k.sem("s_mask_made"), k.sem("s_mask_turned"), k.sem("s_mask_kept")
    with ExitStack() as local:
        def sb(name, shape, dt=F32):
            return local.enter_context(nc.sbuf_tensor("s" + name, shape, dt))
        bands, _, offdiag, cap, sim, work, best, cut, mask_now = k.network
        b2, b3 = k.small.b2, k.small.b3
        window = sb("window", [P, R, 32])
        shift = sb("shift", [P, R, 4, 2])
        unit1 = sb("unit1", [P, R, STEP_I, S])
        unit2 = sb("unit2", [P, 2, 4, S])
        turned = local.enter_context(nc.psum_tensor("sturned", [P, 1024], BF16))
        pre = local.enter_context(nc.psum_tensor("spre", [P, 2, 2, 512], F32))
        simp = local.enter_context(nc.psum_tensor("ssims", [P, 512], F32))
        block = local.enter_context(nc.Block())
        plus = k.hplus[:, :].rearrange("p (n c x) -> p n c x", c=4, x=32)
        maskf = k.mask[:, :, :].rearrange("p t s -> p (t s)")
        capf = cap[:, :, :].rearrange("p r e -> p (r e)")
        offf = offdiag[:, :, :].rearrange("p t s -> p (t s)")

        @block.gpsimd
        def _(pool):
            with pool.Fori(0, TILES) as n:
                with pool.Fori(0, STEPS // R) as m:
                    for u in range(R):
                        t = n * STEPS + m * R + u
                        pool.wait_ge(units, t * STEP_I + STEP_I)
                        pause(pool, k)
                        pool.tensor_copy(shift[:, u, :, :].unsqueeze(1),
                                         plus[:, bass.ds(n, 1), :, bass.ds(m * (2 * R) + 2 * u, 2)]).then_inc(shifted, 1)
                        pool.wait_ge(summed, t + 1)
                        pause(pool, k)
                        pool.tensor_copy(window[:, u, :],
                                         bands[:, bass.ds(m * (32 * R) + 32 * u, 32)]).then_inc(windowed, 1)

        def first_layer(ve, b, t, u, extra=None):
            ve.wait_ge(shifted, t + 1)
            ve.wait_ge(products, t * 2 + 2)
            pause(ve, k)
            for j in range(STEP_I):
                ve.tensor_scalar(unit1[:, u, j, :], k.hneg[:, bass.ds(b * S, S)],
                                 shift[:, u, j // 2, j % 2:j % 2 + 1], 0.0, ALU.add, ALU.max).then_inc(units, 1)
                if extra and j in extra:
                    extra[j]()

        def search_round(ve, r, done):
            def top8():
                ve.wait_ge(search, done)
                pause(ve, k)
                ve.max(best[:, :], work[:, :]).then_inc(search, 1)

            def capped():
                ve.wait_ge(search, done + 1)
                ve.tensor_tensor(cut[:, :], best[:, :], capf[:, bass.ds(r * 8, 8)], ALU.min).then_inc(search, 1)

            def taken():
                ve.wait_ge(search, done + 2)
                pause(ve, k)
                ve.match_replace(work[:, :], cut[:, :], work[:, :], GONE).then_inc(search, 1)
            return top8, capped, taken

        def begin_search(ve, n, q):
            ve.wait_ge(sim_out, n + 1)
            ve.wait_ge(search, n * PER + 1)
            pause(ve, k)
            ve.tensor_tensor(work[:, :], sim[:, :], offf[:, bass.ds(q * S, S)], ALU.mult).then_inc(search, 1)

        def end_search(ve, n):
            ve.wait_ge(search, n * PER + PER)
            pause(ve, k)
            ve.tensor_scalar(maskf[:, bass.ds(n * S, S)], work[:, :], GONE, -OFF, ALU.not_equal,
                             ALU.mult).then_inc(search, 1)
            ve.wait_ge(mask_turned, n + 1)
            ve.tensor_scalar(mask_now[:, :], work[:, :], GONE, -OFF, ALU.not_equal, ALU.mult).then_inc(mask_made, 1)

        @block.vector
        def _(ve):
            ve.sem_inc(units, R * STEP_I)
            ve.sem_inc(search, 1)
            with ve.Fori(0, B) as b:
                with ve.Fori(0, TB) as q:
                    n = b * TB + q
                    t0, s0 = n * STEPS, n * PER + 2
                    first_layer(ve, b, t0, 0)
                    first_layer(ve, b, t0 + 1, 1)
                    begin_search(ve, n, q)
                    a, c, z = search_round(ve, n * 0, s0)
                    first_layer(ve, b, t0 + 2, 2, {1: a, 5: c})
                    first_layer(ve, b, t0 + 3, 3, {1: z})
                    with ve.Fori(0, STEPS // R - 1) as m:
                        for v in range(2):
                            a, c, z = search_round(ve, m * 2 + 1 + v, s0 + m * 6 + 3 + 3 * v)
                            first_layer(ve, b, t0 + m * R + (R + 2 * v), 2 * v, {1: a, 5: c})
                            first_layer(ve, b, t0 + m * R + (R + 2 * v + 1), 2 * v + 1, {1: z})
                    end_search(ve, n)
            ve.wait_ge(search, TILES * PER + 1)
            ve.wait_ge(mask_made, TILES)

        mask_tf = k.mask_t[:, :, :, :].rearrange("p t j s -> p (t j s)")

        def keep_mask(act, n):
            act.wait_ge(mask_turned, n + 2)
            act.activation(mask_tf[:, bass.ds(n * S, S)], turned[:, 0:S], ACT.Copy).then_inc(mask_kept, 1)

        def step_done(act, t, v):
            for h in range(2):
                act.wait_ge(products, t * 2 + h + 1 + AHEAD1)
                act.wait_ge(summed, t + (AHEAD3 - 1))
                act.activation(unit2[:, v, 2 * h:2 * h + 2, :], pre[:, h, :, :], ACT.Relu,
                               bias=b2[:, 0:1]).then_inc(hidden, 1)

        def tile_done(act, n):
            act.wait_ge(summed, n * STEPS + STEPS + AHEAD3)
            act.wait_ge(search, n * PER + 2)
            act.activation(sim[:, :], simp[:, :], ACT.Identity, bias=b3[:, 0:1]).then_inc(sim_out, 1)
            keep_mask(act, n)

        @block.scalar
        def _(act):
            act.sem_inc(hidden, AHEAD2)
            act.sem_inc(sim_out, 1)
            act.sem_inc(mask_kept, 1)
            step_done(act, 0, 0)
            with act.Fori(0, TILES - 1) as n:
                with act.Fori(0, STEPS // 2) as m:
                    for v in range(2):
                        step_done(act, n * STEPS + m * 2 + (1 + v), 1 - v)
                tile_done(act, n)
            t0 = (TILES - 1) * STEPS
            with act.Fori(0, STEPS // 2 - 1) as m:
                for v in range(2):
                    step_done(act, m * 2 + (t0 + 1 + v), 1 - v)
            step_done(act, t0 + STEPS - 1, 1)
            tile_done(act, TILES - 1)

        def second_layer(pe, t, u):
            for h in range(2):
                pe.wait_ge(units, t * STEP_I + (R * STEP_I + 4 * h + 4))
                pe.wait_ge(hidden, t * 2 + h + 1)
                for c in range(2 * h, 2 * h + 2):
                    for s in range(2):
                        mm = pe.matmul(pre[s * KW:(s + 1) * KW, h, c % 2, :], k.w2t[:, :], unit1[:, u, 2 * c + s, :],
                                       start=True, stop=True)
                mm.then_inc(products, 1)

        def third_layer(pe, n, t, u, first=False):
            pe.wait_ge(windowed, t + 1)
            pe.wait_ge(hidden, t * 2 + 2 + AHEAD2)
            if first:
                pe.wait_ge(sim_out, n + 1)
            for c in range(4):
                mm = pe.matmul(simp[32 * c:32 * c + 32, :], window[:, u, :], unit2[:, u % 2, c, :], start=first,
                               stop=False, skip_group_check=True)
            mm.then_inc(summed, 1)

        def turn_mask(pe, n):
            pe.wait_ge(mask_made, n + 1)
            pe.wait_ge(mask_kept, n + 1)
            for j in range(TB):
                mm = pe.transpose(turned[:, j * P:(j + 1) * P], mask_now[:, j * P:(j + 1) * P], k.identb[:, :])
            mm.then_inc(mask_turned, 1)

        def tile(pe, n, more):
            t0 = n * STEPS
            for u in range(1, R):
                second_layer(pe, t0 + u, u)
                third_layer(pe, n, t0 + u - 1, u - 1, first=u == 1)
            with pe.Fori(0, STEPS // R - 1) as m:
                for u in range(R):
                    t = t0 + m * R + (R + u)
                    second_layer(pe, t, u)
                    third_layer(pe, n, t - 1, (u - 1) % R)
            if more:
                second_layer(pe, t0 + STEPS, 0)
            turn_mask(pe, n)
            third_layer(pe, n, t0 + STEPS - 1, R - 1)

        @block.tensor
        def _(pe):
            pe.sem_inc(products, AHEAD1)
            pe.sem_inc(summed, AHEAD3)
            pe.sem_inc(mask_turned, 1)
            second_layer(pe, 0, 0)
            with pe.Fori(0, TILES - 1) as n:
                tile(pe, n, True)
            tile(pe, TILES - 1, False)


def second_attention(k):
    nc = k.nc
    U = 4 * TB
    R = 4
    set_up = k.sem("a1_set_up")
    q_in, k_in = ([k.sem(f"a1_{n}{r}") for r in range(R)] for n in ("q_in", "k_in"))
    v_in, mask_in = k.sem("a1_v_in"), k.sem("a1_mask_in")
    scored, peak, split, peaks_turned, q_ready = (k.sem("a1_" + n) for n in (
        "scored", "peak", "split", "peaks_turned", "q_ready"))
    masked, exped, mixed, mixed_ready, mixed_turned, normal = (k.sem("a1_" + n) for n in (
        "masked", "exped", "mixed", "mixed_ready", "mixed_turned", "normal"))
    search, mask_made, mask_turned, mask_kept = (k.sem("a1_" + n) for n in (
        "search", "mask_made", "mask_turned", "mask_kept"))
    SPLIT = 5
    assert ROUNDS <= G - 1
    LASTG = B * G - 1
    UNITS_AT = (3, 2, 3, 2, 3, 3, 0, 0)
    assert sum(UNITS_AT) == U
    NORMAL_AT = sum(UNITS_AT[:4])
    with ExitStack() as local:
        def sb(name, shape, dt=F32):
            return local.enter_context(nc.sbuf_tensor("b" + name, shape, dt))
        qs, ks = sb("qs", [P, R, S], BF16), sb("ks", [P, R, S], BF16)
        qm = sb("qm", [P, 2, S], BF16)
        vg = sb("vg", [P, 2, TB, 4, 32])
        junk = sb("junk", [P, 2, S], BF16)
        peaks = sb("peaks", [P, TB, 4])
        rest = sb("rest", [P, TB, 4])
        neg = sb("neg", [P, TB, 4])
        peak_parts = sb("peak_parts", [P, TB, 4, 32], BF16)
        pt = sb("pt", [P, 2, 4, TB, S])
        mixed_s = sb("mixed_s", [P, S])
        inv = sb("inv", [P, TB, 4])
        mask_s = sb("mask_s", [P, TB, S], BF16)
        s1 = local.enter_context(nc.psum_tensor("bs1", [P, 2, 512], F32))
        s2 = local.enter_context(nc.psum_tensor("bs2", [P, 2, 2, 512], F32))
        om = local.enter_context(nc.psum_tensor("bom", [P, 512], F32))
        misc = local.enter_context(nc.psum_tensor("bmisc", [P, 512], F32))
        miscb = misc[:, :].bitcast(BF16)
        offdiag, cap, sim, work, best, cut, mask_now = k.network[2:]
        block = local.enter_context(nc.Block())
        maskf = k.mask[:, :, :].rearrange("p t s -> p (t s)")
        mask_t = k.mask_t[:, :, :, :].rearrange("p t j s -> p j t s")
        parts_flat = peak_parts[:, :, :, :].rearrange("p q c r -> p q (c r)")
        ao_groups = k.ao[:, :, :].rearrange("p t (g c d) -> p t g c d", c=4, d=HD1)

        @block.sync
        def _(sp):
            with sp.Fori(0, B) as b:
                qd, kd = (a.rearrange("b p g s -> (b p) (g s)")[bass.ds(b * P, P), :] for a in (k.q_dram, k.k_dram))
                for g in range(G):
                    sp.wait_ge(masked, b * (8 * G) + 8 * g + 8)
                    pause(sp, k)
                    u = g % R
                    sp.dma_start(qs[:, u, :], qd[:, g * S:(g + 1) * S]).then_inc(q_in[u], 16)
                    sp.dma_start(ks[:, u, :], kd[:, g * S:(g + 1) * S]).then_inc(k_in[u], 16)

        @block.gpsimd
        def _(pool):
            pool.memset(peak_parts[:, :, :, :], 0.0).then_inc(set_up, 1)
            pool.memset(vg[:, :, :, :, :], 0.0).then_inc(set_up, 1)
            pool.wait_ge(set_up, 2)
            pool.memset(vg[:, :, :, :, 2:3], 1.0).then_inc(set_up, 1)
            vt = k.v[:, :, :].rearrange("p t (g c d) -> p t g c d", c=4, d=2)
            with pool.Fori(0, B) as b:
                for g in range(G):
                    pool.wait_ge(mixed, b * G + g + 1)
                    pause(pool, k)
                    pool.tensor_copy(vg[:, g % 2, :, :, 0:2],
                                     vt[:, bass.ds(b * TB, TB), g, :, :]).then_inc(v_in, 1)


        def scores1(pe, it, g, n):
            c, q = divmod(n, TB)
            if n == 0:
                uses = (it - g % R) * (16 // R) + 16
                pe.wait_ge(q_in[g % R], uses)
                pe.wait_ge(k_in[g % R], uses)
            pe.wait_ge(peak, it * U + n + 1)
            pe.matmul(s1[:, n % 2, :], qs[32 * c:32 * c + 32, g % R, q * P:(q + 1) * P],
                      ks[32 * c:32 * c + 32, g % R, :], start=True, stop=True).then_inc(scored, 1)

        def turn_peaks(pe, it):
            pe.wait_ge(split, it * SPLIT + SPLIT + 1)
            pause(pe, k)
            for q in range(TB):
                mm = pe.transpose(miscb[:, q * P:(q + 1) * P], parts_flat[:, q, :], k.identb[:, :])
            mm.then_inc(peaks_turned, 1)

        def scores2(pe, b, it, g, n, z):
            c, h = divmod(n, 2)
            j = 2 * h + z
            if z == 0:
                if n == 0:
                    pe.wait_ge(q_ready, it + 1)
                pe.wait_ge(exped, it * 8 + n + 1)
            pe.matmul(s2[:, n % 2, z, :], ks[32 * c:32 * c + 32, g % R, j * P:(j + 1) * P],
                      qm[32 * c:32 * c + 32, g % 2, :], start=True, stop=False)
            mm = pe.matmul(s2[:, n % 2, z, :].rearrange("p (t s) -> p t s", t=TB), k.identb[:, :],
                           mask_t[:, j, bass.ds(b * TB + 1, TB), :], start=False, stop=True)
            if z:
                mm.then_inc(masked, 1)

        def mix(pe, it, g, j):
            if j == 0:
                pe.wait_ge(v_in, it + 1)
                pe.wait_ge(mixed_ready, it + 1)
            pe.wait_ge(exped, it * 8 + (7 if j < 2 else 8) + 2)
            for c in range(4):
                mm = pe.matmul(om[32 * c:32 * c + 32, :], vg[:, g % 2, j, c, :], pt[:, g % 2, c, j, :],
                               start=j == 0, stop=j == TB - 1, skip_group_check=True)
            if j == TB - 1:
                mm.then_inc(mixed, 1)

        def turn_mixed(pe, it, peaks_added):
            pe.wait_ge(mixed_ready, it + 2)
            pe.wait_ge(q_ready, peaks_added)
            for q in range(TB):
                mm = pe.transpose(misc[:, q * P:(q + 1) * P], mixed_s[:, q * P:(q + 1) * P], k.ident[:, :])
            mm.then_inc(mixed_turned, 1)

        def group_on_tensor(pe, b, g, age=2, last=False, first_sequence=False):
            it = b * G + g
            n1 = 0

            def next_unit():
                nonlocal n1
                if n1 < sum(UNITS_AT[:n + 1]) and not last:
                    scores1(pe, it + 1, (g + 1) % G, n1)
                    n1 += 1

            for n in range(8):
                if n == 7 and not last:
                    if age:
                        pe.wait_ge(normal, it * 2 - 1)
                    if first_sequence and g == ROUNDS:
                        pe.wait_ge(mask_kept, 1)
                    turn_peaks(pe, it + 1)
                for z in range(2):
                    scores2(pe, b, it, g, n, z)
                    next_unit()
                if n % 2 == 0 and age:
                    mix(pe, it - 1, (g - 1) % G, n // 2)
                next_unit()
                if n == 2 and age == 2:
                    turn_mixed(pe, it - 2, it + 1)
                if n == 5 and first_sequence and g == ROUNDS:
                    pe.wait_ge(mask_made, 2)
                    pe.wait_ge(normal, it * 2 - 1)
                    for j in range(TB):
                        mm = pe.transpose(miscb[:, j * P:(j + 1) * P], mask_now[:, j * P:(j + 1) * P], k.identb[:, :])
                    mm.then_inc(mask_turned, 1)

        @block.tensor
        def _(pe):
            pe.sem_inc(masked, 8 * R)
            pe.sem_inc(mixed, 2)
            pe.sem_inc(mixed_turned, 1)
            pe.sem_inc(peaks_turned, 1)
            pe.wait_ge(set_up, 3)
            for n in range(U):
                scores1(pe, 0, 0, n)
            turn_peaks(pe, 0)
            for g in range(G):
                group_on_tensor(pe, 0, g, age=min(g, 2), first_sequence=True)
            with pe.Fori(1, B - 1) as b:
                for g in range(G):
                    group_on_tensor(pe, b, g)
            for g in range(G):
                group_on_tensor(pe, B - 1, g, last=g == G - 1)
            pe.wait_ge(normal, LASTG * 2 - 1)
            turn_mixed(pe, LASTG - 1, B * G)
            for j in range(TB):
                mix(pe, LASTG, G - 1, j)
            pe.wait_ge(normal, LASTG * 2 + 1)
            turn_mixed(pe, LASTG, B * G)

        def group_on_scalar(act, b, g, first, first_sequence=False):
            it = b * G + g
            for n in range(8):
                c, h = divmod(n, 2)
                act.wait_ge(masked, it * 8 + n + 1 + 8 * R)
                if n == 0:
                    act.wait_ge(mixed, it + 1)
                act.activation(pt[:, g % 2, c, 2 * h:2 * h + 2, :], s2[:, n % 2, :, :], ACT.Exp,
                               scale=HD1 ** -0.5).then_inc(exped, 1)
                if n == 5 and first_sequence and g == ROUNDS:
                    act.wait_ge(mask_turned, 1)
                    act.activation(k.mask_t[:, TILES, :, :], miscb[:, 0:S].rearrange("p (j s) -> p j s", j=TB),
                                   ACT.Copy).then_inc(mask_kept, 1)
                if n == 6 and not first:
                    take_mixed(act, it - 1)

        def take_mixed(act, it):
            act.wait_ge(mixed, it + 3)
            act.wait_ge(mixed_turned, it + 1)
            act.activation(mixed_s[:, :], om[:, :], ACT.Copy).then_inc(mixed_ready, 1)

        @block.scalar
        def _(act):
            act.sem_inc(exped, 2)
            act.sem_inc(mixed_ready, 1)
            for g in range(G):
                group_on_scalar(act, 0, g, g == 0, first_sequence=True)
            with act.Fori(1, B) as b:
                for g in range(G):
                    group_on_scalar(act, b, g, False)
            take_mixed(act, LASTG)

        def fetch_masks(ve, b):
            ve.wait_ge(peak, b * (G * U) + 2)
            ve.tensor_copy(mask_s[:, :, :].rearrange("p t s -> p (t s)"),
                           maskf[:, bass.ds(b * (TB * S) + S, TB * S)]).then_inc(mask_in, 1)
            ve.wait_ge(mask_in, b + 1)

        def search_step(ve, r, part):
            ve.wait_ge(search, 3 * r + part + 1)
            if part == 0:
                ve.max(best[:, :], work[:, :]).then_inc(search, 1)
            elif part == 1:
                ve.tensor_tensor(cut[:, :], best[:, :], cap[:, r, :], ALU.min).then_inc(search, 1)
            else:
                ve.match_replace(work[:, :], cut[:, :], work[:, :], GONE).then_inc(search, 1)

        def find_peak(ve, it, n):
            c, q = divmod(n, TB)
            if n == 0:
                ve.wait_ge(split, it * SPLIT + 1)
            ve.wait_ge(scored, it * U + n + 1)
            ve.wait_ge(peak, it * U + n + 1)
            pause(ve, k)
            ve.tensor_tensor_reduce(junk[:, n % 2, :], s1[:, n % 2, :], mask_s[:, q, :],
                                    1.0, GONE, ALU.add, ALU.max, peaks[:, q, c:c + 1]).then_inc(peak, 1)

        def split_peaks(ve, it):
            n = Tally(it, SPLIT, 1)
            part = lambda z: peak_parts[:, :, :, z]
            ve.wait_ge(peak, it * U + U + 2)
            ve.wait_ge(peaks_turned, it + 1)
            ve.tensor_scalar(neg[:, :, :], peaks[:, :, :], -1.0, None, ALU.mult).then_inc(split, n.up())
            ve.wait_ge(split, n.now())
            ve.tensor_copy(part(0), neg[:, :, :]).then_inc(split, n.up())
            ve.wait_ge(split, n.now())
            ve.tensor_tensor(rest[:, :, :], neg[:, :, :], part(0), ALU.subtract).then_inc(split, n.up())
            ve.wait_ge(split, n.now())
            ve.tensor_copy(part(1), rest[:, :, :]).then_inc(split, n.up())
            ve.wait_ge(split, n.now())
            ve.tensor_tensor(part(2), rest[:, :, :], part(1), ALU.subtract).then_inc(split, n.up())
            assert n.n == SPLIT

        def add_peaks(ve, it, g):
            ve.wait_ge(peaks_turned, it + 2)
            ve.wait_ge(masked, it * 8 + 8 * R - 8)
            ve.tensor_tensor(qm[:, g % 2, :], miscb[:, 0:S], qs[:, g % R, :], ALU.add).then_inc(q_ready, 1)

        def normalise(ve, b, it, g):
            ve.wait_ge(mixed_turned, it + 2)
            o = misc[:, :].rearrange("p (q c r) -> p q c r", q=TB, c=4)
            ve.wait_ge(normal, it * 2 + 1)
            ve.reciprocal(inv[:, :, :], o[:, :, :, 2]).then_inc(normal, 1)
            ve.wait_ge(normal, it * 2 + 2)
            ve.tensor_tensor(ao_groups[:, bass.ds(b * TB, TB), g, :, :], o[:, :, :, 0:2],
                             inv[:, :, :].unsqueeze(3).broadcast_to([P, TB, 4, HD1]), ALU.mult).then_inc(normal, 1)

        def group_on_vector(ve, b, g, age=2, last=False, first_sequence=False):
            it = b * G + g
            done_b, done_g = (b, g - 2) if g >= 2 else (b - 1, g + G - 2)
            next_b, next_g = (b, g + 1) if g < G - 1 else (b + 1, 0)
            if g == G - 1 and not last:
                fetch_masks(ve, next_b)
            for n in range(U + 1):
                if n == NORMAL_AT and age == 2:
                    normalise(ve, done_b, it - 2, done_g)
                if n < U and not last:
                    find_peak(ve, it + 1, n)
                if first_sequence and g < ROUNDS and n in (3, 7, 11):
                    search_step(ve, g, n // 4)
                if first_sequence and g == ROUNDS and n == 3:
                    ve.wait_ge(search, 3 * ROUNDS + 1)
                    for dst in (k.mask[:, TILES, :], mask_now[:, :]):
                        ve.tensor_scalar(dst, work[:, :], GONE, -OFF, ALU.not_equal, ALU.mult).then_inc(mask_made, 1)
                    ve.wait_ge(mask_made, 2)
            if not last:
                split_peaks(ve, it + 1)
                add_peaks(ve, it + 1, next_g)

        @block.vector
        def _(ve):
            ve.sem_inc(peak, 2)
            ve.sem_inc(split, 1)
            ve.sem_inc(normal, 1)
            ve.wait_ge(set_up, 3)
            fetch_masks(ve, 0)
            ve.tensor_tensor(work[:, :], sim[:, :], offdiag[:, 0, :], ALU.mult).then_inc(search, 1)
            for n in range(U):
                find_peak(ve, 0, n)
            split_peaks(ve, 0)
            add_peaks(ve, 0, 0)
            for g in range(G):
                group_on_vector(ve, 0, g, age=min(g, 2), first_sequence=True)
            with ve.Fori(1, B - 1) as b:
                for g in range(G):
                    group_on_vector(ve, b, g)
            for g in range(G):
                group_on_vector(ve, B - 1, g, last=g == G - 1)
            for g in range(G - 2, G):
                normalise(ve, B - 1, (B - 1) * G + g, g)
            ve.wait_ge(normal, B * G * 2 + 1)


def second_output(k):
    nc = k.nc
    ao_turned, ao_ready, out_done, step = (k.sem("o_" + n) for n in ("ao_turned", "ao_ready", "out_done", "step"))
    with ExitStack() as local:
        ao_t = local.enter_context(nc.sbuf_tensor("oao_t", [KW, 2, S], F32))
        bout, s = k.small.bout, Statistics(k, "ln4", local)
        tmp = local.enter_context(nc.sbuf_tensor("otmp", [P, 2, 2, S], F32))
        turned = local.enter_context(nc.psum_tensor("oturned", [P, 2, 512], F32))
        out = local.enter_context(nc.psum_tensor("oout", [P, 2, 2, 512], F32))
        block = local.enter_context(nc.Block())

        @block.tensor
        def _(pe):
            for b in range(B + 1):
                if b < B:
                    if b >= 2:
                        pe.wait_ge(ao_ready, b - 1)
                    for q in range(TB):
                        mm = pe.transpose(turned[0:KW, b % 2, q * P:(q + 1) * P], k.ao[:, b * TB + q, :], k.ident[:, :])
                    mm.then_inc(ao_turned, 1)
                if b:
                    pe.wait_ge(ao_ready, b)
                    if b >= 3:
                        pe.wait_ge(step, 4 * (b - 3) + 2)
                    for q in range(TB):
                        mm = pe.matmul(out[:, (b - 1) % 2, q // 2, (q % 2) * D:(q % 2) * D + D],
                                       ao_t[:, (b - 1) % 2, q * P:(q + 1) * P], k.woutt[:, :], start=True, stop=True)
                    mm.then_inc(out_done, 1)

        @block.scalar
        def _(act):
            for b in range(B):
                act.wait_ge(ao_turned, b + 1)
                if b >= 2:
                    act.wait_ge(out_done, b - 1)
                act.activation(ao_t[:, b % 2, :], turned[0:KW, b % 2, :], ACT.Copy).then_inc(ao_ready, 1)
            take_root(act, s)

        @block.vector
        def _(ve):
            ve.wait_ge(k.small_loaded, k.SMALL_LOADED)
            for b in range(B):
                ve.wait_ge(out_done, b + 1)
                ve.wait_ge(step, 4 * b)
                for h in range(2):
                    ve.tensor_tensor(tmp[:, b % 2, h, :].rearrange("p (t n) -> p t n", t=2),
                                     out[:, b % 2, h, :].rearrange("p (t n) -> p t n", t=2),
                                     bout[:, :].unsqueeze(1).broadcast_to([P, 2, D]), ALU.add).then_inc(step, 1)
                ve.wait_ge(step, 4 * b + 2)
                for h in range(2):
                    x = k.x[:, b * TB + 2 * h:b * TB + 2 * h + 2, :].rearrange("p t d -> p (t d)")
                    ve.tensor_tensor(x, x, tmp[:, b % 2, h, :], ALU.add).then_inc(step, 1)
                for j in range(TB):
                    ve.wait_ge(step, 4 * b + 3 + j // 2)
                    ve.bn_stats(s.stats[:, b * TB + j, :], k.x[:, b * TB + j, :]).then_inc(s.tile_done, 1)
            finish_statistics(ve, k, s)


def last_layer(k):
    nc = k.nc
    biased, normed, turned, xt_ready, done, step = (k.sem("f_" + n) for n in (
        "biased", "normed", "turned", "xt_ready", "done", "step"))
    stored = [k.sem(f"f_stored{z}") for z in range(2)]
    with ExitStack() as local:
        def sb(name, shape, dt=F32):
            return local.enter_context(nc.sbuf_tensor("f" + name, shape, dt))
        base = sb("base", [P, 2, TB, D])
        rows, xt = sb("rows", [P, 2, TB, D]), sb("xt", [P, 2, C, S])
        tmp = sb("tmp", [P, 2, TB, D])
        bank = local.enter_context(nc.psum_tensor("fbank", [P, 2, 4, 512], F32))
        outs = k.out.rearrange("b (t p) d -> p b t d", p=P)
        block = local.enter_context(nc.Block())

        @block.sync
        def _(sp):
            for b in range(B):
                sp.wait_ge(step, 2 * b + 2)
                sp.dma_start(outs[:, b, :, :], tmp[:, b % 2, :, :]).then_inc(stored[b % 2], 16)
            for z in range(2):
                sp.wait_ge(stored[z], 16 * B // 2)

        @block.gpsimd
        def _(pool):
            for b in range(B):
                if b >= 2:
                    pool.wait_ge(step, 2 * (b - 1))
                pool.tensor_tensor(base[:, b % 2, :, :], k.x[:, b * TB:b * TB + TB, :],
                                   k.small.bias[:, :].unsqueeze(1).broadcast_to([P, TB, D]), ALU.add).then_inc(biased, 1)

        @block.vector
        def _(ve):
            for b in range(B + 1):
                if b < B:
                    if b >= 2:
                        ve.wait_ge(turned, 2 * b - 2)
                    for j in range(TB):
                        normalise_tile(ve, k, k.x, rows[:, b % 2, :, :], b, j).then_inc(normed, 1)
                if b:
                    a = b - 1
                    ve.wait_ge(done, a + 1)
                    if a >= 2:
                        ve.wait_ge(stored[a % 2], 16 * (a // 2))
                    ve.wait_ge(biased, a + 1)
                    for h in range(2):
                        part = slice(2 * h, 2 * h + 2)
                        ve.tensor_tensor(tmp[:, a % 2, part, :], bank[:, a % 2, 2 + h, :].rearrange("p (t n) -> p t n", t=2),
                                         base[:, a % 2, part, :], ALU.add).then_inc(step, 1)

        @block.scalar
        def _(act):
            for b in range(B):
                for c in range(C):
                    act.wait_ge(turned, b * C + c + 1)
                    if b >= 2:
                        act.wait_ge(done, b - 1)
                    act.activation(xt[:, b % 2, c, :], bank[:, b % 2, c, :], ACT.Copy).then_inc(xt_ready, 1)

        @block.tensor
        def _(pe):
            for b in range(B):
                pe.wait_ge(normed, b * TB + TB)
                if b >= 2:
                    pe.wait_ge(step, 2 * b - 2)
                    pe.wait_ge(xt_ready, 2 * b - 2)
                for c in range(C):
                    for j in range(TB):
                        mm = transpose_features(pe, k, bank[:, b % 2, c, :], rows[:, b % 2, :, :], j, c)
                    mm.then_inc(turned, 1)
                pe.wait_ge(xt_ready, b * C + C)
                for j in range(TB):
                    for c in range(C):
                        mm = pe.matmul(bank[:, b % 2, 2 + j // 2, (j % 2) * D:(j % 2) * D + D],
                                       xt[:, b % 2, c, j * P:(j + 1) * P], k.wft[:, c, :], start=c == 0, stop=c == C - 1)
                mm.then_inc(done, 1)


def build(nc, ins, out):
    with ExitStack() as ctx:
        k = Kernel(nc, ctx, ins, out)

        def sb(name, shape, dt=F32, of=ctx):
            return of.enter_context(nc.sbuf_tensor(name, shape, dt))
        k.x = sb("x", [P, TILES, D])
        k.ident, k.identb = sb("ident", [P, P]), sb("identb", [P, P], BF16)
        k.mean, k.rstd = sb("mean", [P, TILES]), sb("rstd", [P, TILES])
        k.passed = k.sem("passed")
        k.w0_loaded, k.W0_LOADED = k.sem("w0_loaded"), 16 * 10
        k.small_loaded, k.SMALL_LOADED = k.sem("small_loaded"), 16 * 27
        k.small = Small(sb("gamma", [P, C]), sb("beta", [P, C]), sb("b1", [P, 1]), sb("bqk", [KW, 2]), sb("bv", [P, KW]),
                        sb("w3", [P, 1]), sb("b2", [P, 1]), sb("b3", [P, 1]), sb("bout", [P, D]), sb("bias", [P, D]))
        k.raw_loaded, k.RAW_LOADED = k.sem("raw_loaded"), 16 * 8
        k.raw = RawWeights(sb("w1raw", [P, D]), sb("w2raw", [KW, P]), sb("wqkraw", [P, D]),
                           sb("wvraw", [KW, D]), sb("woutraw", [P, C, KW]),
                           sb("wfraw", [P, C, D]), sb("wscale", [P, C]))
        with ExitStack() as local:
            wq, wk, wv, wo = (sb("a0" + name, [P, C, D], of=local) for name in ("wq", "wk", "wv", "wo"))
            bq, bk = sb("a0bq", [P, 2], of=local), sb("a0bk", [P, 2], of=local)
            bv, bo = sb("a0bv", [P, D], of=local), sb("a0bo", [P, D], of=local)
            k.w0 = FirstWeights(wq, wk, wv, wo, bq, bk, bv, bo)
            load_and_constants(k)
            first_attention(k)
        with ExitStack() as local:
            k.xt = sb("xt", [P, C, N], of=local)
            k.shares_dram = nc.dram_tensor("shares", (EXPERTS + SHARED // FE, N), F32, kind="Internal").ap()
            R = EXPERT_SLOTS
            k.expert_slots = ExpertSlots(
                sb("wg", [P, R, C, 2, FE], of=local), sb("wu", [P, R, C, 2, FE], of=local), sb("wd", [P, R, D], of=local),
                *([k.sem(f"e_{n}{r}") for r in range(R)] for n in ("gate_in", "up_in", "down_in")))
            router(k)
            experts(k)
        k.w1t, k.wqkvt, k.w2t = sb("w1t", [P, C, P]), sb("wqkvt", [P, C, 3 * KW]), sb("w2t", [P, KW])
        k.woutt, k.wft = sb("woutt", [KW, D]), sb("wft", [P, C, D])
        k.q_dram = nc.dram_tensor("q_parts", (B, P, G, S), BF16, kind="Internal").ap()
        k.k_dram = nc.dram_tensor("k_parts", (B, P, G, S), BF16, kind="Internal").ap()
        k.v = sb("v", [P, TILES, KW])
        k.mask = sb("mask", [P, TILES + 1, S], BF16)
        k.mask_t = sb("mask_t", [P, TILES + 1, TB, P], BF16)
        k.ao = sb("ao", [P, TILES, KW])
        with ExitStack() as local:
            k.network_set_up = k.sem("s_set_up")
            k.network = Network(sb("bands", [P, STEPS * 34], of=local), sb("top", [P, 2], of=local),
                                sb("offdiag", [P, TB, S], of=local), sb("cap", [P, ROUNDS, 8], of=local),
                                sb("sim", [P, S], of=local), sb("work", [P, S], of=local),
                                sb("best", [P, 8], of=local), sb("cut", [P, 8], of=local),
                                sb("mask_now", [P, S], BF16, of=local))
            with ExitStack() as inner:
                k.hneg, k.hplus = sb("hneg", [P, N], of=inner), sb("hplus", [P, N], of=inner)
                with ExitStack() as innermost:
                    k.y = sb("y", [P, TILES, D], of=innermost)
                    normalise_and_turn_weights(k)
                    second_projections(k)
                pairwise(k)
            second_attention(k)
        second_output(k)
        last_layer(k)


INPUTS = ["L0_attn_x", "L0_attn_Wq", "L0_attn_bq", "L0_attn_Wk", "L0_attn_bk", "L0_attn_Wv", "L0_attn_bv",
          "L0_attn_Wo", "L0_attn_bo", "L0_ffn_router_w", "L0_ffn_router_bias", "L0_ffn_wg", "L0_ffn_wu",
          "L0_ffn_wd", "L0_ffn_swg", "L0_ffn_swu", "L0_ffn_swd", "L1_attn_gamma", "L1_attn_beta", "L1_attn_W1",
          "L1_attn_b1", "L1_attn_W2", "L1_attn_b2", "L1_attn_W3", "L1_attn_b3", "L1_attn_Wqkv", "L1_attn_bqkv",
          "L1_attn_Wout", "L1_attn_bout", "L1_ffn_weight", "L1_ffn_scale_weight", "L1_ffn_bias"]


def kernel(**inputs):
    import numpy as np
    import concourse.bacc as bacc
    from concourse.bass_utils import run_bass_kernel_spmd

    nc = bacc.Bacc("TRN2", target_bir_lowering=False, num_devices=1)
    arrays, aps = {}, {}
    for name in INPUTS:
        a = np.ascontiguousarray(inputs[name])
        arrays[name] = a
        aps[name] = nc.dram_tensor(name, a.shape, mybir.dt.from_np(a.dtype), kind="ExternalInput").ap()
    out = nc.dram_tensor("out", (B, S, D), F32, kind="ExternalOutput").ap()
    build(nc, aps, out)
    return run_bass_kernel_spmd(nc, [arrays], core_ids=[0]).results[0]["out"]
```
